# Optimizing a Trainium2 kernel written in Bass

```python
import numpy as np
import jax
import jax.numpy as jnp

def _softmax(x, axis=-1):
    return jax.nn.softmax(x, axis=axis)

def _gelu(x):
    return jax.nn.gelu(x, approximate=True)

def _silu(x):
    return jax.nn.silu(x)

def _sigmoid(x):
    return jax.nn.sigmoid(x)

def _layernorm(x, axis=-1, eps=1e-05):
    m = jnp.mean(x, axis=axis, keepdims=True)
    v = jnp.var(x, axis=axis, keepdims=True)
    return (x - m) / jnp.sqrt(v + eps)

def _scatter_add(tgt, idx, src, axis=0):
    return tgt.at[idx].add(src)

def _segment_sum(src, seg, n):
    return jax.ops.segment_sum(src, seg, n)
kernel_name = 'mk_gnn_preln_d4_gnn_r32_770cde'

def setup_inputs(seed: int=0):
    np.random.seed(seed)
    _w = jnp.asarray

    def _rec_inputs():
        import jax
        import jax.numpy as jnp
        _gk = jax.random.key(seed)
        x = -0.000202 + 1 * jax.random.normal(jax.random.fold_in(_gk, 1), (3125, 64), jnp.float32)
        _s = jax.random.randint(jax.random.fold_in(_gk, 2), (25000,), 0, 3125, jnp.int32)
        _d = jax.random.randint(jax.random.fold_in(_gk, 3), (25000,), 0, 3125, jnp.int32)
        _loop = jnp.arange(3125, dtype=jnp.int32)
        src = jnp.concatenate([_s, _d, _loop])
        dst = jnp.concatenate([_d, _s, _loop])
        _o = jnp.argsort(dst, stable=True)
        src = src[_o]
        dst = dst[_o]
        edge_attr_2 = jax.random.uniform(jax.random.fold_in(_gk, 11), (53125, 2), jnp.float32, 0.0, 1)
        edge_attr_32 = 0.000196303 + 1.00016 * jax.random.normal(jax.random.fold_in(_gk, 12), (53125, 32), jnp.float32)
        return (x, src, dst, edge_attr_2, edge_attr_32)
    x, src, dst, edge_attr_2, edge_attr_32 = _rec_inputs()

    def _L0_gnn_setup():
        import jax, jax.numpy as jnp
        import numpy as np
        N = 3125
        E = 50000
        F_IN = 64
        HID = 128
        OUT = 64

        def _sage(x, src, dst, Wn, bn, Wr):
            msg = x[src]
            agg = jax.ops.segment_sum(msg, dst, num_segments=N)
            deg = jax.ops.segment_sum(jnp.ones((src.shape[0],), x.dtype), dst, num_segments=N)
            mean = agg / jnp.maximum(deg, 1.0)[:, None]
            return mean @ Wn + bn + x @ Wr
        key = jax.random.key(seed)
        ks = jax.random.split(key, 12)
        s = lambda k, i, o: jax.random.normal(k, (i, o), jnp.float32) / np.sqrt(i)
        x = jax.random.normal(ks[0], (N, F_IN), jnp.float32)
        edge_index = jax.random.randint(ks[1], (2, E), 0, N, dtype=jnp.int64)
        return {'x': x, 'edge_index': edge_index, 'W1n': s(ks[2], F_IN, HID), 'b1n': jnp.zeros((HID,), jnp.float32), 'W1r': s(ks[3], F_IN, HID), 'Wl1': s(ks[4], F_IN, HID), 'bl1': jnp.zeros((HID,), jnp.float32), 'W2n': s(ks[5], HID, OUT), 'b2n': jnp.zeros((OUT,), jnp.float32), 'W2r': s(ks[6], HID, OUT), 'Wl2': s(ks[7], HID, OUT), 'bl2': jnp.zeros((OUT,), jnp.float32)}
    _L0_gnn_all = _L0_gnn_setup()
    _L0_gnn_in = {k: v for k, v in _L0_gnn_all.items() if k in ('W1n', 'b1n', 'W1r', 'Wl1', 'bl1', 'W2n', 'b2n', 'W2r', 'Wl2', 'bl2')}
    del _L0_gnn_all

    def _L1_gnn_setup():
        import jax, jax.numpy as jnp
        import numpy as np
        N, E = (50000, 25000)
        H, KC, EC, NH = (64, 64, 32, 4)
        HPH, KPH = (H // NH, KC // NH)

        def ssp(x):
            return jax.nn.softplus(x) - jnp.log(2.0).astype(x.dtype)

        def grouped_lin(x, w):
            return jnp.einsum('nhi,hoi->nho', x, w)

        def lin(x, w, b):
            return x @ w.T + b

        def segment_softmax(logits, seg, num_segments):
            m = jax.ops.segment_max(logits, seg, num_segments=num_segments)
            m = jnp.where(jnp.isfinite(m), m, 0.0)
            e = jnp.exp(logits - m[seg])
            s = jax.ops.segment_sum(e, seg, num_segments=num_segments)
            return e / s[seg]
        key = jax.random.key(seed)
        ks = jax.random.split(key, 24)
        sc = 0.05
        inp = {'x': jax.random.normal(ks[0], (N, H), jnp.float32), 'edge_index': jax.random.randint(ks[1], (2, E), 0, N, jnp.int64), 'edge_attr': jax.random.normal(ks[2], (E, EC), jnp.float32), 'k_w': jax.random.normal(ks[3], (NH, KPH, HPH), jnp.float32) * sc, 'q_w': jax.random.normal(ks[4], (NH, KPH, HPH), jnp.float32) * sc, 'v_w': jax.random.normal(ks[5], (NH, HPH, HPH), jnp.float32) * sc, 'wkn_w1': jax.random.normal(ks[6], (KPH, EC), jnp.float32) * sc, 'wkn_b1': jnp.zeros((KPH,), jnp.float32), 'wkn_w2': jax.random.normal(ks[7], (KPH, KPH), jnp.float32) * sc, 'wkn_b2': jnp.zeros((KPH,), jnp.float32), 'wkl_w': jax.random.normal(ks[8], (KPH, KPH), jnp.float32) * sc, 'wkl_b': jnp.zeros((KPH,), jnp.float32), 'wvn_w1': jax.random.normal(ks[9], (HPH, EC), jnp.float32) * sc, 'wvn_b1': jnp.zeros((HPH,), jnp.float32), 'wvn_w2': jax.random.normal(ks[10], (HPH, HPH), jnp.float32) * sc, 'wvn_b2': jnp.zeros((HPH,), jnp.float32), 'wvl_w': jax.random.normal(ks[11], (HPH, HPH), jnp.float32) * sc, 'wvl_b': jnp.zeros((HPH,), jnp.float32), 'cen_w': jax.random.normal(ks[12], (H, H), jnp.float32) * sc, 'cen_b': jnp.zeros((H,), jnp.float32), 'out_w': jax.random.normal(ks[13], (H, H), jnp.float32) * sc, 'out_b': jnp.zeros((H,), jnp.float32)}
        return inp
    _L1_gnn_all = _L1_gnn_setup()
    _L1_gnn_in = {k: v for k, v in _L1_gnn_all.items() if k in ('k_w', 'q_w', 'v_w', 'wkn_w1', 'wkn_b1', 'wkn_w2', 'wkn_b2', 'wkl_w', 'wkl_b', 'wvn_w1', 'wvn_b1', 'wvn_w2', 'wvn_b2', 'wvl_w', 'wvl_b', 'cen_w', 'cen_b', 'out_w', 'out_b')}
    del _L1_gnn_all

    def _L2_gnn_setup():
        import jax, jax.numpy as jnp
        import numpy as np
        N_NODES = 3125
        N_EDGES = 1250000
        D_FEAT = 64
        UNITS = 64
        key = jax.random.key(seed)
        k1, k2, k3 = jax.random.split(key, 3)
        features = jax.random.normal(k1, (N_NODES, D_FEAT), dtype=jnp.float32)
        edge_index = jax.random.randint(k2, (2, N_EDGES), 0, N_NODES, dtype=jnp.int64)
        weight = jax.random.normal(k3, (D_FEAT, UNITS), dtype=jnp.float32) * (1.0 / np.sqrt(D_FEAT))
        bias = jnp.zeros((UNITS,), dtype=jnp.float32)
        return {'features': features, 'edge_index': edge_index, 'weight': weight, 'bias': bias}
    _L2_gnn_all = _L2_gnn_setup()
    _L2_gnn_in = {k: v for k, v in _L2_gnn_all.items() if k in ('weight', 'bias')}
    del _L2_gnn_all

    def _L3_gnn_setup():
        import jax, jax.numpy as jnp
        import numpy as np
        import math
        N_NODES = 3125
        EMB = 64
        HEADS = 2
        HEAD_DIM = EMB // HEADS
        N_EDGES = 50000
        EDGE_ATTR_DIM = 2
        BN_EPS = 1e-05

        def _layer(x, src, dst, edge_attr, W_kqv, b_kqv, W_edge, b_edge, W_att1, b_att1, W_att2, b_att2, W_out, b_out, bn_gamma, bn_beta):
            N, D = x.shape
            H, E = (HEADS, HEAD_DIM)
            kqv = x @ W_kqv + b_kqv
            q = kqv[dst, :D].reshape(-1, H, E)
            k = kqv[src, D:2 * D].reshape(-1, H, E) / math.sqrt(E)
            v = kqv[src, 2 * D:].reshape(-1, H, E)
            ea = (edge_attr @ W_edge + b_edge).reshape(-1, H, E)
            feat = jnp.concatenate([k, q, jax.nn.relu(ea)], axis=-1)
            h = jax.nn.relu(feat @ W_att1 + b_att1)
            a = (h @ W_att2 + b_att2)[..., 0]
            amax = jax.ops.segment_max(a, dst, num_segments=N)
            ex = jnp.exp(a - amax[dst])
            denom = jax.ops.segment_sum(ex, dst, num_segments=N)
            alpha = ex / denom[dst]
            msg = (alpha[..., None] * v).reshape(-1, H * E)
            msg = msg @ W_out + b_out
            out = jax.ops.segment_sum(msg, dst, num_segments=N)
            out = out + x
            out = out / jnp.sqrt(1.0 + BN_EPS) * bn_gamma + bn_beta
            return out
        key = jax.random.key(seed)
        ks = jax.random.split(key, 16)
        s = 0.05
        inp = {'x': jax.random.normal(ks[0], (N_NODES, EMB), jnp.float32), 'edge_index': jax.random.randint(ks[1], (2, N_EDGES), 0, N_NODES, jnp.int32), 'edge_attr': jax.random.uniform(ks[2], (N_EDGES, EDGE_ATTR_DIM), jnp.float32), 'W_kqv': jax.random.normal(ks[3], (EMB, 3 * EMB), jnp.float32) * s, 'b_kqv': jnp.zeros((3 * EMB,), jnp.float32), 'W_edge': jax.random.normal(ks[4], (EDGE_ATTR_DIM, EMB), jnp.float32) * s, 'b_edge': jnp.zeros((EMB,), jnp.float32), 'W_att1': jax.random.normal(ks[5], (3 * HEAD_DIM, HEAD_DIM), jnp.float32) * s, 'b_att1': jnp.zeros((HEAD_DIM,), jnp.float32), 'W_att2': jax.random.normal(ks[6], (HEAD_DIM, 1), jnp.float32) * s, 'b_att2': jnp.zeros((1,), jnp.float32), 'W_out': jax.random.normal(ks[7], (EMB, EMB), jnp.float32) * s, 'b_out': jnp.zeros((EMB,), jnp.float32), 'bn_gamma': jnp.ones((EMB,), jnp.float32), 'bn_beta': jnp.zeros((EMB,), jnp.float32)}
        return inp
    _L3_gnn_all = _L3_gnn_setup()
    _L3_gnn_in = {k: v for k, v in _L3_gnn_all.items() if k in ('W_kqv', 'b_kqv', 'W_edge', 'b_edge', 'W_att1', 'b_att1', 'W_att2', 'b_att2', 'W_out', 'b_out', 'bn_gamma', 'bn_beta')}
    del _L3_gnn_all
    return {'x': x, 'src': src, 'dst': dst, 'edge_attr_2': edge_attr_2, 'edge_attr_32': edge_attr_32, 'L0_gnn_W1n': _L0_gnn_in['W1n'], 'L0_gnn_b1n': _L0_gnn_in['b1n'], 'L0_gnn_W1r': _L0_gnn_in['W1r'], 'L0_gnn_Wl1': _L0_gnn_in['Wl1'], 'L0_gnn_bl1': _L0_gnn_in['bl1'], 'L0_gnn_W2n': _L0_gnn_in['W2n'], 'L0_gnn_b2n': _L0_gnn_in['b2n'], 'L0_gnn_W2r': _L0_gnn_in['W2r'], 'L0_gnn_Wl2': _L0_gnn_in['Wl2'], 'L0_gnn_bl2': _L0_gnn_in['bl2'], 'L1_gnn_k_w': _L1_gnn_in['k_w'], 'L1_gnn_q_w': _L1_gnn_in['q_w'], 'L1_gnn_v_w': _L1_gnn_in['v_w'], 'L1_gnn_wkn_w1': _L1_gnn_in['wkn_w1'], 'L1_gnn_wkn_b1': _L1_gnn_in['wkn_b1'], 'L1_gnn_wkn_w2': _L1_gnn_in['wkn_w2'], 'L1_gnn_wkn_b2': _L1_gnn_in['wkn_b2'], 'L1_gnn_wkl_w': _L1_gnn_in['wkl_w'], 'L1_gnn_wkl_b': _L1_gnn_in['wkl_b'], 'L1_gnn_wvn_w1': _L1_gnn_in['wvn_w1'], 'L1_gnn_wvn_b1': _L1_gnn_in['wvn_b1'], 'L1_gnn_wvn_w2': _L1_gnn_in['wvn_w2'], 'L1_gnn_wvn_b2': _L1_gnn_in['wvn_b2'], 'L1_gnn_wvl_w': _L1_gnn_in['wvl_w'], 'L1_gnn_wvl_b': _L1_gnn_in['wvl_b'], 'L1_gnn_cen_w': _L1_gnn_in['cen_w'], 'L1_gnn_cen_b': _L1_gnn_in['cen_b'], 'L1_gnn_out_w': _L1_gnn_in['out_w'], 'L1_gnn_out_b': _L1_gnn_in['out_b'], 'L2_gnn_weight': _L2_gnn_in['weight'], 'L2_gnn_bias': _L2_gnn_in['bias'], 'L3_gnn_W_kqv': _L3_gnn_in['W_kqv'], 'L3_gnn_b_kqv': _L3_gnn_in['b_kqv'], 'L3_gnn_W_edge': _L3_gnn_in['W_edge'], 'L3_gnn_b_edge': _L3_gnn_in['b_edge'], 'L3_gnn_W_att1': _L3_gnn_in['W_att1'], 'L3_gnn_b_att1': _L3_gnn_in['b_att1'], 'L3_gnn_W_att2': _L3_gnn_in['W_att2'], 'L3_gnn_b_att2': _L3_gnn_in['b_att2'], 'L3_gnn_W_out': _L3_gnn_in['W_out'], 'L3_gnn_b_out': _L3_gnn_in['b_out'], 'L3_gnn_bn_gamma': _L3_gnn_in['bn_gamma'], 'L3_gnn_bn_beta': _L3_gnn_in['bn_beta']}

def reference(x, src, dst, edge_attr_2, edge_attr_32, L0_gnn_W1n, L0_gnn_b1n, L0_gnn_W1r, L0_gnn_Wl1, L0_gnn_bl1, L0_gnn_W2n, L0_gnn_b2n, L0_gnn_W2r, L0_gnn_Wl2, L0_gnn_bl2, L1_gnn_k_w, L1_gnn_q_w, L1_gnn_v_w, L1_gnn_wkn_w1, L1_gnn_wkn_b1, L1_gnn_wkn_w2, L1_gnn_wkn_b2, L1_gnn_wkl_w, L1_gnn_wkl_b, L1_gnn_wvn_w1, L1_gnn_wvn_b1, L1_gnn_wvn_w2, L1_gnn_wvn_b2, L1_gnn_wvl_w, L1_gnn_wvl_b, L1_gnn_cen_w, L1_gnn_cen_b, L1_gnn_out_w, L1_gnn_out_b, L2_gnn_weight, L2_gnn_bias, L3_gnn_W_kqv, L3_gnn_b_kqv, L3_gnn_W_edge, L3_gnn_b_edge, L3_gnn_W_att1, L3_gnn_b_att1, L3_gnn_W_att2, L3_gnn_b_att2, L3_gnn_W_out, L3_gnn_b_out, L3_gnn_bn_gamma, L3_gnn_bn_beta):
    import jax
    import jax.numpy as jnp

    def _L0_gnn_ref(x, edge_index, W1n, b1n, W1r, Wl1, bl1, W2n, b2n, W2r, Wl2, bl2):
        import jax, jax.numpy as jnp
        import numpy as np
        N = 3125
        E = 50000
        F_IN = 64
        HID = 128
        OUT = 64

        def _sage(x, src, dst, Wn, bn, Wr):
            msg = x[src]
            agg = jax.ops.segment_sum(msg, dst, num_segments=N)
            deg = jax.ops.segment_sum(jnp.ones((src.shape[0],), x.dtype), dst, num_segments=N)
            mean = agg / jnp.maximum(deg, 1.0)[:, None]
            return mean @ Wn + bn + x @ Wr
        src, dst = (edge_index[0], edge_index[1])
        h = _sage(x, src, dst, W1n, b1n, W1r) + (x @ Wl1 + bl1)
        h = jax.nn.relu(h)
        out = _sage(h, src, dst, W2n, b2n, W2r) + (h @ Wl2 + bl2)
        return out

    def _L1_gnn_ref(x, edge_index, edge_attr, k_w, q_w, v_w, wkn_w1, wkn_b1, wkn_w2, wkn_b2, wkl_w, wkl_b, wvn_w1, wvn_b1, wvn_w2, wvn_b2, wvl_w, wvl_b, cen_w, cen_b, out_w, out_b):
        import jax, jax.numpy as jnp
        import numpy as np
        N, E = (50000, 25000)
        H, KC, EC, NH = (64, 64, 32, 4)
        HPH, KPH = (H // NH, KC // NH)

        def ssp(x):
            return jax.nn.softplus(x) - jnp.log(2.0).astype(x.dtype)

        def grouped_lin(x, w):
            return jnp.einsum('nhi,hoi->nho', x, w)

        def lin(x, w, b):
            return x @ w.T + b

        def segment_softmax(logits, seg, num_segments):
            m = jax.ops.segment_max(logits, seg, num_segments=num_segments)
            m = jnp.where(jnp.isfinite(m), m, 0.0)
            e = jnp.exp(logits - m[seg])
            s = jax.ops.segment_sum(e, seg, num_segments=num_segments)
            return e / s[seg]
        n = x.shape[0]
        row, col = (edge_index[0], edge_index[1])
        xh = x.reshape(n, NH, HPH)
        h_keys = grouped_lin(xh, k_w)
        h_queries = grouped_lin(xh, q_w)
        h_values = grouped_lin(xh, v_w)
        W_k = lin(ssp(lin(edge_attr, wkn_w1, wkn_b1)), wkn_w2, wkn_b2)
        keys_j = lin(W_k[:, None, :] * h_keys[col], wkl_w, wkl_b)
        queries_i = h_queries[row]
        qk_ij = jnp.sum(queries_i * keys_j, axis=-1)
        alpha = segment_softmax(qk_ij, row, n)
        W_v = lin(ssp(lin(edge_attr, wvn_w1, wvn_b1)), wvn_w2, wvn_b2)
        msg_j = lin(W_v[:, None, :] * h_values[col], wvl_w, wvl_b)
        msg_j = alpha[:, :, None] * msg_j
        aggr = jax.ops.segment_sum(msg_j, row, num_segments=n).reshape(n, H)
        out = lin(x, cen_w, cen_b) + aggr
        return lin(ssp(out), out_w, out_b)

    def _L2_gnn_ref(features, edge_index, weight, bias):
        import jax, jax.numpy as jnp
        import numpy as np
        N_NODES = 3125
        N_EDGES = 1250000
        D_FEAT = 64
        UNITS = 64
        num_nodes = features.shape[0]
        row = edge_index[0]
        col = edge_index[1]
        ones = jnp.ones(row.shape[0], dtype=features.dtype)
        degrees = jax.ops.segment_sum(ones, row, num_segments=num_nodes)
        deg_inv_sqrt = jnp.power(degrees, -0.5)
        deg_inv_sqrt = jnp.where(jnp.isfinite(deg_inv_sqrt), deg_inv_sqrt, 0.0)
        w = deg_inv_sqrt[row] * deg_inv_sqrt[col]
        msgs = features[col] * w[:, None]
        propagated = jax.ops.segment_sum(msgs, row, num_segments=num_nodes)
        h = propagated @ weight + bias
        return jax.nn.relu(h)

    def _L3_gnn_ref(x, edge_index, edge_attr, W_kqv, b_kqv, W_edge, b_edge, W_att1, b_att1, W_att2, b_att2, W_out, b_out, bn_gamma, bn_beta):
        import jax, jax.numpy as jnp
        import numpy as np
        import math
        N_NODES = 3125
        EMB = 64
        HEADS = 2
        HEAD_DIM = EMB // HEADS
        N_EDGES = 50000
        EDGE_ATTR_DIM = 2
        BN_EPS = 1e-05

        def _layer(x, src, dst, edge_attr, W_kqv, b_kqv, W_edge, b_edge, W_att1, b_att1, W_att2, b_att2, W_out, b_out, bn_gamma, bn_beta):
            N, D = x.shape
            H, E = (HEADS, HEAD_DIM)
            kqv = x @ W_kqv + b_kqv
            q = kqv[dst, :D].reshape(-1, H, E)
            k = kqv[src, D:2 * D].reshape(-1, H, E) / math.sqrt(E)
            v = kqv[src, 2 * D:].reshape(-1, H, E)
            ea = (edge_attr @ W_edge + b_edge).reshape(-1, H, E)
            feat = jnp.concatenate([k, q, jax.nn.relu(ea)], axis=-1)
            h = jax.nn.relu(feat @ W_att1 + b_att1)
            a = (h @ W_att2 + b_att2)[..., 0]
            amax = jax.ops.segment_max(a, dst, num_segments=N)
            ex = jnp.exp(a - amax[dst])
            denom = jax.ops.segment_sum(ex, dst, num_segments=N)
            alpha = ex / denom[dst]
            msg = (alpha[..., None] * v).reshape(-1, H * E)
            msg = msg @ W_out + b_out
            out = jax.ops.segment_sum(msg, dst, num_segments=N)
            out = out + x
            out = out / jnp.sqrt(1.0 + BN_EPS) * bn_gamma + bn_beta
            return out
        src, dst = (edge_index[0], edge_index[1])
        return _layer(x, src, dst, edge_attr, W_kqv, b_kqv, W_edge, b_edge, W_att1, b_att1, W_att2, b_att2, W_out, b_out, bn_gamma, bn_beta)
    edge_index = jnp.stack([src, dst])
    h = jnp.maximum(_layernorm(x, axis=-1), 0.0)
    x = x + _L0_gnn_ref(h, edge_index, L0_gnn_W1n, L0_gnn_b1n, L0_gnn_W1r, L0_gnn_Wl1, L0_gnn_bl1, L0_gnn_W2n, L0_gnn_b2n, L0_gnn_W2r, L0_gnn_Wl2, L0_gnn_bl2)
    h = jnp.maximum(_layernorm(x, axis=-1), 0.0)
    x = x + _L1_gnn_ref(h, edge_index, edge_attr_32, L1_gnn_k_w, L1_gnn_q_w, L1_gnn_v_w, L1_gnn_wkn_w1, L1_gnn_wkn_b1, L1_gnn_wkn_w2, L1_gnn_wkn_b2, L1_gnn_wkl_w, L1_gnn_wkl_b, L1_gnn_wvn_w1, L1_gnn_wvn_b1, L1_gnn_wvn_w2, L1_gnn_wvn_b2, L1_gnn_wvl_w, L1_gnn_wvl_b, L1_gnn_cen_w, L1_gnn_cen_b, L1_gnn_out_w, L1_gnn_out_b)
    h = jnp.maximum(_layernorm(x, axis=-1), 0.0)
    x = x + _L2_gnn_ref(h, edge_index, L2_gnn_weight, L2_gnn_bias)
    h = jnp.maximum(_layernorm(x, axis=-1), 0.0)
    x = x + _L3_gnn_ref(h, edge_index, edge_attr_2, L3_gnn_W_kqv, L3_gnn_b_kqv, L3_gnn_W_edge, L3_gnn_b_edge, L3_gnn_W_att1, L3_gnn_b_att1, L3_gnn_W_att2, L3_gnn_b_att2, L3_gnn_W_out, L3_gnn_b_out, L3_gnn_bn_gamma, L3_gnn_bn_beta)
    return x

_drawn_inputs = setup_inputs


def setup_inputs(seed=0):
    import zlib

    import numpy as np

    out = dict(_drawn_inputs(seed))
    spreads = {'L0_gnn_b1n': (0.0, 0.1),
     'L0_gnn_bl1': (0.0, 0.1),
     'L0_gnn_b2n': (0.0, 0.1),
     'L0_gnn_bl2': (0.0, 0.1),
     'L1_gnn_wkn_b1': (0.0, 0.8),
     'L1_gnn_wkn_b2': (0.0, 0.8),
     'L1_gnn_wkl_b': (0.0, 2.0),
     'L1_gnn_wvn_b1': (0.0, 0.8),
     'L1_gnn_wvn_b2': (0.0, 0.8),
     'L1_gnn_wvl_b': (0.0, 2.0),
     'L1_gnn_cen_b': (0.0, 2.0),
     'L1_gnn_out_b': (0.0, 0.8),
     'L2_gnn_bias': (0.0, 0.8),
     'L3_gnn_b_kqv': (0.0, 2.0),
     'L3_gnn_b_edge': (0.0, 2.0),
     'L3_gnn_b_att1': (0.0, 2.0),
     'L3_gnn_b_out': (0.0, 0.1),
     'L3_gnn_bn_gamma': (1.0, 0.2),
     'L3_gnn_bn_beta': (0.0, 0.8)}
    factors = {'edge_attr_2': 64.0,
     'edge_attr_32': 8.0,
     'L1_gnn_k_w': 8.0,
     'L1_gnn_q_w': 8.0,
     'L1_gnn_v_w': 8.0,
     'L1_gnn_wkn_w1': 8.0,
     'L1_gnn_wkn_w2': 8.0,
     'L1_gnn_wkl_w': 8.0,
     'L1_gnn_wvn_w1': 8.0,
     'L1_gnn_wvn_w2': 8.0,
     'L1_gnn_wvl_w': 8.0,
     'L3_gnn_W_edge': 64.0,
     'L3_gnn_W_att1': 64.0,
     'L3_gnn_W_att2': 64.0,
     'L1_gnn_cen_w': 7.255,
     'L3_gnn_W_kqv': 6.916}
    for name, (base, spread) in spreads.items():
        noise = np.random.default_rng([zlib.crc32(name.encode()), seed]).standard_normal(out[name].shape)
        drawn = base * np.exp(spread * noise) if base else spread * noise
        out[name] = jnp.asarray(drawn.astype(out[name].dtype))
    for name, factor in factors.items():
        out[name] = (out[name] * factor).astype(out[name].dtype)
    return out
```

```python
from contextlib import ExitStack

import concourse.bass as bass
from concourse import mybir

ALU = mybir.AluOpType
ACT = mybir.ActivationFunctionType
F32 = mybir.dt.float32
BF16 = mybir.dt.bfloat16
I32 = mybir.dt.int32
AX = mybir.AxisListType.X

P = 128
N, E = 3125, 53125
NT = -(-N // P)
NP = NT * P
CH = 416
EP = CH * P
HALF = EP // 2
PAD = NP - 1
D = 64
U = 8
G = CH // U
FAR = -1.0e30
LN2 = 0.6931471805599453
EPS = 1e-5

SRC, DST = 0, 1


def done(k):
    return k + 3


def freed(k):
    return k + 1


def flat(ap):
    return ap.rearrange("p a b -> p (a b)")


class Parts:
    pass


class Stage:

    def __init__(self, nc, ctx, name):
        self.nc, self.ctx, self.name, self.sems = nc, ctx, name, []

    def sb(self, name, shape, dt=F32):
        return self.ctx.enter_context(self.nc.sbuf_tensor(f"{self.name}_{name}", shape, dt))

    def ps(self, name, shape, dt=F32):
        return self.ctx.enter_context(self.nc.psum_tensor(f"{self.name}_{name}", shape, dt))

    def sem(self, name):
        self.sems.append(self.ctx.enter_context(self.nc.semaphore(f"{self.name}_{name}")))
        return self.sems[-1]

    def gather_sem(self, name):
        return self.nc.alloc_semaphore(f"{self.name}_{name}")

    def sb2(self, name, shape, dt=F32):
        return [self.sb(f"{name}{b}", shape, dt) for b in range(2)]

    def ps2(self, name, shape, dt=F32):
        return [self.ps(f"{name}{b}", shape, dt) for b in range(2)]

    def sem2(self, name):
        return [self.sem(f"{name}{b}") for b in range(2)]

    def block(self):
        self.ctx.callback(self.clear)
        return self.ctx.enter_context(self.nc.Block())

    def clear(self):
        for s in self.sems:
            self.nc.gpsimd.sem_clear(s)
        self.nc.all_engine_barrier()


class Steps:

    def __init__(self, eng, sem, at=0):
        self.eng, self.sem, self.n = eng, sem, at

    def __call__(self, ins):
        self.n += 1
        ins.then_inc(self.sem, 1)
        self.eng.wait_ge(self.sem, self.n)


def make_constants(nc, name, k):
    with ExitStack() as ctx:
        at = Stage(nc, ctx, name)
        col_i = at.sb("col_i", [P, P], I32)
        row_i = at.sb("row_i", [P, P], I32)
        row_f = at.sb("row_f", [P, P])
        iotas = at.sem("iotas")
        made = at.sem("made")
        block = at.block()

        @block.gpsimd
        def _(pool):
            nc.gpsimd.iota(col_i[:], pattern=[[1, P]], base=0, channel_multiplier=0).then_inc(iotas, 1)
            nc.gpsimd.iota(row_i[:], pattern=[[0, P]], base=0, channel_multiplier=1).then_inc(iotas, 1)

        @block.vector
        def _(dve):
            step = Steps(dve, made)
            dve.wait_ge(iotas, 2)
            step(nc.vector.tensor_copy(k.count[:], col_i[:]))
            step(nc.vector.tensor_copy(row_f[:], row_i[:]))
            step(nc.vector.tensor_tensor(k.before[:], row_f[:], k.count[:], ALU.is_lt))
            step(nc.vector.tensor_tensor(k.upto[:], row_f[:], k.count[:], ALU.is_le))
            step(nc.vector.tensor_tensor(k.ident[:], row_f[:], k.count[:], ALU.is_equal))
            step(nc.vector.tensor_copy(k.before16[:], k.before[:]))
            step(nc.vector.memset(k.ones[:], 1.0))
            step(nc.vector.tensor_copy(k.ones16[:], k.ones[:]))


def make_records(nc, name, src, dst, attr, width, record):
    per, left = E // P, E % P
    assert per + 1 == CH
    with ExitStack() as ctx:
        at = Stage(nc, ctx, name)
        rec = at.sb("rec", [P, CH, width], I32)
        ends = at.sb("ends", [P, 2, CH], I32)
        feat = at.sb("feat", [P, CH, width - 2])
        loaded = at.sem("loaded")
        padded = at.sem("padded")
        packed = at.sem("packed")
        stored = at.sem("stored")
        block = at.block()
        a = attr.rearrange("e f -> (e f)")
        f = width - 2

        @block.vector
        def _(dve):
            nc.vector.memset(ends[:, :, per:CH], PAD).then_inc(padded, 1)
            nc.vector.memset(feat[:, per:CH, :], 0.0).then_inc(padded, 1)
            dve.wait_ge(loaded, 16 * 6)
            for column in (SRC, DST):
                nc.vector.tensor_copy(rec[:, :, column], ends[:, column, :]).then_inc(packed, 1)

        @block.scalar
        def _(act):
            act.wait_ge(loaded, 16 * 6)
            nc.scalar.copy(rec[:, :, 2:width].bitcast(F32), feat[:]).then_inc(packed, 1)

        @block.sync
        def _(sp):
            sp.wait_ge(padded, 2)
            for column, ap in ((SRC, src), (DST, dst)):
                sp.dma_start(ends[:, column, 0:per], ap[0:per * P].rearrange("(p j) -> p j", p=P)).then_inc(loaded, 16)
                sp.dma_start(ends[0:left, column, per:CH], ap[per * P:E].rearrange("(p j) -> p j", j=1)).then_inc(loaded, 16)
            sp.dma_start(feat[:, 0:per, :], a[0:per * P * f].rearrange("(p j f) -> p j f", p=P, f=f)).then_inc(loaded, 16)
            sp.dma_start(feat[0:left, per:CH, :], a[per * P * f:E * f].rearrange("(p j f) -> p j f", p=left, f=f)).then_inc(loaded, 16)
            sp.wait_ge(packed, 3)
            sp.dma_start(record[0:per * P, :].rearrange("(p j) w -> p j w", p=P), rec[:, 0:per, :]).then_inc(stored, 16)
            sp.dma_start(record[per * P:EP, :].rearrange("(p j) w -> p j w", j=1), rec[:, per:CH, :]).then_inc(stored, 16)
            sp.wait_ge(stored, 32)


def count_digits(nc, name, k, record, column, shift, base, node_count):
    with ExitStack() as ctx:
        at = Stage(nc, ctx, name)
        key = at.sb2("key", [P, U, 2], I32)
        dig_i = at.sb2("dig_i", [P, U], I32)
        dig = at.sb2("dig", [P, U])
        hot = at.sb2("hot", [P, U, P], BF16)
        top_i = at.sb2("top_i", [P, U], I32)
        top = at.sb2("top", [P, U])
        hot_top = at.sb2("hot_top", [P, U, NT], BF16)
        counts = at.sb("counts", [P, CH])
        upto = at.sb("upto_chunk", [P, CH])
        no_data = at.sb("no_data", [P, CH])
        chunk_ps = at.ps2("chunk_ps", [P, 512])
        node_ps = at.ps2("node_ps", [P, 512])
        start_ps = at.ps("start_ps", [P, 512])
        sem = at.sem
        key_in = at.sem2("key_in")
        split, digits, top_digits, hot_made = sem("split"), sem("digits"), sem("top_digits"), sem("hot_made")
        tops_split, top_hot = sem("tops_split"), sem("top_hot")
        counted, copied, added, scanned, summed = sem("counted"), sem("copied"), sem("added"), sem("scanned"), sem("summed")
        block = at.block()
        keys = record.rearrange("(c p) w -> p c w", p=P)

        @block.sync
        def _(sp):
            for b in range(2):
                sp.dma_start(key[b][:], keys[:, b * U:(b + 1) * U, 0:2]).then_inc(key_in[b], 16)
            with sp.Fori(0, G // 2 - 1) as i:
                for b in range(2):
                    g = 2 * i + b
                    sp.wait_ge(split, done(g))
                    if node_count is not None:
                        sp.wait_ge(tops_split, done(g))
                    sp.dma_start(key[b][:], keys[:, bass.ds((g + 2) * U, U), 0:2]).then_inc(key_in[b], 16)

        @block.vector
        def _(dve):
            dve.sem_inc(split, 2)
            dve.sem_inc(digits, 2)
            dve.sem_inc(hot_made, 2)
            dve.sem_inc(tops_split, 2)
            dve.sem_inc(top_digits, 2)
            dve.sem_inc(top_hot, 2)
            if node_count is not None:
                nc.vector.memset(node_count[:], 0.0).then_inc(added, 1)
            with dve.Fori(0, G // 2) as i:
                for b in range(2):
                    g = 2 * i + b
                    dve.wait_ge(key_in[b], 16 * (i + 1))
                    dve.wait_ge(counted, freed(g))
                    nc.vector.tensor_scalar(dig_i[b][:], key[b][:, :, column], shift, P - 1, ALU.logical_shift_right, ALU.bitwise_and).then_inc(split, 1)
                    dve.wait_ge(split, done(g))
                    nc.vector.tensor_copy(dig[b][:], dig_i[b][:]).then_inc(digits, 1)
                    dve.wait_ge(digits, done(g))
                    nc.vector.tensor_tensor(hot[b][:], dig[b][:].unsqueeze(2).to_broadcast([P, U, P]),
                                            k.count[:].unsqueeze(1).to_broadcast([P, U, P]), ALU.is_equal).then_inc(hot_made, 1)
                    if node_count is not None:
                        nc.vector.tensor_scalar(top_i[b][:], key[b][:, :, column], 7, P - 1, ALU.logical_shift_right, ALU.bitwise_and).then_inc(tops_split, 1)
                        dve.wait_ge(tops_split, done(g))
                        nc.vector.tensor_copy(top[b][:], top_i[b][:]).then_inc(top_digits, 1)
                        dve.wait_ge(top_digits, done(g))
                        nc.vector.tensor_tensor(hot_top[b][:], top[b][:].unsqueeze(2).to_broadcast([P, U, NT]),
                                                k.count[:, 0:NT].unsqueeze(1).to_broadcast([P, U, NT]), ALU.is_equal).then_inc(top_hot, 1)
                        dve.wait_ge(counted, done(g))
                        dve.wait_ge(added, g + 1)
                        nc.vector.tensor_tensor(node_count[:], node_count[:], node_ps[b][:, 0:NT], ALU.add).then_inc(added, 1)
            nc.vector.memset(no_data[:], 0.0).then_inc(scanned, 1)
            dve.wait_ge(scanned, 1)
            dve.wait_ge(copied, G + 2)
            nc.vector.tensor_tensor_scan(upto[:], counts[:], no_data[:], 0.0, ALU.add, ALU.add).then_inc(scanned, 1)
            dve.wait_ge(scanned, 2)
            nc.vector.tensor_tensor(no_data[:], upto[:], counts[:], ALU.subtract).then_inc(scanned, 1)
            dve.wait_ge(scanned, 3)
            dve.wait_ge(summed, 1)
            nc.vector.tensor_scalar(base[:], no_data[:], start_ps[:, 0:1], None, ALU.add).then_inc(scanned, 1)

        @block.tensor
        def _(pe):
            pe.sem_inc(counted, 2)
            with pe.Fori(0, G // 2) as i:
                for b in range(2):
                    g = 2 * i + b
                    if node_count is not None:
                        pe.wait_ge(top_hot, done(g))
                        if b == 0:
                            pe.wait_ge(added, g + 1)
                    pe.wait_ge(copied, freed(g))
                    pe.wait_ge(hot_made, done(g))
                    if node_count is not None:
                        for u in range(U):
                            nc.tensor.matmul(node_ps[b][:, 0:NT], hot[b][:, u, :], hot_top[b][:, u, :], start=(u == 0), stop=(u == U - 1))
                    for u in range(U):
                        last = nc.tensor.matmul(chunk_ps[b][:, u:u + 1], hot[b][:, u, :], k.ones16[:, 0:1], start=True, stop=True)
                    last.then_inc(counted, 1)
            pe.wait_ge(scanned, 2)
            nc.tensor.matmul(start_ps[:, 0:1], k.before[:], upto[:, CH - 1:CH], start=True, stop=True).then_inc(summed, 1)

        @block.scalar
        def _(act):
            act.sem_inc(copied, 2)
            with act.Fori(0, G // 2) as i:
                for b in range(2):
                    g = 2 * i + b
                    act.wait_ge(counted, done(g))
                    nc.scalar.copy(counts[:, bass.ds(g * U, U)], chunk_ps[b][:, 0:U]).then_inc(copied, 1)


def move_records(nc, name, k, record, column, shift, width, base, out):
    with ExitStack() as ctx:
        at = Stage(nc, ctx, name)
        rec = at.sb2("rec", [P, U, width], I32)
        dig_i = at.sb2("dig_i", [P, U], I32)
        dig = at.sb2("dig", [P, U])
        hot = at.sb2("hot", [P, U, P], BF16)
        picked = at.sb2("picked", [P, U, P])
        place = at.sb2("place", [P, U], I32)
        base_g = at.sb2("base_g", [P, U, P])
        gate = at.sb("gate", [P, 2])
        place_ps = at.ps2("place_ps", [P, U, P])
        sem = at.sem
        rec_in = at.sem2("rec_in")
        moved = [at.gather_sem(f"moved{b}") for b in range(2)]
        split, digits, hot_made, based, ranked, pick, placed, gated = (
            sem("split"), sem("digits"), sem("hot_made"), sem("based"), sem("ranked"), sem("pick"), sem("placed"), sem("gated"))
        block = at.block()
        records = record.rearrange("(c p) w -> p c w", p=P)

        @block.sync
        def _(sp):
            for b in range(2):
                sp.dma_start(rec[b][:], records[:, b * U:(b + 1) * U, :]).then_inc(rec_in[b], 16)
            with sp.Fori(0, G // 2 - 1) as i:
                for b in range(2):
                    g = 2 * i + b
                    sp.wait_ge(moved[b], 16 * U * (i + 1))
                    sp.dma_start(rec[b][:], records[:, bass.ds((g + 2) * U, U), :]).then_inc(rec_in[b], 16)

        @block.scalar
        def _(act):
            act.sem_inc(based, 2)
            with act.Fori(0, G // 2) as i:
                for b in range(2):
                    g = 2 * i + b
                    act.wait_ge(ranked, freed(g))
                    nc.scalar.copy(base_g[b][:], base[:, bass.ds(g * U, U)].unsqueeze(2).to_broadcast([P, U, P])).then_inc(based, 1)

        @block.tensor
        def _(pe):
            pe.sem_inc(ranked, 2)
            with pe.Fori(0, G // 2) as i:
                for b in range(2):
                    g = 2 * i + b
                    pe.wait_ge(based, done(g))
                    pe.wait_ge(pick, freed(g))
                    pe.wait_ge(hot_made, done(g))
                    for h in range(2):
                        half = slice(h * U // 2, (h + 1) * U // 2)
                        nc.tensor.matmul(flat(place_ps[b][:, half, :]), k.before16[:], flat(hot[b][:, half, :]), start=True, stop=True, skip_group_check=True)
                        for u in range(h * U // 2, (h + 1) * U // 2):
                            last = nc.tensor.matmul(place_ps[b][:, u, :], base_g[b][:, u, :], k.ident[:], start=False,
                                                    stop=True, skip_group_check=True)
                    last.then_inc(ranked, 1)

        @block.vector
        def _(dve):
            for s in (split, digits, hot_made, pick, placed):
                dve.sem_inc(s, 2)
            with dve.Fori(0, G // 2) as i:
                for b in range(2):
                    g = 2 * i + b
                    dve.wait_ge(rec_in[b], 16 * (i + 1))
                    dve.wait_ge(placed, freed(g))
                    nc.vector.tensor_scalar(dig_i[b][:], rec[b][:, :, column], shift, P - 1, ALU.logical_shift_right, ALU.bitwise_and).then_inc(split, 1)
                    dve.wait_ge(split, done(g))
                    nc.vector.tensor_copy(dig[b][:], dig_i[b][:]).then_inc(digits, 1)
                    dve.wait_ge(digits, done(g))
                    nc.vector.tensor_tensor(hot[b][:], dig[b][:].unsqueeze(2).to_broadcast([P, U, P]),
                                            k.count[:].unsqueeze(1).to_broadcast([P, U, P]), ALU.is_equal).then_inc(hot_made, 1)
                    dve.wait_ge(hot_made, done(g))
                    dve.wait_ge(ranked, done(g))
                    nc.vector.tensor_tensor(picked[b][:], place_ps[b][:], hot[b][:], ALU.mult).then_inc(pick, 1)
                    dve.wait_ge(pick, done(g))
                    with nc.allow_low_precision(reason="whole numbers below 2**24 sum in float32 and land as integers"):
                        nc.vector.tensor_reduce(place[b][:], picked[b][:], AX, ALU.add).then_inc(placed, 1)

        @block.gpsimd
        def _(pool):
            nc.gpsimd.memset(gate[:], 0.0).then_inc(gated, 1)
            with pool.Fori(0, G // 2) as i:
                for b in range(2):
                    g = 2 * i + b
                    pool.wait_ge(gated, g + 1)
                    pool.wait_ge(rec_in[b], 16 * (i + 1))
                    pool.wait_ge(placed, done(g))
                    nc.gpsimd.tensor_tensor(gate[:, 0:1], gate[:, 1:2], gate[:, 1:2], ALU.add).then_inc(gated, 1)
                    for u in range(U):
                        nc.gpsimd.indirect_dma_start(out=out, out_offset=bass.IndirectOffsetOnAxis(ap=place[b][:, u:u + 1], axis=0),
                                                     in_=rec[b][:, u, :], in_offset=None).then_inc(moved[b], 16)
            for b in range(2):
                pool.wait_ge(moved[b], 16 * U * (G // 2))


def sort_records(nc, name, k, record, column, width, middle, out, node_count):
    with nc.sbuf_tensor(f"{name}_base", [P, CH], F32) as base:
        count_digits(nc, f"{name}_lane_count", k, record, column, 0, base, node_count)
        move_records(nc, f"{name}_lane_move", k, record, column, 0, width, base, middle)
        count_digits(nc, f"{name}_tile_count", k, middle, column, 7, base, None)
        move_records(nc, f"{name}_tile_move", k, middle, column, 7, width, base, out)


def mark_segments(nc, name, k, record, column, node_count, last_edge, has_edges, crosses, keep_row, far_row):
    with ExitStack() as ctx:
        at = Stage(nc, ctx, name)
        sb = at.sb
        sem = at.sem
        here, prior = sb("here", [P, CH, 2], I32), sb("prior", [P, CH, 2], I32)
        keep, far = sb("keep", [P, CH]), sb("far", [P, CH])
        zeros, tile_upto, ends, starts = sb("zeros", [P, NT]), sb("tile_upto", [P, NT]), sb("ends", [P, NT]), sb("starts", [P, NT])
        ends_ps = at.ps("ends_ps", [P, 512])
        sums_ps = at.ps("sums_ps", [P, 512])
        loaded, cleared, summed, marked, stored = sem("loaded"), sem("cleared"), sem("summed"), sem("marked"), sem("stored")
        block = at.block()

        @block.sync
        def _(sp):
            sp.dma_start(here[:], record[:, 0:2].rearrange("(p j) w -> p j w", p=P)).then_inc(loaded, 16)
            sp.wait_ge(cleared, 1)
            sp.dma_start(prior[0:1, 1:CH, :], record[0:CH - 1, 0:2].rearrange("(p j) w -> p j w", p=1)).then_inc(loaded, 16)
            sp.dma_start(prior[1:P, :, :], record[CH - 1:EP - 1, 0:2].rearrange("(p j) w -> p j w", p=P - 1)).then_inc(loaded, 16)
            sp.wait_ge(marked, 2)
            sp.dma_start(keep_row.rearrange("(p j) -> p j", p=P), keep[:]).then_inc(stored, 16)
            sp.dma_start(far_row.rearrange("(p j) -> p j", p=P), far[:]).then_inc(stored, 16)
            sp.wait_ge(stored, 32)

        @block.tensor
        def _(pe):
            nc.tensor.matmul(ends_ps[:, 0:NT], k.upto[:], node_count[:], start=True, stop=True).then_inc(summed, 1)
            nc.tensor.matmul(sums_ps[:, 0:NT], k.ones[:], node_count[:], start=True, stop=True).then_inc(summed, 1)

        @block.vector
        def _(dve):
            nc.vector.memset(prior[0:1, 0:1, :], -1).then_inc(cleared, 1)
            step = Steps(dve, marked)
            dve.wait_ge(loaded, 16 * 3)
            step(nc.vector.tensor_tensor(keep[:], here[:, :, column], prior[:, :, column], ALU.is_equal))
            step(nc.vector.tensor_scalar(far[:], keep[:], -1.0, -FAR, ALU.add, ALU.mult))
            step(nc.vector.memset(zeros[:], 0.0))
            dve.wait_ge(summed, 2)
            step(nc.vector.tensor_tensor_scan(tile_upto[:], sums_ps[:, 0:NT], zeros[:], 0.0, ALU.add, ALU.add))
            step(nc.vector.tensor_tensor(ends[:], tile_upto[:], sums_ps[:, 0:NT], ALU.subtract))
            step(nc.vector.tensor_tensor(ends[:], ends[:], ends_ps[:, 0:NT], ALU.add))
            step(nc.vector.tensor_tensor(starts[:], ends[:], node_count[:], ALU.subtract))
            step(nc.vector.tensor_scalar(last_edge[:], ends[:], -1.0, 0.0, ALU.add, ALU.max))
            step(nc.vector.tensor_scalar(has_edges[:], node_count[:], 1.0, None, ALU.min))
            step(nc.vector.tensor_scalar(starts[:], starts[:], float(HALF), None, ALU.is_lt))
            step(nc.vector.tensor_scalar(ends[:], ends[:], float(HALF), None, ALU.is_gt))
            step(nc.vector.tensor_tensor(crosses[:], starts[:], ends[:], ALU.mult))


def sum_over_edges(nc, name, k, record, ends, table, keep_row, running):
    Q = U // 2
    with ExitStack() as ctx:
        at = Stage(nc, ctx, name)
        rec = at.sb2("rec", [P, 2, Q, 2], I32)
        keep = at.sb2("keep", [P, Q * P])
        rows = at.sb2("rows", [P, Q, 2, D])
        run = at.sb2("run", [P, Q * P])
        back = at.sb2("back", [P, Q, 2, D])
        gate = at.sb("gate", [P, 2])
        rows_ps, back_ps = at.ps2("rows_ps", [P, Q, P]), at.ps2("back_ps", [P, Q, P])
        rec_in, keep_in, gathered, stored = at.sem2("rec_in"), at.sem2("keep_in"), [at.gather_sem(f"gathered{b}") for b in range(2)], at.sem("stored")
        turned, scanned, returned, copied, sent = at.sem("turned"), at.sem("scanned"), at.sem("returned"), at.sem("copied"), at.sem("sent")
        cleared, gated = at.sem("cleared"), at.sem("gated")
        block = at.block()
        records = record.rearrange("(s c p) w -> s p c w", s=2, p=P)
        runs = running.rearrange("(s c p) f -> s p c f", s=2, p=P)

        def load_records(sp, g, b):
            for s in range(2):
                sp.dma_start(rec[b][:, s, :, :], records[s][:, bass.ds(g * Q, Q), 0:2]).then_inc(rec_in[b], 16)

        def load_keep(sp, g, b):
            for s in range(2):
                row = keep_row[s * HALF:(s + 1) * HALF].rearrange("(o e) -> o e", o=1)[:, bass.ds(g * Q * P, Q * P)]
                sp.dma_start(keep[b][s * D:(s + 1) * D, :], row.to_broadcast([D, Q * P])).then_inc(keep_in[b], 16)

        def store(sp, g, b):
            sp.wait_ge(copied, done(g))
            for s in range(2):
                sp.dma_start(runs[s][:, bass.ds(g * Q, Q), :], back[b][:, :, s, :]).then_inc(stored, 16)
            sp.wait_ge(stored, 32 * (g + 1))
            sp.sem_inc(sent, 1)

        @block.sync
        def _(sp):
            sp.sem_inc(sent, 2)
            for b in range(2):
                load_records(sp, b, b)
                load_keep(sp, b, b)
            with sp.Fori(0, G // 2 - 1) as i:
                for b in range(2):
                    g = 2 * i + b
                    sp.wait_ge(gathered[b], 16 * U * (i + 1))
                    load_records(sp, g + 2, b)
                    sp.wait_ge(scanned, done(g))
                    load_keep(sp, g + 2, b)
                    store(sp, g, b)
            for b in range(2):
                store(sp, G - 2 + b, b)

        @block.gpsimd
        def _(pool):
            nc.gpsimd.memset(gate[:], 0.0).then_inc(gated, 1)
            with pool.Fori(0, G // 2) as i:
                for b in range(2):
                    g = 2 * i + b
                    pool.wait_ge(gated, g + 1)
                    pool.wait_ge(turned, freed(g))
                    pool.wait_ge(rec_in[b], 32 * (i + 1))
                    nc.gpsimd.tensor_tensor(gate[:, 0:1], gate[:, 1:2], gate[:, 1:2], ALU.add).then_inc(gated, 1)
                    for u in range(Q):
                        for s in range(2):
                            nc.gpsimd.indirect_dma_start(out=rows[b][:, u, s, :], out_offset=None, in_=table,
                                                         in_offset=bass.IndirectOffsetOnAxis(ap=rec[b][:, s, u, ends:ends + 1], axis=0)).then_inc(gathered[b], 16)

        @block.tensor
        def _(pe):
            pe.sem_inc(turned, 2)
            pe.sem_inc(returned, 2)
            with pe.Fori(0, G // 2) as i:
                for b in range(2):
                    g = 2 * i + b
                    pe.wait_ge(scanned, freed(g))
                    pe.wait_ge(gathered[b], 16 * U * (i + 1))
                    for u in range(Q):
                        last = nc.tensor.transpose(rows_ps[b][:, u, :], flat(rows[b][:, u, :, :]), k.ident[:])
                    last.then_inc(turned, 1)
                    pe.wait_ge(copied, freed(g))
                    pe.wait_ge(scanned, done(g))
                    for u in range(Q):
                        last = nc.tensor.transpose(back_ps[b][:, u, :], run[b][:, u * P:(u + 1) * P], k.ident[:])
                    last.then_inc(returned, 1)

        @block.vector
        def _(dve):
            nc.vector.memset(run[1][:], 0.0).then_inc(cleared, 1)
            dve.wait_ge(cleared, 1)
            dve.sem_inc(scanned, 2)
            with dve.Fori(0, G // 2) as i:
                for b in range(2):
                    g = 2 * i + b
                    dve.wait_ge(keep_in[b], 32 * (i + 1))
                    dve.wait_ge(returned, freed(g))
                    dve.wait_ge(scanned, done(g - 1))
                    dve.wait_ge(turned, done(g))
                    nc.vector.tensor_tensor_scan(run[b][:], keep[b][:], flat(rows_ps[b][:]), run[1 - b][:, Q * P - 1:Q * P],
                                                 ALU.mult, ALU.add).then_inc(scanned, 1)

        @block.scalar
        def _(act):
            act.sem_inc(copied, 2)
            with act.Fori(0, G // 2) as i:
                for b in range(2):
                    g = 2 * i + b
                    act.wait_ge(sent, freed(g))
                    act.wait_ge(returned, done(g))
                    nc.scalar.copy(back[b][:].rearrange("p a s f -> p (a s f)"), flat(back_ps[b][:])).then_inc(copied, 1)


def rows_at_last_edges(nc, name, running, last_edge, out):
    with ExitStack() as ctx:
        at = Stage(nc, ctx, name)
        gathered = at.gather_sem("gathered")
        block = at.block()

        @block.gpsimd
        def _(pool):
            for t in range(NT):
                nc.gpsimd.indirect_dma_start(out=out[:, t, :], out_offset=None, in_=running,
                                             in_offset=bass.IndirectOffsetOnAxis(ap=last_edge[:, t:t + 1], axis=0)).then_inc(gathered, 16)
            pool.wait_ge(gathered, 16 * NT)


def node_sums(nc, name, running, last_edge, has_edges, crosses, scale, out):
    with ExitStack() as ctx:
        at = Stage(nc, ctx, name)
        sums, middle, part = at.sb("sums", [P, NT, D]), at.sb("middle", [P, D]), at.sb("part", [P, NT, D])
        rows_at_last_edges(nc, f"{name}_ends", running, last_edge, sums)
        loaded, stepped = at.sem("loaded"), at.sem("stepped")
        block = at.block()
        wide = lambda col: col[:].unsqueeze(2).to_broadcast([P, NT, D])

        @block.sync
        def _(sp):
            sp.dma_start(middle[:], running[HALF - 1:HALF, :].to_broadcast([P, D])).then_inc(loaded, 16)

        @block.vector
        def _(dve):
            step = Steps(dve, stepped)
            dve.wait_ge(loaded, 16)
            step(nc.vector.tensor_tensor(part[:], middle[:].unsqueeze(1).to_broadcast([P, NT, D]), wide(crosses), ALU.mult))
            step(nc.vector.tensor_tensor(sums[:], sums[:], part[:], ALU.add))
            step(nc.vector.tensor_tensor(sums[:], sums[:], wide(has_edges), ALU.mult))
            step(nc.vector.tensor_tensor(out, sums[:], wide(scale), ALU.mult))


def node_averages(nc, name, running, last_edge, has_edges, out):
    with ExitStack() as ctx:
        at = Stage(nc, ctx, name)
        sums, part = at.sb("sums", [P, NT, 2 * D]), at.sb("part", [P, NT, D])
        rows_at_last_edges(nc, f"{name}_ends", running, last_edge, sums)
        stepped = at.sem("stepped")
        block = at.block()

        @block.vector
        def _(dve):
            step = Steps(dve, stepped)
            step(nc.vector.reciprocal(part[:], sums[:, :, D:2 * D]))
            step(nc.vector.tensor_tensor(part[:], part[:], has_edges[:].unsqueeze(2).to_broadcast([P, NT, D]), ALU.mult))
            step(nc.vector.tensor_tensor(out, sums[:, :, 0:D], part[:], ALU.mult))


def linear(nc, name, k, rows, weights, width, bias, out):
    B = 5
    with ExitStack() as ctx:
        at = Stage(nc, ctx, name)
        held, turned_rows = at.sb("held", [P, B, P]), at.sb("turned_rows", [P, B, P])
        turn_ps, out_ps = at.ps("turn_ps", [P, 8, P]), at.ps("out_ps", [P, 6, 256])
        in_hand, turned, copied, multiplied, added = at.sem("in_hand"), at.sem("turned"), at.sem("copied"), at.sem("multiplied"), at.sem("added")
        block = at.block()

        @block.tensor
        def _(pe):
            pe.sem_inc(turned, 1)
            pe.sem_inc(multiplied, 1)
            with pe.Fori(0, NT // B) as j:
                pe.wait_ge(copied, j + 1)
                pe.wait_ge(in_hand, j + 1)
                for t in range(B):
                    last = nc.tensor.transpose(turn_ps[:, t, :], held[:, t, :], k.ident[:])
                last.then_inc(turned, 1)
                pe.wait_ge(added, j + 1)
                pe.wait_ge(copied, j + 2)
                for t in range(B):
                    last = nc.tensor.matmul(out_ps[:, t, 0:width], turned_rows[:, t, :], weights[:, 0:width], start=True, stop=True)
                last.then_inc(multiplied, 1)

        @block.scalar
        def _(act):
            act.sem_inc(copied, 1)
            with act.Fori(0, NT // B) as j:
                act.wait_ge(turned, j + 1)
                nc.scalar.copy(held[:], rows[:, bass.ds(B * j, B), :]).then_inc(in_hand, 1)
                act.wait_ge(multiplied, j + 1)
                act.wait_ge(turned, j + 2)
                nc.scalar.copy(flat(turned_rows[:]), flat(turn_ps[:, 0:B, :])).then_inc(copied, 1)

        @block.vector
        def _(dve):
            dve.sem_inc(added, 1)
            with dve.Fori(0, NT // B) as j:
                dve.wait_ge(multiplied, j + 2)
                nc.vector.tensor_tensor(out[:, bass.ds(B * j, B), 0:width], out_ps[:, 0:B, 0:width],
                                        bias[:, 0:width].unsqueeze(1).to_broadcast([P, B, width]), ALU.add).then_inc(added, 1)


def layer_norm(nc, step, root, x, out, centred, squares, stat):
    v = nc.vector
    wide = lambda: stat[:].unsqueeze(2).to_broadcast([P, NT, D])
    step(v.tensor_reduce(stat[:], x, AX, ALU.add))
    step(v.tensor_scalar(stat[:], stat[:], 1.0 / D, None, ALU.mult))
    step(v.tensor_tensor(centred[:], x, wide(), ALU.subtract))
    step(v.tensor_tensor(squares[:], centred[:], centred[:], ALU.mult))
    step(v.tensor_reduce(stat[:], squares[:], AX, ALU.add))
    step(v.tensor_scalar(stat[:], stat[:], 1.0 / D, EPS, ALU.mult, ALU.add))
    root()
    step(v.reciprocal(stat[:], stat[:]))
    step(v.tensor_tensor(centred[:], centred[:], wide(), ALU.mult))
    step(v.tensor_scalar(out, centred[:], 0.0, None, ALU.max))


def attention_pass(nc, name, k, record, width, near, table, near_table, near_width, far_row, running, front):
    L = U * P
    far_end = DST if near == SRC else SRC
    with ExitStack() as ctx:
        at = Stage(nc, ctx, name)
        w = Parts()
        w.at, w.nc, w.k = at, nc, k
        w.rec = at.sb2("rec", [P, U, width], I32)
        w.wide_rows = at.sb2("wide_rows", [P, U, table.shape[1]])
        w.near_rows = at.sb2("near_rows", [P, U, near_width])
        w.logits = at.sb("logits", [P, U, 4])
        w.logits_wide = at.sb("logits_wide", [P, U, 2, D])
        w.logits_ps, w.values_ps = at.ps("logits_ps", [P, U, P]), at.ps("values_ps", [P, U, P])
        back_ps = at.ps("back_ps", [P, U // 2, P])
        far = at.sb2("far", [P, L])
        top = at.sb2("top", [P, 1 + L])
        fade = at.sb("fade", [P, 2, L])
        scaled = at.sb("scaled", [P, L])
        run = at.sb2("run", [P, L])
        back = at.sb2("back", [P, U, P])
        gate = at.sb("gate", [P, 2])
        w.rec_in, far_in, w.gathered, stored = at.sem2("rec_in"), at.sem2("far_in"), [at.gather_sem(f"gathered{b}") for b in range(2)], at.sem("stored")
        w.rows_used, gated, cleared = at.sem("rows_used"), at.sem("gated"), at.sem("cleared")
        w.logits_made, w.widened = at.sem("logits_made"), at.sem("widened")
        w.rec_used, scaled_done = at.sem("rec_used"), at.sem("scaled_done")
        turned = w.turned = at.sem("turned")
        topped, exponents, factors = at.sem("topped"), at.sem("exponents"), at.sem("factors")
        weighted, scanned, returned, copied, sent = at.sem("weighted"), at.sem("scanned"), at.sem("returned"), at.sem("copied"), at.sem("sent")
        front.buffers(w)
        block = at.block()
        records = record.rearrange("(c p) w -> p c w", p=P)
        runs = running.rearrange("(c p) f -> p c f", p=P)
        far_ap = far_row.rearrange("(o e) -> o e", o=1)

        def each_group(eng, first, body):
            first()
            with eng.Fori(0, G // 2 - 1) as i:
                for b in range(2):
                    body(2 * i + b, b, i, True)
            for b in range(2):
                body(G - 2 + b, b, G // 2 - 1, b == 0)

        @block.sync
        def _(sp):
            def load(g, b):
                sp.dma_start(w.rec[b][:], records[:, bass.ds(g * U, U), :]).then_inc(w.rec_in[b], 16)

            def load_far(g, b):
                sp.dma_start(far[b][:], far_ap[:, bass.ds(g * L, L)].to_broadcast([P, L])).then_inc(far_in[b], 16)

            def first():
                sp.sem_inc(sent, 2)
                for b in range(2):
                    load(b, b)
                    load_far(b, b)

            def body(g, b, i, more):
                if not isinstance(g, int):
                    sp.wait_ge(w.rec_used, done(g))
                    sp.wait_ge(w.gathered[b], 16 * 2 * U * (i + 1))
                    load(g + 2, b)
                    sp.wait_ge(exponents, done(g))
                    load_far(g + 2, b)
                sp.wait_ge(copied, 2 * g + 2 + 1)
                sp.dma_start(runs[:, bass.ds(g * U, U), :], back[b][:]).then_inc(stored, 16)
                sp.wait_ge(stored, 16 * (g + 1))
                sp.sem_inc(sent, 1)

            each_group(sp, first, body)

        @block.gpsimd
        def _(pool):
            nc.gpsimd.memset(gate[:], 0.0).then_inc(gated, 1)
            with pool.Fori(0, G // 2) as i:
                for b in range(2):
                    g = 2 * i + b
                    pool.wait_ge(gated, g + 1)
                    pool.wait_ge(w.rows_used, freed(g))
                    pool.wait_ge(turned, freed(g))
                    pool.wait_ge(w.rec_in[b], 16 * (i + 1))
                    nc.gpsimd.tensor_tensor(gate[:, 0:1], gate[:, 1:2], gate[:, 1:2], ALU.add).then_inc(gated, 1)
                    for u in range(U):
                        nc.gpsimd.indirect_dma_start(out=w.wide_rows[b][:, u, :], out_offset=None, in_=table,
                                                     in_offset=bass.IndirectOffsetOnAxis(ap=w.rec[b][:, u, far_end:far_end + 1], axis=0)).then_inc(w.gathered[b], 16)
                        nc.gpsimd.indirect_dma_start(out=w.near_rows[b][:, u, :], out_offset=None, in_=near_table,
                                                     in_offset=bass.IndirectOffsetOnAxis(ap=w.rec[b][:, u, near:near + 1], axis=0)).then_inc(w.gathered[b], 16)

        @block.tensor
        def _(pe):
            def turn(g, b, i):
                front.pe(w, pe, g, b, i)
                pe.wait_ge(exponents, done(g - 1))
                pe.wait_ge(w.widened, 2 * g + 4)
                for u in range(U):
                    nc.tensor.transpose(w.logits_ps[:, u, :], flat(w.logits_wide[:, u, :, :]), k.ident[:])
                pe.wait_ge(weighted, done(g - 1))
                front.values_ready(w, pe, g, b, i)
                for u in range(U):
                    last = nc.tensor.transpose(w.values_ps[:, u, :], front.values(w, b, u), k.ident[:])
                last.then_inc(turned, 1)

            def first():
                pe.sem_inc(turned, 2)
                pe.sem_inc(returned, 4)
                front.pe_start(w, pe)
                turn(0, 0, 0)

            def body(g, b, i, more):
                if more:
                    turn(g + 1, 1 - b, i + b)
                pe.wait_ge(scanned, done(g))
                for h in range(2):
                    pe.wait_ge(copied, 2 * g + h + 1)
                    for u in range(U // 2):
                        c = h * U // 2 + u
                        last = nc.tensor.transpose(back_ps[:, u, :], run[b][:, c * P:(c + 1) * P], k.ident[:])
                    last.then_inc(returned, 1)

            each_group(pe, first, body)

        @block.vector
        def _(dve):
            def first():
                nc.vector.memset(run[1][:], 0.0).then_inc(cleared, 1)
                nc.vector.memset(top[1][:], FAR).then_inc(cleared, 1)
                for s in (topped, exponents, weighted, scanned, w.logits_made):
                    dve.sem_inc(s, 2)
                dve.wait_ge(cleared, 2)
                front.dve_start(w, dve)
                front.dve(w, dve, 0, 0, 0)

            def body(g, b, i, more):
                if more:
                    front.dve_early(w, dve, g + 1, 1 - b, i + b)
                dve.wait_ge(exponents, done(g - 1))
                nc.vector.tensor_copy(top[b][:, 0:1], top[1 - b][:, L:L + 1]).then_inc(topped, 1)
                dve.wait_ge(topped, 2 * g + 1 + 2)
                dve.wait_ge(far_in[b], 16 * (i + 1))
                dve.wait_ge(turned, done(g))
                nc.vector.tensor_tensor_scan(top[b][:, 1:1 + L], far[b][:], flat(w.logits_ps[:]), top[b][:, 0:1],
                                             ALU.add, ALU.max).then_inc(topped, 1)
                dve.wait_ge(topped, 2 * g + 2 + 2)
                dve.wait_ge(scanned, done(g - 1))
                nc.vector.tensor_tensor(scaled[:], top[b][:, 0:L], far[b][:], ALU.add).then_inc(scaled_done, 1)
                nc.vector.tensor_tensor(fade[:, 1, :], flat(w.logits_ps[:]), top[b][:, 1:1 + L], ALU.subtract).then_inc(scaled_done, 1)
                dve.wait_ge(scaled_done, 2 * g + 2)
                nc.vector.tensor_tensor(fade[:, 0, :], scaled[:], top[b][:, 1:1 + L], ALU.subtract).then_inc(exponents, 1)
                if more:
                    front.dve(w, dve, g + 1, 1 - b, i + b)
                dve.wait_ge(exponents, done(g))
                dve.wait_ge(factors, g + 1)
                nc.vector.tensor_tensor(scaled[:], flat(w.values_ps[:]), fade[:, 1, :], ALU.mult).then_inc(weighted, 1)
                dve.wait_ge(weighted, done(g))
                dve.wait_ge(returned, 2 * g + 2)
                nc.vector.tensor_tensor_scan(run[b][:], fade[:, 0, :], scaled[:], run[1 - b][:, L - 1:L], ALU.mult, ALU.add).then_inc(scanned, 1)

            each_group(dve, first, body)

        @block.scalar
        def _(act):
            def widen(g, b):
                act.wait_ge(turned, done(g - 1))
                act.wait_ge(w.logits_made, done(g))
                H = front.heads
                for s in range(2):
                    nc.scalar.activation(w.logits_wide[:, :, s, :].rearrange("p u (h f) -> p u h f", h=H),
                                         w.logits[:, :, 0:H].unsqueeze(3).to_broadcast([P, U, H, D // H]),
                                         ACT.Identity, bias=front.logit_bias).then_inc(w.widened, 1)

            def first():
                act.sem_inc(copied, 1)
                act.sem_inc(w.widened, 2)
                front.act_start(w, act)
                front.act(w, act, 0, 0, 0)
                widen(0, 0)

            def body(g, b, i, more):
                if more:
                    front.act(w, act, g + 1, 1 - b, i + b)
                act.wait_ge(exponents, done(g))
                nc.scalar.activation(fade[:].rearrange("p a l -> p (a l)"), fade[:].rearrange("p a l -> p (a l)"), ACT.Exp).then_inc(factors, 1)
                if more:
                    widen(g + 1, 1 - b)
                act.wait_ge(sent, freed(g))
                for h in range(2):
                    act.wait_ge(returned, 2 * g + h + 5)
                    nc.scalar.copy(flat(back[b][:, h * U // 2:(h + 1) * U // 2, :]), flat(back_ps[:])).then_inc(copied, 1)

            each_group(act, first, body)


class FilterFront:

    heads, logit_bias = 4, 0.0
    F = 32

    def __init__(self, weights):
        self.c = weights

    def buffers(self, w):
        at = w.at
        self.features_ps = at.ps("features_ps", [P, 2, 2 * P])
        self.filter_ps = at.ps("filter_ps", [P, U, 2, self.F])
        self.packed = at.sb("packed", [P, U, self.F])
        self.features, self.size, self.log = at.sb("features", [P, 2 * P]), at.sb("size", [P, 2 * P]), at.sb("log", [P, 2 * P])
        self.positive, self.soft = at.sb("positive", [P, 2 * P]), at.sb("soft", [P, 2 * P])
        self.keyed, self.queried, self.sums = at.sb("keyed", [P, U, D]), at.sb("queried", [P, U, D]), at.sb("sums", [P, U, 4])
        self.value_rows = at.sb("value_rows", [P, U, 2 * D])
        self.features_turned, self.features_in, self.hidden, self.sized, self.raised, self.logged = (
            at.sem("features_turned"), at.sem("features_in"), at.sem("hidden"), at.sem("sized"), at.sem("raised"), at.sem("logged"))
        self.rectified, self.softened, self.filtered, self.stepped, self.ones_set = (
            at.sem("rectified"), at.sem("softened"), at.sem("filtered"), at.sem("stepped"), at.sem("ones_set"))

    def values(self, w, b, u):
        return self.value_rows[:, u, :]

    def values_ready(self, w, pe, g, b, i):
        pe.wait_ge(w.rows_used, done(g))

    def act_start(self, w, act):
        for s in (w.rec_used, self.features_in, self.sized, self.raised, self.logged):
            act.sem_inc(s, 2)

    def act(self, w, act, g, b, i):
        nc = w.nc
        act.wait_ge(self.features_turned, done(g - 1))
        act.wait_ge(w.rec_in[b], 16 * (i + 1))
        nc.scalar.copy(self.packed[:], w.rec[b][:, :, 2:2 + self.F].bitcast(F32)).then_inc(w.rec_used, 1)
        act.wait_ge(self.hidden, done(g - 1))
        act.wait_ge(self.features_turned, done(g))
        nc.scalar.copy(self.features[:], self.features_ps[:, 0, :]).then_inc(self.features_in, 1)
        act.wait_ge(self.softened, done(g - 1))
        act.wait_ge(self.hidden, done(g))
        nc.scalar.activation(self.size[:], self.features_ps[:, 1, :], ACT.Abs, bias=self.c.hidden_bias[:]).then_inc(self.sized, 1)
        act.wait_ge(self.sized, done(g))
        nc.scalar.activation(self.size[:], self.size[:], ACT.Exp, scale=-1.0).then_inc(self.raised, 1)
        act.wait_ge(self.raised, done(g))
        nc.scalar.activation(self.log[:], self.size[:], ACT.Ln, scale=0.5, bias=self.c.half[:]).then_inc(self.logged, 1)

    def pe_start(self, w, pe):
        for s in (self.features_turned, self.hidden, self.filtered):
            pe.sem_inc(s, 2)

    def pe(self, w, pe, g, b, i):
        nc, k, F = w.nc, w.k, self.F
        pe.wait_ge(self.softened, done(g - 1))
        pe.wait_ge(w.rec_used, done(g))
        for h in range(2):
            last = nc.tensor.transpose(self.features_ps[:, 0, h * P:(h + 1) * P], flat(self.packed[:, 4 * h:4 * h + 4, :]), k.ident[:])
        last.then_inc(self.features_turned, 1)
        pe.wait_ge(self.features_in, done(g))
        nc.tensor.matmul(self.features_ps[:, 1, :], self.c.hidden[:], self.features[:], start=True, stop=True).then_inc(self.hidden, 1)
        pe.wait_ge(w.rows_used, done(g - 1))
        pe.wait_ge(self.softened, done(g))
        for h in range(2):
            out = self.filter_ps[:, 4 * h:4 * h + 4, 0, :]
            nc.tensor.matmul(out, self.soft[:, h * P:(h + 1) * P], self.c.filter[:], start=True, stop=False)
            last = nc.tensor.matmul(out, k.ones[0:1, :], self.c.filter_bias[:], start=False, stop=True)
        last.then_inc(self.filtered, 1)

    def dve_start(self, w, dve):
        for s in (w.rows_used, self.rectified, self.softened):
            dve.sem_inc(s, 2)
        w.nc.vector.memset(self.value_rows[:], 1.0).then_inc(self.ones_set, 1)
        dve.wait_ge(self.ones_set, 1)
        self.dve_early(w, dve, 0, 0, 0)

    def dve_early(self, w, dve, g, b, i):
        nc = w.nc
        dve.wait_ge(self.softened, done(g - 1))
        dve.wait_ge(self.sized, done(g))
        nc.vector.tensor_scalar(self.positive[:], self.features_ps[:, 1, :], self.c.hidden_bias[:], 0.0, ALU.add, ALU.max).then_inc(self.rectified, 1)
        dve.wait_ge(self.rectified, done(g))
        dve.wait_ge(self.filtered, done(g - 1))
        dve.wait_ge(self.logged, done(g))
        nc.vector.tensor_tensor(self.soft[:], self.positive[:], self.log[:], ALU.add).then_inc(self.softened, 1)

    def dve(self, w, dve, g, b, i):
        nc, H = w.nc, self.heads
        heads = lambda ap: ap.rearrange("p u (h f) -> p u h f", h=H)
        filters = lambda at: self.filter_ps[:, :, 0, at:at + D // H].unsqueeze(2).to_broadcast([P, U, H, D // H])
        dve.wait_ge(w.gathered[b], 16 * 2 * U * (i + 1))
        dve.wait_ge(self.filtered, done(g))
        dve.wait_ge(w.logits_made, done(g - 1))
        nc.vector.tensor_tensor(heads(self.keyed[:]), heads(w.wide_rows[b][:, :, 0:D]), filters(0), ALU.mult).then_inc(self.stepped, 1)
        dve.wait_ge(self.stepped, 3 * g + 1)
        nc.vector.tensor_tensor(self.queried[:], self.keyed[:], w.near_rows[b][:, :, 0:D], ALU.mult).then_inc(self.stepped, 1)
        dve.wait_ge(self.stepped, 3 * g + 2)
        nc.vector.tensor_reduce(self.sums[:], heads(self.queried[:]), AX, ALU.add).then_inc(self.stepped, 1)
        dve.wait_ge(self.stepped, 3 * g + 3)
        dve.wait_ge(w.widened, 2 * g + 2)
        nc.vector.tensor_tensor(w.logits[:], self.sums[:], w.near_rows[b][:, :, D:D + H], ALU.add).then_inc(w.logits_made, 1)
        dve.wait_ge(w.turned, done(g - 1))
        nc.vector.tensor_tensor(heads(self.value_rows[:, :, 0:D]), heads(w.wide_rows[b][:, :, D:2 * D]), filters(D // H), ALU.mult).then_inc(w.rows_used, 1)


class MixFront:

    heads = 2
    F = 2

    def __init__(self, weights):
        self.c = weights
        self.logit_bias = weights.out_bias[:]

    def buffers(self, w):
        at = w.at
        self.features = at.sb("features", [P, U, self.F])
        self.turned_features = at.sb("turned_features", [U * self.F, P])
        self.edge = at.sb("edge", [P, U // 2, P])
        self.with_keys, self.mixed_rows, self.hidden = at.sb("with_keys", [P, U, D]), at.sb("mixed_rows", [P, U, D]), at.sb("hidden", [P, U, D])
        self.features_ps = at.ps("features_ps", [P, 4 * P])
        self.edge_ps = at.ps("edge_ps", [P, U // 2, P])
        self.mix_ps = at.ps("mix_ps", [P, 2, U // 2, D])
        self.features_turned, self.features_in, self.edged, self.rectified = (
            at.sem("features_turned"), at.sem("features_in"), at.sem("edged"), at.sem("rectified"))
        self.mixed, self.mix_read, self.stepped = at.sem("mixed"), at.sem("mix_read"), at.sem("stepped")

    def values(self, w, b, u):
        return w.wide_rows[b][:, u, D:3 * D]

    def values_ready(self, w, pe, g, b, i):
        pe.wait_ge(w.gathered[b], 16 * 2 * U * (i + 1))

    def act_start(self, w, act):
        for s in (w.rec_used, self.features_in, self.rectified):
            act.sem_inc(s, 2)

    def act(self, w, act, g, b, i):
        nc = w.nc
        act.wait_ge(self.features_turned, done(g - 1))
        act.wait_ge(w.rec_in[b], 16 * (i + 1))
        nc.scalar.copy(self.features[:], w.rec[b][:, :, 2:4].bitcast(F32)).then_inc(w.rec_used, 1)
        act.wait_ge(self.edged, done(g - 1))
        act.wait_ge(self.features_turned, done(g))
        nc.scalar.copy(self.turned_features[:], self.features_ps[0:U * self.F, 0:P]).then_inc(self.features_in, 1)
        act.wait_ge(self.mixed, done(g - 1))
        act.wait_ge(self.edged, done(g))
        nc.scalar.activation(flat(self.edge[:]), flat(self.edge_ps[:]), ACT.Relu, bias=self.c.edge_bias[:]).then_inc(self.rectified, 1)

    def pe_start(self, w, pe):
        for s in (self.features_turned, self.edged, self.mixed):
            pe.sem_inc(s, 2)

    def pe(self, w, pe, g, b, i):
        nc, k = w.nc, w.k
        pe.wait_ge(self.features_in, done(g - 1))
        pe.wait_ge(w.rec_used, done(g))
        nc.tensor.transpose(self.features_ps[0:U * self.F, 0:P], flat(self.features[:]), k.ident[:]).then_inc(self.features_turned, 1)
        pe.wait_ge(self.rectified, done(g - 1))
        pe.wait_ge(self.features_in, done(g))
        for u in range(U // 2):
            last = nc.tensor.matmul(self.edge_ps[:, u, :], self.c.edge[:, u, :], self.turned_features[:], start=True, stop=True)
        last.then_inc(self.edged, 1)
        pe.wait_ge(self.mix_read, done(g - 1))
        pe.wait_ge(self.rectified, done(g))
        for u in range(U // 2):
            last = nc.tensor.matmul(self.mix_ps[:, :, u, :], self.edge[:, u, :], self.c.mix[:], start=True, stop=True)
        last.then_inc(self.mixed, 1)

    def dve_start(self, w, dve):
        for s in (w.rows_used, self.mix_read):
            dve.sem_inc(s, 2)

    def dve_early(self, w, dve, g, b, i):
        pass

    def dve(self, w, dve, g, b, i):
        nc, H = w.nc, self.heads
        dve.wait_ge(w.gathered[b], 16 * 2 * U * (i + 1))
        dve.wait_ge(self.mixed, done(g))
        dve.wait_ge(w.logits_made, done(g - 1))
        nc.vector.tensor_tensor(self.with_keys[:], self.mix_ps[:].rearrange("p a u f -> p (a u) f"), w.wide_rows[b][:, :, 0:D], ALU.add).then_inc(self.mix_read, 1)
        dve.wait_ge(self.mix_read, done(g))
        nc.vector.tensor_tensor(self.mixed_rows[:], self.with_keys[:], w.near_rows[b][:, :, 0:D], ALU.add).then_inc(w.rows_used, 1)
        dve.wait_ge(w.rows_used, done(g))
        nc.vector.scalar_tensor_tensor(self.hidden[:], self.mixed_rows[:], 0.0, self.c.out[:].unsqueeze(1).to_broadcast([P, U, D]), ALU.max, ALU.mult).then_inc(self.stepped, 1)
        dve.wait_ge(self.stepped, g + 1)
        dve.wait_ge(w.widened, 2 * g + 2)
        nc.vector.tensor_reduce(w.logits[:, :, 0:H], self.hidden[:].rearrange("p u (h f) -> p u h f", h=H), AX, ALU.add).then_inc(w.logits_made, 1)


def make_weight_buffers(sb):
    c, c_filter, c_mix = Parts(), Parts(), Parts()
    c.sage1 = sb("sage1", [P, P])
    c.sage1_bias = sb("sage1_bias", [P, P])
    c.sage2 = sb("sage2", [P, P])
    c.sage2_bias = sb("sage2_bias", [P, P])
    c.tables1 = sb("tables1", [P, 196])
    c.tables1_bias = sb("tables1_bias", [P, 196])
    c.value1 = sb("value1", [P, D])
    c.value1_bias = sb("value1_bias", [P, D])
    c.value_bias1 = sb("value_bias1", [P, D])
    c.out1 = sb("out1", [P, D])
    c.out1_bias = sb("out1_bias", [P, D])
    c.gcn = sb("gcn", [P, D])
    c.gcn_bias = sb("gcn_bias", [P, D])
    c.kqv = sb("kqv", [P, 3 * D])
    c.kqv_bias = sb("kqv_bias", [P, 3 * D])
    c.mix3 = sb("mix3", [P, P])
    c.mix3_bias = sb("mix3_bias", [P, P])
    c.out3 = sb("out3", [P, D])
    c.edge_count_bias = sb("edge_count_bias", [P, D])
    c.gamma = sb("gamma", [P, D])
    c.beta = sb("beta", [P, D])
    c_filter.hidden = sb("hidden_w", [P, P])
    c_filter.hidden_bias = sb("hidden_b", [P, 1])
    c_filter.filter = sb("filter_w", [P, P])
    c_filter.filter_bias = sb("filter_b", [1, P])
    c_filter.half = sb("half", [P, 1])
    c_mix.edge = sb("edge_w", [2 * U, U // 2, P])
    c_mix.edge_bias = sb("edge_b", [P, 1])
    c_mix.mix = sb("mix_w", [P, P])
    c_mix.out = sb("mix_out", [P, D])
    c_mix.out_bias = sb("mix_out_b", [P, 1])
    c.filter, c.mix = c_filter, c_mix
    return c


def load_weights(nc, name, k, a):
    c = k.weights
    with ExitStack() as ctx:
        at = Stage(nc, ctx, name)
        more1, more2 = at.sb("more1", [P, 2 * D]), at.sb("more2", [P, D])
        more_bias1, more_bias2 = at.sb("more_bias1", [P, 2 * D]), at.sb("more_bias2", [P, D])
        query, key = at.sb("query", [D, 2 * D]), at.sb("key", [D, D + 4])
        query_ps = at.ps("query_ps", [P, 512])
        cleared, loaded, stepped, multiplied = at.sem("cleared"), at.sem("loaded"), at.sem("stepped"), at.sem("multiplied")
        block = at.block()
        zeroed = [c.sage2_bias, c.tables1, c.tables1_bias, c.value1, c.out1, c.gcn, c.kqv, c.mix3, c.mix3_bias, c.out3,
                  c.filter.hidden, c.filter.filter, c.mix.edge, c.mix.mix, query, key]
        row = lambda v: v.rearrange("(o f) -> o f", o=1)
        every = lambda v: row(v).to_broadcast([P, v.shape[0]])
        column = lambda v: v.rearrange("(f o) -> f o", o=1)
        moves = [
            (c.sage1[0:D, :], a["W1n"]), (c.sage1[D:P, :], a["W1r"]), (more1[D:P, :], a["Wl1"]),
            (c.sage1_bias[:], every(a["b1n"])), (more_bias1[:], every(a["bl1"])),
            (c.sage2[:, 0:D], a["W2n"]), (c.sage2[:, D:P], a["W2r"]), (more2[:], a["Wl2"]),
            (c.sage2_bias[:, D:P], every(a["b2n"])), (more_bias2[:], every(a["bl2"])),
            (c.value1[D:P, :], a["cen_wT"]), (c.value1_bias[:], every(a["cen_b"])),
            (c.out1[0:D, :], a["out_wT"]), (c.out1_bias[:], every(a["out_b"])),
            (c.gcn[0:D, :], a["gcn_w"]), (c.gcn_bias[:], every(a["gcn_b"])),
            (c.kqv[D:P, :], a["W_kqv"]), (c.kqv_bias[:], every(a["b_kqv"])),
            (c.out3[0:D, :], a["W_out"]), (c.edge_count_bias[:], every(a["b_out"])),
            (c.gamma[:], every(a["gamma"])), (c.beta[:], every(a["beta"])),
            (c.mix.out_bias[:], every(a["b_att2"])),
        ]
        for h in range(4):
            s = slice(16 * h, 16 * (h + 1))
            under = slice(D + 16 * h, D + 16 * (h + 1))
            moves += [(c.tables1[under, s], a["k_wT"][h]), (c.tables1[under, under], a["v_wT"][h]),
                      (query[s, under], a["q_w"][h]), (key[s, s], a["wkl_w"]), (key[s, D + h:D + h + 1], column(a["wkl_b"])),
                      (c.value1[s, s], a["wvl_wT"]), (c.value_bias1[:, s], every(a["wvl_b"]))]
        for u in range(4):
            lo, hi = slice(32 * u, 32 * u + 16), slice(32 * u + 16, 32 * u + 32)
            both = slice(32 * u, 32 * u + 32)
            moves += [(c.filter.hidden[both, lo], a["wkn_w1T"]), (c.filter.hidden[both, hi], a["wvn_w1T"]),
                      (c.filter.hidden_bias[lo, :], column(a["wkn_b1"])), (c.filter.hidden_bias[hi, :], column(a["wvn_b1"])),
                      (c.filter.filter[lo, lo], a["wkn_w2T"]), (c.filter.filter[hi, hi], a["wvn_w2T"]),
                      (c.filter.filter_bias[:, lo], row(a["wkn_b2"])), (c.filter.filter_bias[:, hi], row(a["wvn_b2"]))]
            for half in range(2):
                chunk = u + 4 * half
                moves.append((c.mix.edge[2 * chunk:2 * chunk + 2, u, half * D:(half + 1) * D], a["W_edge"]))
        for h in range(2):
            s = slice(32 * h, 32 * (h + 1))
            under = slice(D + 32 * h, D + 32 * (h + 1))
            moves += [(c.mix3[s, under], a["W_att1"][32:64, :]), (c.mix3[under, s], a["W_att1"][0:32, :]),
                      (c.mix3_bias[:, under], every(a["b_att1"])), (c.mix.out[:, s], every(a["w_att2"])),
                      (c.mix.mix[s, s], a["W_att1"][64:96, :]), (c.mix.mix[under, under], a["W_att1"][64:96, :]),
                      (c.mix.edge_bias[h * D:(h + 1) * D, :], column(a["b_edge"]))]

        @block.sync
        def _(sp):
            sp.wait_ge(cleared, len(zeroed))
            with nc.allow_non_contiguous_dma(reason="small biases turned into columns"):
                for out, in_ in moves:
                    sp.dma_start(out, in_).then_inc(loaded, 16)

        @block.tensor
        def _(pe):
            pe.wait_ge(loaded, 16 * len(moves))
            nc.tensor.matmul(query_ps[:, 0:D + 4], query[:], key[:], start=True, stop=True).then_inc(multiplied, 1)

        @block.vector
        def _(dve):
            for z in zeroed:
                nc.vector.memset(z[:], 0.0).then_inc(cleared, 1)
            nc.vector.memset(c.filter.half[:], 0.5)
            step = Steps(dve, stepped)
            dve.wait_ge(loaded, 16 * len(moves))
            step(nc.vector.tensor_tensor(c.sage1[D:P, :], c.sage1[D:P, :], more1[D:P, :], ALU.add))
            step(nc.vector.tensor_tensor(c.sage2[:, D:P], c.sage2[:, D:P], more2[:], ALU.add))
            step(nc.vector.tensor_tensor(c.sage1_bias[:], c.sage1_bias[:], more_bias1[:], ALU.add))
            step(nc.vector.tensor_tensor(c.sage2_bias[:, D:P], c.sage2_bias[:, D:P], more_bias2[:], ALU.add))
            step(nc.vector.tensor_scalar(c.mix3[D:P, :], c.mix3[D:P, :], 32.0 ** -0.5, None, ALU.mult))
            dve.wait_ge(multiplied, 1)
            step(nc.vector.tensor_copy(c.tables1[:, P:P + D + 4], query_ps[:, 0:D + 4]))


def node_stage(nc, name, k, program, stores=(), roots=0):
    with ExitStack() as ctx:
        at = Stage(nc, ctx, name)
        centred, squares, stat = at.sb("centred", [P, NT, D]), at.sb("squares", [P, NT, D]), at.sb("stat", [P, NT])
        stepped, stored, finished = at.sem("stepped"), at.sem("stored"), at.sem("finished")
        squared, rooted = at.sem("squared"), at.sem("rooted")
        block = at.block()

        @block.vector
        def _(dve):
            step = Steps(dve, stepped)
            given = [0]

            def root():
                given[0] += 1
                dve.sem_inc(squared, 1)
                dve.wait_ge(rooted, given[0])

            norm = lambda x, out: layer_norm(nc, step, root, x, out, centred, squares, stat)
            o = Parts()
            o.v, o.step, o.root, o.norm, o.tmp, o.stat = nc.vector, step, root, norm, centred, stat
            program(o)
            dve.sem_inc(finished, 1)

        @block.scalar
        def _(act):
            for r in range(roots):
                act.wait_ge(squared, r + 1)
                nc.scalar.sqrt(stat[:], stat[:]).then_inc(rooted, 1)

        @block.sync
        def _(sp):
            sp.wait_ge(finished, 1)
            for out, in_ in stores:
                sp.dma_start(out, in_).then_inc(stored, 16)
            if stores:
                sp.wait_ge(stored, 16 * len(stores))


def shifted_softplus(nc, name, k, x, out):
    with ExitStack() as ctx:
        at = Stage(nc, ctx, name)
        size = at.sb("size", [P, NT, D])
        sized, logged, stepped = at.sem("sized"), at.sem("logged"), at.sem("stepped")
        block = at.block()

        @block.scalar
        def _(act):
            step = Steps(act, sized)
            step(nc.scalar.activation(size[:], x, ACT.Abs))
            step(nc.scalar.activation(size[:], size[:], ACT.Exp, scale=-1.0))
            nc.scalar.activation(size[:], size[:], ACT.Ln, scale=0.5, bias=k.weights.filter.half[:]).then_inc(logged, 1)

        @block.vector
        def _(dve):
            dve.wait_ge(logged, 1)
            nc.vector.scalar_tensor_tensor(out, x, 0.0, size[:], ALU.max, ALU.add).then_inc(stepped, 1)


def build(nc, a, out):
    dram = lambda name, shape, dt=F32: nc.dram_tensor(name, shape, dt, kind="Internal").ap()
    by_tile = lambda table: table.rearrange("(t p) f -> p t f", p=P)
    with ExitStack() as ctx:
        sb = Stage(nc, ctx, "all").sb
        count, before, upto, ident, ones = (sb(n, [P, P]) for n in ("count", "before", "upto", "ident", "ones"))
        k = Parts()
        k.count, k.before, k.upto, k.ident, k.ones = count, before, upto, ident, ones
        k.before16, k.ones16 = sb("before16", [P, P], BF16), sb("ones16", [P, P], BF16)
        k.weights = make_weight_buffers(sb)
        c = k.weights
        make_constants(nc, "constants", k)
        load_weights(nc, "weights", k, a)

        record2, record32 = dram("record2", (EP, 4), I32), dram("record32", (EP, 34), I32)
        middle2, middle32 = dram("middle2", (EP, 4), I32), dram("middle32", (EP, 34), I32)
        by_dst, by_src = dram("by_dst", (EP, 4), I32), dram("by_src", (EP, 34), I32)
        rows = [Parts(), Parts()]
        for r, n in zip(rows, ("dst", "src")):
            r.keep, r.far = dram(f"keep_{n}", (EP,)), dram(f"far_{n}", (EP,))
            r.count, r.some, r.crosses = sb(f"count_{n}", [P, NT]), sb(f"some_{n}", [P, NT]), sb(f"crosses_{n}", [P, NT])
            r.last = sb(f"last_{n}", [P, NT], I32)
        into, outof = rows
        make_records(nc, "records2", a["src"], a["dst"], a["edge_attr_2"], 4, record2)
        make_records(nc, "records32", a["src"], a["dst"], a["edge_attr_32"], 34, record32)
        sort_records(nc, "sort_dst", k, record2, DST, 4, middle2, by_dst, into.count)
        sort_records(nc, "sort_src", k, record32, SRC, 34, middle32, by_src, outof.count)
        mark_segments(nc, "mark_dst", k, by_dst, DST, into.count, into.last, into.some, into.crosses, into.keep, into.far)
        mark_segments(nc, "mark_src", k, by_src, SRC, outof.count, outof.last, outof.some, outof.crosses, outof.keep, outof.far)

        x, wide, tall = sb("x", [P, NT, D]), sb("wide", [P, NT, P]), sb("tall", [P, NT, 196])
        scale = sb("scale", [P, NT])
        summed, own = wide[:, :, 0:D], wide[:, :, D:P]
        over = lambda col: col[:].unsqueeze(2).to_broadcast([P, NT, D])
        each = lambda bias: bias[:].unsqueeze(1).to_broadcast([P, NT, D])
        table = dram("table", (NP, D))
        running, weighted = dram("running", (EP, D)), dram("weighted", (EP, P))
        with ExitStack() as first:
            at = Stage(nc, first, "load_x")
            loaded, cleared = at.sem("loaded"), at.sem("cleared")
            block = at.block()
            whole = N // P

            @block.vector
            def _(dve):
                nc.vector.memset(x[:, whole:NT, :], 0.0).then_inc(cleared, 1)

            @block.sync
            def _(sp):
                sp.dma_start(x[:, 0:whole, :], by_tile(a["x"][0:whole * P, :])).then_inc(loaded, 16)
                sp.wait_ge(cleared, 1)
                sp.dma_start(x[0:N - whole * P, whole, :], a["x"][whole * P:N, :]).then_inc(loaded, 16)
                sp.wait_ge(loaded, 32)

        def start0(o):
            v, step, tmp = o.v, o.step, o.tmp
            o.norm(x[:], own)
            step(v.tensor_scalar(scale[:], into.count[:], 1.0, None, ALU.max))
            step(v.reciprocal(scale[:], scale[:]))
        node_stage(nc, "start0", k, start0, [(by_tile(table), own)], roots=1)
        sum_over_edges(nc, "sage1_sum", k, by_dst, SRC, table, into.keep, running)
        node_sums(nc, "sage1_mean", running, into.last, into.some, into.crosses, scale, summed)
        linear(nc, "sage1", k, wide, c.sage1, P, c.sage1_bias, tall)

        def hidden0(o):
            v, step, tmp = o.v, o.step, o.tmp
            step(v.tensor_scalar(wide[:], tall[:, :, 0:P], 0.0, None, ALU.max))
        node_stage(nc, "hidden0", k, hidden0)
        linear(nc, "sage2", k, wide, c.sage2, P, c.sage2_bias, tall)

        def own0(o):
            v, step, tmp = o.v, o.step, o.tmp
            step(v.tensor_tensor(x[:], x[:], tall[:, :, D:P], ALU.add))
        node_stage(nc, "own0", k, own0, [(by_tile(table), tall[:, :, 0:D])])
        sum_over_edges(nc, "sage2_sum", k, by_dst, SRC, table, into.keep, running)
        node_sums(nc, "sage2_mean", running, into.last, into.some, into.crosses, scale, summed)

        def start1(o):
            v, step, tmp = o.v, o.step, o.tmp
            step(v.tensor_tensor(x[:], x[:], summed, ALU.add))
            o.norm(x[:], own)
        node_stage(nc, "start1", k, start1, roots=1)
        linear(nc, "tables1", k, wide, c.tables1, 196, c.tables1_bias, tall)
        keys_values, queries = dram("keys_values", (NP, P)), dram("queries", (NP, D + 4))
        node_stage(nc, "store1", k, lambda o: None, [(by_tile(keys_values), tall[:, :, 0:P]), (by_tile(queries), tall[:, :, P:P + D + 4])])
        attention_pass(nc, "attend1", k, by_src, 34, SRC, keys_values, queries, D + 4, outof.far, weighted, FilterFront(c.filter))
        node_averages(nc, "average1", weighted, outof.last, outof.some, summed)
        linear(nc, "value1", k, wide, c.value1, D, c.value1_bias, tall)

        def value1(o):
            v, step, tmp = o.v, o.step, o.tmp
            step(v.tensor_tensor(tmp[:], over(outof.some), each(c.value_bias1), ALU.mult))
            step(v.tensor_tensor(tmp[:], tmp[:], tall[:, :, 0:D], ALU.add))
            step(v.tensor_copy(own, tmp[:]))
        node_stage(nc, "biased1", k, value1)
        shifted_softplus(nc, "soft1", k, own, summed)
        linear(nc, "out1", k, wide, c.out1, D, c.out1_bias, tall)

        def start2(o):
            v, step, tmp = o.v, o.step, o.tmp
            step(v.tensor_tensor(x[:], x[:], tall[:, :, 0:D], ALU.add))
            o.norm(x[:], own)
            step(v.tensor_scalar(o.stat[:], outof.count[:], 1.0, None, ALU.max))
            o.root()
            step(v.reciprocal(o.stat[:], o.stat[:]))
            step(v.tensor_tensor(scale[:], o.stat[:], outof.some[:], ALU.mult))
            step(v.tensor_tensor(tmp[:], own, over(scale), ALU.mult))
            step(v.tensor_copy(own, tmp[:]))
        node_stage(nc, "start2", k, start2, [(by_tile(table), own)], roots=2)
        sum_over_edges(nc, "gcn_sum", k, by_src, DST, table, outof.keep, running)
        node_sums(nc, "gcn_scale", running, outof.last, outof.some, outof.crosses, scale, summed)
        linear(nc, "gcn", k, wide, c.gcn, D, c.gcn_bias, tall)

        def start3(o):
            v, step, tmp = o.v, o.step, o.tmp
            step(v.scalar_tensor_tensor(x[:], tall[:, :, 0:D], 0.0, x[:], ALU.max, ALU.add))
            o.norm(x[:], own)
        node_stage(nc, "start3", k, start3, roots=1)
        linear(nc, "kqv", k, wide, c.kqv, 3 * D, c.kqv_bias, tall)
        mixed, mix_values, mix_queries = sb("mixed", [P, NT, P]), dram("mix_values", (NP, 3 * D)), dram("mix_queries", (NP, D))
        linear(nc, "mix3", k, tall[:, :, 0:P], c.mix3, P, c.mix3_bias, mixed)

        def pack3(o):
            v, step, tmp = o.v, o.step, o.tmp
            step(v.tensor_copy(tall[:, :, 0:D], mixed[:, :, 0:D]))
            step(v.tensor_copy(tmp[:], tall[:, :, P:P + D]))
            step(v.memset(tall[:, :, P:P + D], 1.0))
            step(v.tensor_copy(tall[:, :, D:P], tmp[:]))
        node_stage(nc, "pack3", k, pack3, [(by_tile(mix_values), tall[:, :, 0:3 * D]), (by_tile(mix_queries), mixed[:, :, D:P])])
        attention_pass(nc, "attend3", k, by_dst, 4, DST, mix_values, mix_queries, D, into.far, weighted, MixFront(c.mix))
        node_averages(nc, "average3", weighted, into.last, into.some, summed)

        linear(nc, "out3", k, wide, c.out3, D, c.tables1_bias, tall)

        def finish3(o):
            v, step, tmp = o.v, o.step, o.tmp
            step(v.tensor_tensor(tmp[:], over(into.count), each(c.edge_count_bias), ALU.mult))
            step(v.tensor_tensor(tmp[:], tmp[:], tall[:, :, 0:D], ALU.add))
            step(v.tensor_tensor(tmp[:], tmp[:], own, ALU.add))
            step(v.tensor_scalar(tmp[:], tmp[:], (1.0 + EPS) ** -0.5, None, ALU.mult))
            step(v.tensor_tensor(tmp[:], tmp[:], each(c.gamma), ALU.mult))
            step(v.tensor_tensor(tmp[:], tmp[:], each(c.beta), ALU.add))
            step(v.tensor_tensor(x[:], x[:], tmp[:], ALU.add))
        whole = N // P
        node_stage(nc, "finish3", k, finish3, [(by_tile(out[0:whole * P, :]), x[:, 0:whole, :]), (out[whole * P:N, :], x[0:N - whole * P, whole, :])])


_NAMES = {
    "x": "x", "src": "src", "dst": "dst", "edge_attr_2": "edge_attr_2", "edge_attr_32": "edge_attr_32",
    "W1n": "L0_gnn_W1n", "b1n": "L0_gnn_b1n", "W1r": "L0_gnn_W1r", "Wl1": "L0_gnn_Wl1", "bl1": "L0_gnn_bl1",
    "W2n": "L0_gnn_W2n", "b2n": "L0_gnn_b2n", "W2r": "L0_gnn_W2r", "Wl2": "L0_gnn_Wl2", "bl2": "L0_gnn_bl2",
    "k_wT": "L1_gnn_k_w", "q_w": "L1_gnn_q_w", "v_wT": "L1_gnn_v_w",
    "wkn_w1T": "L1_gnn_wkn_w1", "wkn_b1": "L1_gnn_wkn_b1", "wkn_w2T": "L1_gnn_wkn_w2", "wkn_b2": "L1_gnn_wkn_b2",
    "wkl_w": "L1_gnn_wkl_w", "wkl_b": "L1_gnn_wkl_b",
    "wvn_w1T": "L1_gnn_wvn_w1", "wvn_b1": "L1_gnn_wvn_b1", "wvn_w2T": "L1_gnn_wvn_w2", "wvn_b2": "L1_gnn_wvn_b2",
    "wvl_wT": "L1_gnn_wvl_w", "wvl_b": "L1_gnn_wvl_b",
    "cen_wT": "L1_gnn_cen_w", "cen_b": "L1_gnn_cen_b", "out_wT": "L1_gnn_out_w", "out_b": "L1_gnn_out_b",
    "gcn_w": "L2_gnn_weight", "gcn_b": "L2_gnn_bias",
    "W_kqv": "L3_gnn_W_kqv", "b_kqv": "L3_gnn_b_kqv", "W_edge": "L3_gnn_W_edge", "b_edge": "L3_gnn_b_edge",
    "W_att1": "L3_gnn_W_att1", "b_att1": "L3_gnn_b_att1", "w_att2": "L3_gnn_W_att2", "b_att2": "L3_gnn_b_att2",
    "W_out": "L3_gnn_W_out", "b_out": "L3_gnn_b_out", "gamma": "L3_gnn_bn_gamma", "beta": "L3_gnn_bn_beta",
}


def kernel(**inputs):
    import numpy as np
    import concourse.bacc as bacc
    from concourse.bass_utils import run_bass_kernel_spmd

    nc = bacc.Bacc("TRN2", target_bir_lowering=False, num_devices=1)
    arrays, args = {}, {}
    for short, name in _NAMES.items():
        v = np.asarray(inputs[name])
        if short.endswith("T"):
            v = np.swapaxes(v, -1, -2)
        if short == "w_att2":
            v = v.reshape(-1)
        v = np.ascontiguousarray(v)
        arrays[f"in_{short}"] = v
        args[short] = nc.dram_tensor(f"in_{short}", v.shape, mybir.dt.from_np(v.dtype), kind="ExternalInput").ap()
    out = nc.dram_tensor("out_x", (N, D), F32, kind="ExternalOutput").ap()
    build(nc, args, out)
    return run_bass_kernel_spmd(nc, [arrays], core_ids=[0]).results[0]["out_x"]
```

```python
from contextlib import ExitStack

import concourse.bass as bass
from concourse import mybir

ALU = mybir.AluOpType
ACT = mybir.ActivationFunctionType
F32 = mybir.dt.float32
BF16 = mybir.dt.bfloat16
I32 = mybir.dt.int32
AX = mybir.AxisListType.X

P = 128
N, E = 3125, 53125
NT = -(-N // P)
NP = NT * P
CH = 416
EP = CH * P
HALF = EP // 2
PAD = NP - 1
D = 64
U = 8
G = CH // U
FAR = -1.0e30
LN2 = 0.6931471805599453
EPS = 1e-5

SRC, DST = 0, 1


def done(k):
    return k + 3


def freed(k):
    return k + 1


def flat(ap):
    return ap.rearrange("p a b -> p (a b)")


class Parts:
    pass


class Stage:

    def __init__(self, nc, ctx, name):
        self.nc, self.ctx, self.name, self.sems = nc, ctx, name, []

    def sb(self, name, shape, dt=F32):
        return self.ctx.enter_context(self.nc.sbuf_tensor(f"{self.name}_{name}", shape, dt))

    def ps(self, name, shape, dt=F32):
        return self.ctx.enter_context(self.nc.psum_tensor(f"{self.name}_{name}", shape, dt))

    def sem(self, name):
        self.sems.append(self.ctx.enter_context(self.nc.semaphore(f"{self.name}_{name}")))
        return self.sems[-1]

    def gather_sem(self, name):
        return self.nc.alloc_semaphore(f"{self.name}_{name}")

    def sb2(self, name, shape, dt=F32):
        return [self.sb(f"{name}{b}", shape, dt) for b in range(2)]

    def ps2(self, name, shape, dt=F32):
        return [self.ps(f"{name}{b}", shape, dt) for b in range(2)]

    def sem2(self, name):
        return [self.sem(f"{name}{b}") for b in range(2)]

    def block(self):
        self.ctx.callback(self.clear)
        return self.ctx.enter_context(self.nc.Block())

    def clear(self):
        for s in self.sems:
            self.nc.gpsimd.sem_clear(s)
        self.nc.all_engine_barrier()


class Steps:

    def __init__(self, eng, sem, at=0):
        self.eng, self.sem, self.n = eng, sem, at

    def __call__(self, ins):
        self.n += 1
        ins.then_inc(self.sem, 1)
        self.eng.wait_ge(self.sem, self.n)


def each_group(eng, body):
    with eng.Fori(0, G // 2 - 1) as i:
        for b in range(2):
            body(2 * i + b, b, i, True)
    for b in range(2):
        body(G - 2 + b, b, G // 2 - 1, b == 0)


def make_constants(nc, name, k):
    with ExitStack() as ctx:
        at = Stage(nc, ctx, name)
        col_i = at.sb("col_i", [P, P], I32)
        row_i = at.sb("row_i", [P, P], I32)
        row_f = at.sb("row_f", [P, P])
        iotas = at.sem("iotas")
        made = at.sem("made")
        block = at.block()

        @block.gpsimd
        def _(pool):
            nc.gpsimd.iota(col_i[:], pattern=[[1, P]], base=0, channel_multiplier=0).then_inc(iotas, 1)
            nc.gpsimd.iota(row_i[:], pattern=[[0, P]], base=0, channel_multiplier=1).then_inc(iotas, 1)

        @block.vector
        def _(dve):
            step = Steps(dve, made)
            dve.wait_ge(iotas, 2)
            step(nc.vector.tensor_copy(k.count[:], col_i[:]))
            step(nc.vector.tensor_copy(row_f[:], row_i[:]))
            step(nc.vector.tensor_tensor(k.before[:], row_f[:], k.count[:], ALU.is_lt))
            step(nc.vector.tensor_tensor(k.upto[:], row_f[:], k.count[:], ALU.is_le))
            step(nc.vector.tensor_tensor(k.ident[:], row_f[:], k.count[:], ALU.is_equal))
            step(nc.vector.memset(k.ones[:], 1.0))
            step(nc.vector.tensor_copy(k.ones16[:], k.ones[:]))
            step(nc.vector.tensor_copy(k.ident16[:], k.ident[:]))
            step(nc.vector.tensor_copy(k.lanes16[:], k.count[:]))
            step(nc.vector.tensor_scalar(k.tiles16[:], k.count[:, 0:NT], float(P), None, ALU.mult))
            step(nc.vector.tensor_scalar(k.later16[:], k.before[:], -1.0, -2.0 ** 14, ALU.add, ALU.mult))


def load_edges(nc, name, src, dst, attr, column, width, e):
    per, left = E // P, E % P
    assert per + 1 == CH
    with ExitStack() as ctx:
        at = Stage(nc, ctx, name)
        ends = at.sb("ends", [P, 2, CH], I32)
        feat = at.sb("feat", [P, CH, width - 2])
        lane, tile = at.sb("lane", [P, CH], I32), at.sb("tile", [P, CH], I32)
        loaded, padded, packed, split = at.sem("loaded"), at.sem("padded"), at.sem("packed"), at.sem("split")
        block = at.block()
        a = attr.rearrange("e f -> (e f)")
        f = width - 2

        @block.vector
        def _(dve):
            nc.vector.memset(ends[:, :, per:CH], PAD).then_inc(padded, 1)
            nc.vector.memset(feat[:, per:CH, :], 0.0).then_inc(padded, 1)
            dve.wait_ge(loaded, 16 * 6)
            key = ends[:, column, :]
            nc.vector.tensor_scalar(lane[:], key, P - 1, None, ALU.bitwise_and).then_inc(split, 1)
            nc.vector.tensor_scalar(tile[:], key, 7, None, ALU.logical_shift_right).then_inc(split, 1)
            nc.vector.tensor_copy(e.key[:], key)
            for c in (SRC, DST):
                nc.vector.tensor_copy(e.rec[:, :, c], ends[:, c, :])
            dve.wait_ge(split, 2)
            nc.vector.tensor_copy(e.lane16[:], lane[:])
            nc.vector.tensor_scalar(e.tile16[:], tile[:], float(P), None, ALU.mult)

        @block.scalar
        def _(act):
            act.wait_ge(loaded, 16 * 6)
            nc.scalar.copy(e.rec[:, :, 2:width].bitcast(F32), feat[:])

        @block.sync
        def _(sp):
            sp.wait_ge(padded, 2)
            for c, ap in ((SRC, src), (DST, dst)):
                sp.dma_start(ends[:, c, 0:per], ap[0:per * P].rearrange("(p j) -> p j", p=P)).then_inc(loaded, 16)
                sp.dma_start(ends[0:left, c, per:CH], ap[per * P:E].rearrange("(p j) -> p j", j=1)).then_inc(loaded, 16)
            sp.dma_start(feat[:, 0:per, :], a[0:per * P * f].rearrange("(p j f) -> p j f", p=P, f=f)).then_inc(loaded, 16)
            sp.dma_start(feat[0:left, per:CH, :], a[per * P * f:E * f].rearrange("(p j f) -> p j f", p=left, f=f)).then_inc(loaded, 16)


def count_edges(nc, name, k, e, r):
    with ExitStack() as ctx:
        at = Stage(nc, ctx, name)
        lanes, tiles = at.sb2("lanes", [P, U, P], BF16), at.sb2("tiles", [P, U, NT], BF16)
        zeros, tile_upto, ends, starts = at.sb("zeros", [P, NT]), at.sb("tile_upto", [P, NT]), at.sb("node_ends", [P, NT]), at.sb("node_starts", [P, NT])
        count_ps, ends_ps, sums_ps = at.ps("count_ps", [P, 512]), at.ps("ends_ps", [P, 512]), at.ps("sums_ps", [P, 512])
        tiles_hot, hot, counted, summed, stepped = at.sem("tiles_hot"), at.sem("hot"), at.sem("counted"), at.sem("summed"), at.sem("stepped")
        block = at.block()

        @block.vector
        def _(dve):
            step = Steps(dve, stepped)
            step(nc.vector.memset(zeros[:], 0.0))
            dve.sem_inc(hot, 2)
            with dve.Fori(0, G // 2) as i:
                for b in range(2):
                    g = 2 * i + b
                    dve.wait_ge(counted, freed(g))
                    nc.vector.tensor_tensor(tiles[b][:], e.tile16[:, bass.ds(g * U, U)].unsqueeze(2).to_broadcast([P, U, NT]),
                                            k.tiles16[:].unsqueeze(1).to_broadcast([P, U, NT]), ALU.is_equal).then_inc(tiles_hot, 1)
                    nc.vector.tensor_tensor(lanes[b][:], e.lane16[:, bass.ds(g * U, U)].unsqueeze(2).to_broadcast([P, U, P]),
                                            k.lanes16[:].unsqueeze(1).to_broadcast([P, U, P]), ALU.is_equal).then_inc(hot, 1)
            dve.wait_ge(counted, done(G - 1))
            step(nc.vector.tensor_copy(r.count[:], count_ps[:, 0:NT]))
            dve.wait_ge(summed, 2)
            step(nc.vector.tensor_tensor_scan(tile_upto[:], sums_ps[:, 0:NT], zeros[:], 0.0, ALU.add, ALU.add))
            step(nc.vector.tensor_tensor(ends[:], tile_upto[:], sums_ps[:, 0:NT], ALU.subtract))
            step(nc.vector.tensor_tensor(ends[:], ends[:], ends_ps[:, 0:NT], ALU.add))
            step(nc.vector.tensor_tensor(starts[:], ends[:], r.count[:], ALU.subtract))
            step(nc.vector.tensor_copy(r.place[:], starts[:]))
            step(nc.vector.tensor_scalar(r.last[:], ends[:], -1.0, 0.0, ALU.add, ALU.max))
            step(nc.vector.tensor_scalar(r.some[:], r.count[:], 1.0, None, ALU.min))
            step(nc.vector.tensor_scalar(starts[:], starts[:], float(HALF), None, ALU.is_lt))
            step(nc.vector.tensor_scalar(ends[:], ends[:], float(HALF), None, ALU.is_gt))
            step(nc.vector.tensor_tensor(r.crosses[:], starts[:], ends[:], ALU.mult))

        @block.tensor
        def _(pe):
            pe.sem_inc(counted, 2)
            pe.wait_ge(stepped, 1)
            nc.tensor.matmul(count_ps[:, 0:NT], k.ones[:], zeros[:], start=True, stop=True, skip_group_check=True)
            with pe.Fori(0, G // 2) as i:
                for b in range(2):
                    g = 2 * i + b
                    pe.wait_ge(tiles_hot, g + 1)
                    pe.wait_ge(hot, done(g))
                    for u in range(U):
                        last = nc.tensor.matmul(count_ps[:, 0:NT], lanes[b][:, u, :], tiles[b][:, u, :], start=False, stop=True, skip_group_check=True)
                    last.then_inc(counted, 1)
            pe.wait_ge(stepped, 2)
            nc.tensor.matmul(ends_ps[:, 0:NT], k.upto[:], r.count[:], start=True, stop=True).then_inc(summed, 1)
            nc.tensor.matmul(sums_ps[:, 0:NT], k.ones[:], r.count[:], start=True, stop=True).then_inc(summed, 1)


def move_edges(nc, name, k, e, width, r, out):
    T = NT
    with ExitStack() as ctx:
        at = Stage(nc, ctx, name)
        rec = at.sb2("rec", [P, U, width], I32)
        digits = at.sb2("digits", [P, 2, U], BF16)
        lanes, tiles = at.sb2("lanes", [P, U, P], BF16), at.sb2("tiles", [P, U, T], BF16)
        turned = at.sb2("turned", [P, U, P], BF16)
        base, base_high, base_rest = at.sb("base", [P, U, T]), at.sb2("base_high", [P, U, T], BF16), at.sb2("base_rest", [P, U, T], BF16)
        same, picked = at.sb2("same", [P, U, P], BF16), at.sb("picked", [P, U, T])
        place = at.sb2("place", [P, U], I32)
        gate = at.sb("gate", [P, 2])
        before_ps, look_ps = at.ps2("before_ps", [P, 512]), at.ps2("look_ps", [P, 512])
        turn_ps, key_ps = at.ps("turn_ps", [P, U, P], BF16), at.ps("key_ps", [P, U, P])
        moved = [at.gather_sem(f"moved{b}") for b in range(2)]
        tiles_hot, hot, held, grouped, turned_in = at.sem("tiles_hot"), at.sem("hot"), at.sem("held"), at.sem("grouped"), at.sem("turned_in")
        based, advanced, compared, looked, picks, placed = (
            at.sem("based"), at.sem("advanced"), at.sem("compared"), at.sem("looked"), at.sem("picks"), at.sem("placed"))
        gated, sent, rec_in, lanes_turned, rounded = at.sem("gated"), at.sem("sent"), at.sem("rec_in"), at.sem("lanes_turned"), at.sem("rounded")
        block = at.block()
        before = lambda b: before_ps[b][:, 0:U * T].rearrange("p (u t) -> p u t", u=U)
        look = lambda b: look_ps[b][:, 0:U * T].rearrange("p (u t) -> p u t", u=U)

        @block.sync
        def _(sp):
            sp.sem_inc(sent, 2)
            with sp.Fori(0, G // 2) as i:
                for b in range(2):
                    sp.wait_ge(moved[b], 16 * U * (i + 1))
                    sp.sem_inc(sent, 1)

        @block.scalar
        def _(act):
            def hold_digits(g, b):
                nc.scalar.copy(digits[b][:, 0, :], e.lane16[:, bass.ds(g * U, U)]).then_inc(held, 1)
                nc.scalar.copy(digits[b][:, 1, :], e.tile16[:, bass.ds(g * U, U)]).then_inc(held, 1)

            act.sem_inc(turned_in, 2)
            hold_digits(0, 0)

            def body(g, b, i, more):
                act.wait_ge(looked, freed(g))
                act.wait_ge(lanes_turned, g + 1)
                nc.scalar.copy(turned[b][:], turn_ps[:]).then_inc(turned_in, 1)
                if more:
                    act.wait_ge(grouped, done(g - 1))
                    hold_digits(g + 1, 1 - b)
                act.wait_ge(sent, freed(g))
                nc.scalar.copy(rec[b][:].bitcast(F32), e.rec[:, bass.ds(g * U, U), :].bitcast(F32)).then_inc(rec_in, 1)

            each_group(act, body)

        @block.tensor
        def _(pe):
            def group(g, b):
                pe.wait_ge(advanced, freed(g))
                pe.wait_ge(tiles_hot, g + 1)
                pe.wait_ge(hot, done(g))
                pe.wait_ge(turned_in, done(g - 1))
                for u in range(U):
                    last = nc.tensor.transpose(turn_ps[:, u, :], lanes[b][:, u, :], k.ident16[:])
                last.then_inc(lanes_turned, 1)
                for u in range(1, U):
                    for earlier in range(u):
                        nc.tensor.matmul(before(b)[:, u, :], lanes[b][:, earlier, :], tiles[b][:, earlier, :], start=(earlier == 0), stop=(earlier == u - 1))
                for u in range(U):
                    nc.tensor.matmul(before(b)[:, 0, :], lanes[b][:, u, :], tiles[b][:, u, :], start=(u == 0), stop=(u == U - 1))
                pe.wait_ge(compared, done(g - 1))
                pe.wait_ge(held, 2 * g + 2)
                for h in range(2):
                    nc.tensor.matmul(flat(key_ps[:, 4 * h:4 * h + 4, :]), k.ident16[:], k.later16[:].unsqueeze(1).to_broadcast([P, 4, P]),
                                     start=True, stop=True, skip_group_check=True)
                    for u in range(4 * h, 4 * h + 4):
                        for d in range(2):
                            last = nc.tensor.matmul(key_ps[:, u, :], digits[b][:, d, u:u + 1].to_broadcast([P, P]), k.ident16[:],
                                                    start=False, stop=True, skip_group_check=True)
                last.then_inc(grouped, 1)

            pe.sem_inc(grouped, 2)
            pe.sem_inc(looked, 2)
            group(0, 0)

            def body(g, b, i, more):
                pe.wait_ge(placed, freed(g))
                pe.wait_ge(turned_in, done(g))
                pe.wait_ge(compared, done(g))
                pe.wait_ge(rounded, 2 * g + 2)
                for u in range(U):
                    nc.tensor.matmul(look(b)[:, u, :], turned[b][:, u, :], base_high[b][:, u, :], start=True, stop=False)
                    nc.tensor.matmul(look(b)[:, u, :], turned[b][:, u, :], base_rest[b][:, u, :], start=False, stop=False)
                    last = nc.tensor.matmul(look(b)[:, u, :], same[b][:, u, :], k.ones16[:, 0:T], start=False, stop=True)
                last.then_inc(looked, 1)
                if more:
                    group(g + 1, 1 - b)

            each_group(pe, body)

        @block.vector
        def _(dve):
            def one_hots(g, b):
                dve.wait_ge(placed, freed(g))
                nc.vector.tensor_tensor(tiles[b][:], e.tile16[:, bass.ds(g * U, U)].unsqueeze(2).to_broadcast([P, U, T]),
                                        k.tiles16[:].unsqueeze(1).to_broadcast([P, U, T]), ALU.is_equal).then_inc(tiles_hot, 1)
                nc.vector.tensor_tensor(lanes[b][:], e.lane16[:, bass.ds(g * U, U)].unsqueeze(2).to_broadcast([P, U, P]),
                                        k.lanes16[:].unsqueeze(1).to_broadcast([P, U, P]), ALU.is_equal).then_inc(hot, 1)

            for s in (hot, based, advanced, compared, picks, placed):
                dve.sem_inc(s, 2)
            one_hots(0, 0)

            def body(g, b, i, more):
                dve.wait_ge(grouped, done(g))
                dve.wait_ge(advanced, done(g - 1))
                dve.wait_ge(looked, freed(g))
                nc.vector.tensor_tensor(base[:, 1:U, :], before(b)[:, 1:U, :], r.place[:].unsqueeze(1).to_broadcast([P, U - 1, T]), ALU.add).then_inc(based, 1)
                nc.vector.tensor_copy(base[:, 0, :], r.place[:]).then_inc(based, 1)
                nc.vector.tensor_tensor(same[b][:], key_ps[:], e.key[:, bass.ds(g * U, U)].unsqueeze(2).to_broadcast([P, U, P]), ALU.is_equal).then_inc(compared, 1)
                dve.wait_ge(based, 2 * g + 4)
                nc.vector.tensor_copy(base_high[b][:], base[:]).then_inc(rounded, 1)
                dve.wait_ge(rounded, 2 * g + 1)
                nc.vector.tensor_tensor(base_rest[b][:], base[:], base_high[b][:], ALU.subtract).then_inc(rounded, 1)
                nc.vector.tensor_tensor(r.place[:], r.place[:], before(b)[:, 0, :], ALU.add).then_inc(advanced, 1)
                if more:
                    one_hots(g + 1, 1 - b)
                dve.wait_ge(looked, done(g))
                dve.wait_ge(tiles_hot, g + 1)
                dve.wait_ge(placed, done(g - 1))
                nc.vector.tensor_tensor(picked[:], look(b), tiles[b][:], ALU.mult).then_inc(picks, 1)
                dve.wait_ge(picks, done(g))
                dve.wait_ge(sent, freed(g))
                with nc.allow_low_precision(reason="whole numbers below 2**24 sum in float32 and land as integers"):
                    nc.vector.tensor_reduce(place[b][:], picked[:], AX, ALU.add).then_inc(placed, 1)

            each_group(dve, body)

        @block.gpsimd
        def _(pool):
            nc.gpsimd.memset(gate[:], 0.0).then_inc(gated, 1)
            with pool.Fori(0, G // 2) as i:
                for b in range(2):
                    g = 2 * i + b
                    pool.wait_ge(gated, g + 1)
                    pool.wait_ge(rec_in, g + 1)
                    pool.wait_ge(placed, done(g))
                    nc.gpsimd.tensor_tensor(gate[:, 0:1], gate[:, 1:2], gate[:, 1:2], ALU.add).then_inc(gated, 1)
                    for u in range(U):
                        nc.gpsimd.indirect_dma_start(out=out, out_offset=bass.IndirectOffsetOnAxis(ap=place[b][:, u:u + 1], axis=0),
                                                     in_=rec[b][:, u, :], in_offset=None).then_inc(moved[b], 16)


def mark_segments(nc, name, record, column, width, keep_row, far_row):
    with ExitStack() as ctx:
        at = Stage(nc, ctx, name)
        here, keep, far = at.sb("here", [P, CH, width], I32), at.sb("keep", [P, CH]), at.sb("far", [P, CH])
        prior = at.sb("prior", [P, 2], I32)
        loaded, cleared, marked, fars, stored = at.sem("loaded"), at.sem("cleared"), at.sem("marked"), at.sem("fars"), at.sem("stored")
        block = at.block()

        @block.sync
        def _(sp):
            sp.dma_start(here[:], record.rearrange("(p j) w -> p j w", p=P)).then_inc(loaded, 16)
            sp.wait_ge(cleared, 1)
            sp.dma_start(prior[1:P, :], record.rearrange("(p j) w -> p j w", p=P)[0:P - 1, CH - 1, 0:2]).then_inc(loaded, 16)
            sp.wait_ge(fars, 1)
            sp.dma_start(keep_row.rearrange("(p j) -> p j", p=P), keep[:]).then_inc(stored, 16)
            sp.dma_start(far_row.rearrange("(p j) -> p j", p=P), far[:]).then_inc(stored, 16)
            sp.wait_ge(stored, 32)

        @block.vector
        def _(dve):
            nc.vector.memset(prior[:], -1).then_inc(cleared, 1)
            dve.wait_ge(loaded, 32)
            nc.vector.tensor_tensor(keep[:, 1:CH], here[:, 1:CH, column], here[:, 0:CH - 1, column], ALU.is_equal).then_inc(marked, 1)
            nc.vector.tensor_tensor(keep[:, 0:1], here[:, 0:1, column], prior[:, column:column + 1], ALU.is_equal).then_inc(marked, 1)
            dve.wait_ge(marked, 2)
            nc.vector.tensor_scalar(far[:], keep[:], -1.0, -FAR, ALU.add, ALU.mult).then_inc(fars, 1)


def order_edges(nc, name, k, src, dst, attr, column, width, r, out):
    with ExitStack() as ctx:
        at = Stage(nc, ctx, name)
        e = Parts()
        e.rec, e.key = at.sb("all_rec", [P, CH, width], I32), at.sb("all_key", [P, CH])
        e.lane16, e.tile16 = at.sb("all_lane", [P, CH], BF16), at.sb("all_tile", [P, CH], BF16)
        load_edges(nc, f"{name}_load", src, dst, attr, column, width, e)
        count_edges(nc, f"{name}_count", k, e, r)
        move_edges(nc, f"{name}_move", k, e, width, r, out)
    mark_segments(nc, f"{name}_mark", out, column, width, r.keep, r.far)


def sum_over_edges(nc, name, k, record, ends, table, keep_row, running):
    Q = U // 2
    with ExitStack() as ctx:
        at = Stage(nc, ctx, name)
        rec = at.sb2("rec", [P, 2, Q, 2], I32)
        keep = at.sb2("keep", [P, Q * P])
        rows = at.sb2("rows", [P, Q, 2, D])
        run = at.sb2("run", [P, Q * P])
        back = at.sb2("back", [P, Q, 2, D])
        gate = at.sb("gate", [P, 2])
        rows_ps, back_ps = at.ps2("rows_ps", [P, Q, P]), at.ps2("back_ps", [P, Q, P])
        rec_in, keep_in, gathered, stored = at.sem2("rec_in"), at.sem2("keep_in"), [at.gather_sem(f"gathered{b}") for b in range(2)], at.sem("stored")
        turned, scanned, returned, copied, sent = at.sem("turned"), at.sem("scanned"), at.sem("returned"), at.sem("copied"), at.sem("sent")
        cleared, gated = at.sem("cleared"), at.sem("gated")
        block = at.block()
        records = record.rearrange("(s c p) w -> s p c w", s=2, p=P)
        runs = running.rearrange("(s c p) f -> s p c f", s=2, p=P)

        def load_records(sp, g, b):
            for s in range(2):
                sp.dma_start(rec[b][:, s, :, :], records[s][:, bass.ds(g * Q, Q), 0:2]).then_inc(rec_in[b], 16)

        def load_keep(sp, g, b):
            for s in range(2):
                row = keep_row[s * HALF:(s + 1) * HALF].rearrange("(o e) -> o e", o=1)[:, bass.ds(g * Q * P, Q * P)]
                sp.dma_start(keep[b][s * D:(s + 1) * D, :], row.to_broadcast([D, Q * P])).then_inc(keep_in[b], 16)

        def store(sp, g, b):
            sp.wait_ge(copied, done(g))
            for s in range(2):
                sp.dma_start(runs[s][:, bass.ds(g * Q, Q), :], back[b][:, :, s, :]).then_inc(stored, 16)
            sp.wait_ge(stored, 32 * (g + 1))
            sp.sem_inc(sent, 1)

        @block.sync
        def _(sp):
            sp.sem_inc(sent, 2)
            for b in range(2):
                load_records(sp, b, b)
                load_keep(sp, b, b)
            with sp.Fori(0, G // 2 - 1) as i:
                for b in range(2):
                    g = 2 * i + b
                    sp.wait_ge(gathered[b], 16 * U * (i + 1))
                    load_records(sp, g + 2, b)
                    sp.wait_ge(scanned, done(g))
                    load_keep(sp, g + 2, b)
                    store(sp, g, b)
            for b in range(2):
                store(sp, G - 2 + b, b)

        @block.gpsimd
        def _(pool):
            nc.gpsimd.memset(gate[:], 0.0).then_inc(gated, 1)
            with pool.Fori(0, G // 2) as i:
                for b in range(2):
                    g = 2 * i + b
                    pool.wait_ge(gated, g + 1)
                    pool.wait_ge(turned, freed(g))
                    pool.wait_ge(rec_in[b], 32 * (i + 1))
                    nc.gpsimd.tensor_tensor(gate[:, 0:1], gate[:, 1:2], gate[:, 1:2], ALU.add).then_inc(gated, 1)
                    for u in range(Q):
                        for s in range(2):
                            nc.gpsimd.indirect_dma_start(out=rows[b][:, u, s, :], out_offset=None, in_=table,
                                                         in_offset=bass.IndirectOffsetOnAxis(ap=rec[b][:, s, u, ends:ends + 1], axis=0)).then_inc(gathered[b], 16)

        @block.tensor
        def _(pe):
            pe.sem_inc(turned, 2)
            pe.sem_inc(returned, 2)
            with pe.Fori(0, G // 2) as i:
                for b in range(2):
                    g = 2 * i + b
                    pe.wait_ge(scanned, freed(g))
                    pe.wait_ge(gathered[b], 16 * U * (i + 1))
                    for u in range(Q):
                        last = nc.tensor.transpose(rows_ps[b][:, u, :], flat(rows[b][:, u, :, :]), k.ident[:])
                    last.then_inc(turned, 1)
                    pe.wait_ge(copied, freed(g))
                    pe.wait_ge(scanned, done(g))
                    for u in range(Q):
                        last = nc.tensor.transpose(back_ps[b][:, u, :], run[b][:, u * P:(u + 1) * P], k.ident[:])
                    last.then_inc(returned, 1)

        @block.vector
        def _(dve):
            nc.vector.memset(run[1][:], 0.0).then_inc(cleared, 1)
            dve.wait_ge(cleared, 1)
            dve.sem_inc(scanned, 2)
            with dve.Fori(0, G // 2) as i:
                for b in range(2):
                    g = 2 * i + b
                    dve.wait_ge(keep_in[b], 32 * (i + 1))
                    dve.wait_ge(returned, freed(g))
                    dve.wait_ge(scanned, done(g - 1))
                    dve.wait_ge(turned, done(g))
                    nc.vector.tensor_tensor_scan(run[b][:], keep[b][:], flat(rows_ps[b][:]), run[1 - b][:, Q * P - 1:Q * P],
                                                 ALU.mult, ALU.add).then_inc(scanned, 1)

        @block.scalar
        def _(act):
            act.sem_inc(copied, 2)
            with act.Fori(0, G // 2) as i:
                for b in range(2):
                    g = 2 * i + b
                    act.wait_ge(sent, freed(g))
                    act.wait_ge(returned, done(g))
                    nc.scalar.copy(back[b][:].rearrange("p a s f -> p (a s f)"), flat(back_ps[b][:])).then_inc(copied, 1)


def rows_at_last_edges(nc, name, running, last_edge, out):
    with ExitStack() as ctx:
        at = Stage(nc, ctx, name)
        gathered = at.gather_sem("gathered")
        block = at.block()

        @block.gpsimd
        def _(pool):
            for t in range(NT):
                nc.gpsimd.indirect_dma_start(out=out[:, t, :], out_offset=None, in_=running,
                                             in_offset=bass.IndirectOffsetOnAxis(ap=last_edge[:, t:t + 1], axis=0)).then_inc(gathered, 16)
            pool.wait_ge(gathered, 16 * NT)


def node_sums(nc, name, running, last_edge, has_edges, crosses, scale, out):
    with ExitStack() as ctx:
        at = Stage(nc, ctx, name)
        sums, middle, part = at.sb("sums", [P, NT, D]), at.sb("middle", [P, D]), at.sb("part", [P, NT, D])
        rows_at_last_edges(nc, f"{name}_ends", running, last_edge, sums)
        loaded, stepped = at.sem("loaded"), at.sem("stepped")
        block = at.block()
        wide = lambda col: col[:].unsqueeze(2).to_broadcast([P, NT, D])

        @block.sync
        def _(sp):
            sp.dma_start(middle[:], running[HALF - 1:HALF, :].to_broadcast([P, D])).then_inc(loaded, 16)

        @block.vector
        def _(dve):
            step = Steps(dve, stepped)
            dve.wait_ge(loaded, 16)
            step(nc.vector.tensor_tensor(part[:], middle[:].unsqueeze(1).to_broadcast([P, NT, D]), wide(crosses), ALU.mult))
            step(nc.vector.tensor_tensor(sums[:], sums[:], part[:], ALU.add))
            step(nc.vector.tensor_tensor(sums[:], sums[:], wide(has_edges), ALU.mult))
            step(nc.vector.tensor_tensor(out, sums[:], wide(scale), ALU.mult))


def node_averages(nc, name, running, last_edge, has_edges, out):
    with ExitStack() as ctx:
        at = Stage(nc, ctx, name)
        sums, part = at.sb("sums", [P, NT, 2 * D]), at.sb("part", [P, NT, D])
        rows_at_last_edges(nc, f"{name}_ends", running, last_edge, sums)
        stepped = at.sem("stepped")
        block = at.block()

        @block.vector
        def _(dve):
            step = Steps(dve, stepped)
            step(nc.vector.reciprocal(part[:], sums[:, :, D:2 * D]))
            step(nc.vector.tensor_tensor(part[:], part[:], has_edges[:].unsqueeze(2).to_broadcast([P, NT, D]), ALU.mult))
            step(nc.vector.tensor_tensor(out, sums[:, :, 0:D], part[:], ALU.mult))


def linear(nc, name, k, rows, weights, width, bias, out):
    B = 5
    with ExitStack() as ctx:
        at = Stage(nc, ctx, name)
        held, turned_rows = at.sb("held", [P, B, P]), at.sb("turned_rows", [P, B, P])
        turn_ps, out_ps = at.ps("turn_ps", [P, 8, P]), at.ps("out_ps", [P, 6, 256])
        in_hand, turned, copied, multiplied, added = at.sem("in_hand"), at.sem("turned"), at.sem("copied"), at.sem("multiplied"), at.sem("added")
        block = at.block()

        @block.tensor
        def _(pe):
            pe.sem_inc(turned, 1)
            pe.sem_inc(multiplied, 1)
            with pe.Fori(0, NT // B) as j:
                pe.wait_ge(copied, j + 1)
                pe.wait_ge(in_hand, j + 1)
                for t in range(B):
                    last = nc.tensor.transpose(turn_ps[:, t, :], held[:, t, :], k.ident[:])
                last.then_inc(turned, 1)
                pe.wait_ge(added, j + 1)
                pe.wait_ge(copied, j + 2)
                for t in range(B):
                    last = nc.tensor.matmul(out_ps[:, t, 0:width], turned_rows[:, t, :], weights[:, 0:width], start=True, stop=True)
                last.then_inc(multiplied, 1)

        @block.scalar
        def _(act):
            act.sem_inc(copied, 1)
            with act.Fori(0, NT // B) as j:
                act.wait_ge(turned, j + 1)
                nc.scalar.copy(held[:], rows[:, bass.ds(B * j, B), :]).then_inc(in_hand, 1)
                act.wait_ge(multiplied, j + 1)
                act.wait_ge(turned, j + 2)
                nc.scalar.copy(flat(turned_rows[:]), flat(turn_ps[:, 0:B, :])).then_inc(copied, 1)

        @block.vector
        def _(dve):
            dve.sem_inc(added, 1)
            with dve.Fori(0, NT // B) as j:
                dve.wait_ge(multiplied, j + 2)
                nc.vector.tensor_tensor(out[:, bass.ds(B * j, B), 0:width], out_ps[:, 0:B, 0:width],
                                        bias[:, 0:width].unsqueeze(1).to_broadcast([P, B, width]), ALU.add).then_inc(added, 1)


def layer_norm(nc, step, root, x, out, centred, squares, stat):
    v = nc.vector
    wide = lambda: stat[:].unsqueeze(2).to_broadcast([P, NT, D])
    step(v.tensor_reduce(stat[:], x, AX, ALU.add))
    step(v.tensor_scalar(stat[:], stat[:], 1.0 / D, None, ALU.mult))
    step(v.tensor_tensor(centred[:], x, wide(), ALU.subtract))
    step(v.tensor_tensor(squares[:], centred[:], centred[:], ALU.mult))
    step(v.tensor_reduce(stat[:], squares[:], AX, ALU.add))
    step(v.tensor_scalar(stat[:], stat[:], 1.0 / D, EPS, ALU.mult, ALU.add))
    root()
    step(v.reciprocal(stat[:], stat[:]))
    step(v.tensor_tensor(centred[:], centred[:], wide(), ALU.mult))
    step(v.tensor_scalar(out, centred[:], 0.0, None, ALU.max))


def attention_pass(nc, name, k, record, width, near, table, near_table, near_width, far_row, running, front):
    L = U * P
    far_end = DST if near == SRC else SRC
    with ExitStack() as ctx:
        at = Stage(nc, ctx, name)
        w = Parts()
        w.at, w.nc, w.k = at, nc, k
        w.rec = at.sb2("rec", [P, U, width], I32)
        w.wide_rows = at.sb2("wide_rows", [P, U, table.shape[1]])
        w.near_rows = at.sb2("near_rows", [P, U, near_width])
        w.logits = at.sb("logits", [P, U, 4])
        w.logits_wide = at.sb("logits_wide", [P, U, 2, D])
        w.logits_ps, w.values_ps = at.ps("logits_ps", [P, U, P]), at.ps("values_ps", [P, U, P])
        back_ps = at.ps("back_ps", [P, U // 2, P])
        far = at.sb2("far", [P, L])
        top = at.sb2("top", [P, 1 + L])
        fade = at.sb("fade", [P, 2, L])
        scaled = at.sb("scaled", [P, L])
        run = at.sb2("run", [P, L])
        back = at.sb2("back", [P, U, P])
        gate = at.sb("gate", [P, 2])
        w.rec_in, far_in, w.gathered, stored = at.sem2("rec_in"), at.sem2("far_in"), [at.gather_sem(f"gathered{b}") for b in range(2)], at.sem("stored")
        w.rows_used, gated, cleared = at.sem("rows_used"), at.sem("gated"), at.sem("cleared")
        w.logits_made, w.widened = at.sem("logits_made"), at.sem("widened")
        w.rec_used, scaled_done = at.sem("rec_used"), at.sem("scaled_done")
        turned = w.turned = at.sem("turned")
        topped, exponents, factors = at.sem("topped"), at.sem("exponents"), at.sem("factors")
        weighted, scanned, returned, copied, sent = at.sem("weighted"), at.sem("scanned"), at.sem("returned"), at.sem("copied"), at.sem("sent")
        front.buffers(w)
        block = at.block()
        records = record.rearrange("(c p) w -> p c w", p=P)
        runs = running.rearrange("(c p) f -> p c f", p=P)
        far_ap = far_row.rearrange("(o e) -> o e", o=1)

        @block.sync
        def _(sp):
            def load(g, b):
                sp.dma_start(w.rec[b][:], records[:, bass.ds(g * U, U), :]).then_inc(w.rec_in[b], 16)

            def load_far(g, b):
                sp.dma_start(far[b][:], far_ap[:, bass.ds(g * L, L)].to_broadcast([P, L])).then_inc(far_in[b], 16)

            def first():
                sp.sem_inc(sent, 2)
                for b in range(2):
                    load(b, b)
                    load_far(b, b)

            def body(g, b, i, more):
                if not isinstance(g, int):
                    sp.wait_ge(w.rec_used, done(g))
                    sp.wait_ge(w.gathered[b], 16 * 2 * U * (i + 1))
                    load(g + 2, b)
                    sp.wait_ge(exponents, done(g))
                    load_far(g + 2, b)
                sp.wait_ge(copied, 2 * g + 2 + 1)
                sp.dma_start(runs[:, bass.ds(g * U, U), :], back[b][:]).then_inc(stored, 16)
                sp.wait_ge(stored, 16 * (g + 1))
                sp.sem_inc(sent, 1)

            first()
            each_group(sp, body)

        @block.gpsimd
        def _(pool):
            nc.gpsimd.memset(gate[:], 0.0).then_inc(gated, 1)
            with pool.Fori(0, G // 2) as i:
                for b in range(2):
                    g = 2 * i + b
                    pool.wait_ge(gated, g + 1)
                    pool.wait_ge(w.rows_used, freed(g))
                    pool.wait_ge(turned, freed(g))
                    pool.wait_ge(w.rec_in[b], 16 * (i + 1))
                    nc.gpsimd.tensor_tensor(gate[:, 0:1], gate[:, 1:2], gate[:, 1:2], ALU.add).then_inc(gated, 1)
                    for u in range(U):
                        nc.gpsimd.indirect_dma_start(out=w.wide_rows[b][:, u, :], out_offset=None, in_=table,
                                                     in_offset=bass.IndirectOffsetOnAxis(ap=w.rec[b][:, u, far_end:far_end + 1], axis=0)).then_inc(w.gathered[b], 16)
                        nc.gpsimd.indirect_dma_start(out=w.near_rows[b][:, u, :], out_offset=None, in_=near_table,
                                                     in_offset=bass.IndirectOffsetOnAxis(ap=w.rec[b][:, u, near:near + 1], axis=0)).then_inc(w.gathered[b], 16)

        @block.tensor
        def _(pe):
            def turn(g, b, i):
                front.pe(w, pe, g, b, i)
                pe.wait_ge(exponents, done(g - 1))
                pe.wait_ge(w.widened, 2 * g + 4)
                for u in range(U):
                    nc.tensor.transpose(w.logits_ps[:, u, :], flat(w.logits_wide[:, u, :, :]), k.ident[:])
                pe.wait_ge(weighted, done(g - 1))
                front.values_ready(w, pe, g, b, i)
                for u in range(U):
                    last = nc.tensor.transpose(w.values_ps[:, u, :], front.values(w, b, u), k.ident[:])
                last.then_inc(turned, 1)

            def first():
                pe.sem_inc(turned, 2)
                pe.sem_inc(returned, 4)
                front.pe_start(w, pe)
                turn(0, 0, 0)

            def body(g, b, i, more):
                if more:
                    turn(g + 1, 1 - b, i + b)
                pe.wait_ge(scanned, done(g))
                for h in range(2):
                    pe.wait_ge(copied, 2 * g + h + 1)
                    for u in range(U // 2):
                        c = h * U // 2 + u
                        last = nc.tensor.transpose(back_ps[:, u, :], run[b][:, c * P:(c + 1) * P], k.ident[:])
                    last.then_inc(returned, 1)

            first()
            each_group(pe, body)

        @block.vector
        def _(dve):
            def first():
                nc.vector.memset(run[1][:], 0.0).then_inc(cleared, 1)
                nc.vector.memset(top[1][:], FAR).then_inc(cleared, 1)
                for s in (topped, exponents, weighted, scanned, w.logits_made):
                    dve.sem_inc(s, 2)
                dve.wait_ge(cleared, 2)
                front.dve_start(w, dve)
                front.dve(w, dve, 0, 0, 0)

            def body(g, b, i, more):
                if more:
                    front.dve_early(w, dve, g + 1, 1 - b, i + b)
                dve.wait_ge(exponents, done(g - 1))
                nc.vector.tensor_copy(top[b][:, 0:1], top[1 - b][:, L:L + 1]).then_inc(topped, 1)
                dve.wait_ge(topped, 2 * g + 1 + 2)
                dve.wait_ge(far_in[b], 16 * (i + 1))
                dve.wait_ge(turned, done(g))
                nc.vector.tensor_tensor_scan(top[b][:, 1:1 + L], far[b][:], flat(w.logits_ps[:]), top[b][:, 0:1],
                                             ALU.add, ALU.max).then_inc(topped, 1)
                dve.wait_ge(topped, 2 * g + 2 + 2)
                dve.wait_ge(scanned, done(g - 1))
                nc.vector.tensor_tensor(scaled[:], top[b][:, 0:L], far[b][:], ALU.add).then_inc(scaled_done, 1)
                nc.vector.tensor_tensor(fade[:, 1, :], flat(w.logits_ps[:]), top[b][:, 1:1 + L], ALU.subtract).then_inc(scaled_done, 1)
                dve.wait_ge(scaled_done, 2 * g + 2)
                nc.vector.tensor_tensor(fade[:, 0, :], scaled[:], top[b][:, 1:1 + L], ALU.subtract).then_inc(exponents, 1)
                if more:
                    front.dve(w, dve, g + 1, 1 - b, i + b)
                dve.wait_ge(exponents, done(g))
                dve.wait_ge(factors, g + 1)
                nc.vector.tensor_tensor(scaled[:], flat(w.values_ps[:]), fade[:, 1, :], ALU.mult).then_inc(weighted, 1)
                dve.wait_ge(weighted, done(g))
                dve.wait_ge(returned, 2 * g + 2)
                nc.vector.tensor_tensor_scan(run[b][:], fade[:, 0, :], scaled[:], run[1 - b][:, L - 1:L], ALU.mult, ALU.add).then_inc(scanned, 1)

            first()
            each_group(dve, body)

        @block.scalar
        def _(act):
            def widen(g, b):
                act.wait_ge(turned, done(g - 1))
                act.wait_ge(w.logits_made, done(g))
                H = front.heads
                for s in range(2):
                    nc.scalar.activation(w.logits_wide[:, :, s, :].rearrange("p u (h f) -> p u h f", h=H),
                                         w.logits[:, :, 0:H].unsqueeze(3).to_broadcast([P, U, H, D // H]),
                                         ACT.Identity, bias=front.logit_bias).then_inc(w.widened, 1)

            def first():
                act.sem_inc(copied, 1)
                act.sem_inc(w.widened, 2)
                front.act_start(w, act)
                front.act(w, act, 0, 0, 0)
                widen(0, 0)

            def body(g, b, i, more):
                if more:
                    front.act(w, act, g + 1, 1 - b, i + b)
                act.wait_ge(exponents, done(g))
                nc.scalar.activation(fade[:].rearrange("p a l -> p (a l)"), fade[:].rearrange("p a l -> p (a l)"), ACT.Exp).then_inc(factors, 1)
                if more:
                    widen(g + 1, 1 - b)
                act.wait_ge(sent, freed(g))
                for h in range(2):
                    act.wait_ge(returned, 2 * g + h + 5)
                    nc.scalar.copy(flat(back[b][:, h * U // 2:(h + 1) * U // 2, :]), flat(back_ps[:])).then_inc(copied, 1)

            first()
            each_group(act, body)


class FilterFront:

    heads, logit_bias = 4, 0.0
    F = 32

    def __init__(self, weights):
        self.c = weights

    def buffers(self, w):
        at = w.at
        self.features_ps = at.ps("features_ps", [P, 2, 2 * P])
        self.filter_ps = at.ps("filter_ps", [P, U, 2, self.F])
        self.packed = at.sb("packed", [P, U, self.F])
        self.features, self.size, self.log = at.sb("features", [P, 2 * P]), at.sb("size", [P, 2 * P]), at.sb("log", [P, 2 * P])
        self.positive, self.soft = at.sb("positive", [P, 2 * P]), at.sb("soft", [P, 2 * P])
        self.keyed, self.queried, self.sums = at.sb("keyed", [P, U, D]), at.sb("queried", [P, U, D]), at.sb("sums", [P, U, 4])
        self.value_rows = at.sb("value_rows", [P, U, 2 * D])
        self.features_turned, self.features_in, self.hidden, self.sized, self.raised, self.logged = (
            at.sem("features_turned"), at.sem("features_in"), at.sem("hidden"), at.sem("sized"), at.sem("raised"), at.sem("logged"))
        self.rectified, self.softened, self.filtered, self.stepped, self.ones_set = (
            at.sem("rectified"), at.sem("softened"), at.sem("filtered"), at.sem("stepped"), at.sem("ones_set"))

    def values(self, w, b, u):
        return self.value_rows[:, u, :]

    def values_ready(self, w, pe, g, b, i):
        pe.wait_ge(w.rows_used, done(g))

    def act_start(self, w, act):
        for s in (w.rec_used, self.features_in, self.sized, self.raised, self.logged):
            act.sem_inc(s, 2)

    def act(self, w, act, g, b, i):
        nc = w.nc
        act.wait_ge(self.features_turned, done(g - 1))
        act.wait_ge(w.rec_in[b], 16 * (i + 1))
        nc.scalar.copy(self.packed[:], w.rec[b][:, :, 2:2 + self.F].bitcast(F32)).then_inc(w.rec_used, 1)
        act.wait_ge(self.hidden, done(g - 1))
        act.wait_ge(self.features_turned, done(g))
        nc.scalar.copy(self.features[:], self.features_ps[:, 0, :]).then_inc(self.features_in, 1)
        act.wait_ge(self.softened, done(g - 1))
        act.wait_ge(self.hidden, done(g))
        nc.scalar.activation(self.size[:], self.features_ps[:, 1, :], ACT.Abs, bias=self.c.hidden_bias[:]).then_inc(self.sized, 1)
        act.wait_ge(self.sized, done(g))
        nc.scalar.activation(self.size[:], self.size[:], ACT.Exp, scale=-1.0).then_inc(self.raised, 1)
        act.wait_ge(self.raised, done(g))
        nc.scalar.activation(self.log[:], self.size[:], ACT.Ln, scale=0.5, bias=self.c.half[:]).then_inc(self.logged, 1)

    def pe_start(self, w, pe):
        for s in (self.features_turned, self.hidden, self.filtered):
            pe.sem_inc(s, 2)

    def pe(self, w, pe, g, b, i):
        nc, k, F = w.nc, w.k, self.F
        pe.wait_ge(self.softened, done(g - 1))
        pe.wait_ge(w.rec_used, done(g))
        for h in range(2):
            last = nc.tensor.transpose(self.features_ps[:, 0, h * P:(h + 1) * P], flat(self.packed[:, 4 * h:4 * h + 4, :]), k.ident[:])
        last.then_inc(self.features_turned, 1)
        pe.wait_ge(self.features_in, done(g))
        nc.tensor.matmul(self.features_ps[:, 1, :], self.c.hidden[:], self.features[:], start=True, stop=True).then_inc(self.hidden, 1)
        pe.wait_ge(w.rows_used, done(g - 1))
        pe.wait_ge(self.softened, done(g))
        for h in range(2):
            out = self.filter_ps[:, 4 * h:4 * h + 4, 0, :]
            nc.tensor.matmul(out, self.soft[:, h * P:(h + 1) * P], self.c.filter[:], start=True, stop=False)
            last = nc.tensor.matmul(out, k.ones[0:1, :], self.c.filter_bias[:], start=False, stop=True)
        last.then_inc(self.filtered, 1)

    def dve_start(self, w, dve):
        for s in (w.rows_used, self.rectified, self.softened):
            dve.sem_inc(s, 2)
        w.nc.vector.memset(self.value_rows[:], 1.0).then_inc(self.ones_set, 1)
        dve.wait_ge(self.ones_set, 1)
        self.dve_early(w, dve, 0, 0, 0)

    def dve_early(self, w, dve, g, b, i):
        nc = w.nc
        dve.wait_ge(self.softened, done(g - 1))
        dve.wait_ge(self.sized, done(g))
        nc.vector.tensor_scalar(self.positive[:], self.features_ps[:, 1, :], self.c.hidden_bias[:], 0.0, ALU.add, ALU.max).then_inc(self.rectified, 1)
        dve.wait_ge(self.rectified, done(g))
        dve.wait_ge(self.filtered, done(g - 1))
        dve.wait_ge(self.logged, done(g))
        nc.vector.tensor_tensor(self.soft[:], self.positive[:], self.log[:], ALU.add).then_inc(self.softened, 1)

    def dve(self, w, dve, g, b, i):
        nc, H = w.nc, self.heads
        heads = lambda ap: ap.rearrange("p u (h f) -> p u h f", h=H)
        filters = lambda at: self.filter_ps[:, :, 0, at:at + D // H].unsqueeze(2).to_broadcast([P, U, H, D // H])
        dve.wait_ge(w.gathered[b], 16 * 2 * U * (i + 1))
        dve.wait_ge(self.filtered, done(g))
        dve.wait_ge(w.logits_made, done(g - 1))
        nc.vector.tensor_tensor(heads(self.keyed[:]), heads(w.wide_rows[b][:, :, 0:D]), filters(0), ALU.mult).then_inc(self.stepped, 1)
        dve.wait_ge(self.stepped, 3 * g + 1)
        nc.vector.tensor_tensor(self.queried[:], self.keyed[:], w.near_rows[b][:, :, 0:D], ALU.mult).then_inc(self.stepped, 1)
        dve.wait_ge(self.stepped, 3 * g + 2)
        nc.vector.tensor_reduce(self.sums[:], heads(self.queried[:]), AX, ALU.add).then_inc(self.stepped, 1)
        dve.wait_ge(self.stepped, 3 * g + 3)
        dve.wait_ge(w.widened, 2 * g + 2)
        nc.vector.tensor_tensor(w.logits[:], self.sums[:], w.near_rows[b][:, :, D:D + H], ALU.add).then_inc(w.logits_made, 1)
        dve.wait_ge(w.turned, done(g - 1))
        nc.vector.tensor_tensor(heads(self.value_rows[:, :, 0:D]), heads(w.wide_rows[b][:, :, D:2 * D]), filters(D // H), ALU.mult).then_inc(w.rows_used, 1)


class MixFront:

    heads = 2
    F = 2

    def __init__(self, weights):
        self.c = weights
        self.logit_bias = weights.out_bias[:]

    def buffers(self, w):
        at = w.at
        self.features = at.sb("features", [P, U, self.F])
        self.turned_features = at.sb("turned_features", [U * self.F, P])
        self.edge = at.sb("edge", [P, U // 2, P])
        self.with_keys, self.mixed_rows, self.hidden = at.sb("with_keys", [P, U, D]), at.sb("mixed_rows", [P, U, D]), at.sb("hidden", [P, U, D])
        self.features_ps = at.ps("features_ps", [P, 4 * P])
        self.edge_ps = at.ps("edge_ps", [P, U // 2, P])
        self.mix_ps = at.ps("mix_ps", [P, 2, U // 2, D])
        self.features_turned, self.features_in, self.edged, self.rectified = (
            at.sem("features_turned"), at.sem("features_in"), at.sem("edged"), at.sem("rectified"))
        self.mixed, self.mix_read, self.stepped = at.sem("mixed"), at.sem("mix_read"), at.sem("stepped")

    def values(self, w, b, u):
        return w.wide_rows[b][:, u, D:3 * D]

    def values_ready(self, w, pe, g, b, i):
        pe.wait_ge(w.gathered[b], 16 * 2 * U * (i + 1))

    def act_start(self, w, act):
        for s in (w.rec_used, self.features_in, self.rectified):
            act.sem_inc(s, 2)

    def act(self, w, act, g, b, i):
        nc = w.nc
        act.wait_ge(self.features_turned, done(g - 1))
        act.wait_ge(w.rec_in[b], 16 * (i + 1))
        nc.scalar.copy(self.features[:], w.rec[b][:, :, 2:4].bitcast(F32)).then_inc(w.rec_used, 1)
        act.wait_ge(self.edged, done(g - 1))
        act.wait_ge(self.features_turned, done(g))
        nc.scalar.copy(self.turned_features[:], self.features_ps[0:U * self.F, 0:P]).then_inc(self.features_in, 1)
        act.wait_ge(self.mixed, done(g - 1))
        act.wait_ge(self.edged, done(g))
        nc.scalar.activation(flat(self.edge[:]), flat(self.edge_ps[:]), ACT.Relu, bias=self.c.edge_bias[:]).then_inc(self.rectified, 1)

    def pe_start(self, w, pe):
        for s in (self.features_turned, self.edged, self.mixed):
            pe.sem_inc(s, 2)

    def pe(self, w, pe, g, b, i):
        nc, k = w.nc, w.k
        pe.wait_ge(self.features_in, done(g - 1))
        pe.wait_ge(w.rec_used, done(g))
        nc.tensor.transpose(self.features_ps[0:U * self.F, 0:P], flat(self.features[:]), k.ident[:]).then_inc(self.features_turned, 1)
        pe.wait_ge(self.rectified, done(g - 1))
        pe.wait_ge(self.features_in, done(g))
        for u in range(U // 2):
            last = nc.tensor.matmul(self.edge_ps[:, u, :], self.c.edge[:, u, :], self.turned_features[:], start=True, stop=True)
        last.then_inc(self.edged, 1)
        pe.wait_ge(self.mix_read, done(g - 1))
        pe.wait_ge(self.rectified, done(g))
        for u in range(U // 2):
            last = nc.tensor.matmul(self.mix_ps[:, :, u, :], self.edge[:, u, :], self.c.mix[:], start=True, stop=True)
        last.then_inc(self.mixed, 1)

    def dve_start(self, w, dve):
        for s in (w.rows_used, self.mix_read):
            dve.sem_inc(s, 2)

    def dve_early(self, w, dve, g, b, i):
        pass

    def dve(self, w, dve, g, b, i):
        nc, H = w.nc, self.heads
        dve.wait_ge(w.gathered[b], 16 * 2 * U * (i + 1))
        dve.wait_ge(self.mixed, done(g))
        dve.wait_ge(w.logits_made, done(g - 1))
        nc.vector.tensor_tensor(self.with_keys[:], self.mix_ps[:].rearrange("p a u f -> p (a u) f"), w.wide_rows[b][:, :, 0:D], ALU.add).then_inc(self.mix_read, 1)
        dve.wait_ge(self.mix_read, done(g))
        nc.vector.tensor_tensor(self.mixed_rows[:], self.with_keys[:], w.near_rows[b][:, :, 0:D], ALU.add).then_inc(w.rows_used, 1)
        dve.wait_ge(w.rows_used, done(g))
        nc.vector.scalar_tensor_tensor(self.hidden[:], self.mixed_rows[:], 0.0, self.c.out[:].unsqueeze(1).to_broadcast([P, U, D]), ALU.max, ALU.mult).then_inc(self.stepped, 1)
        dve.wait_ge(self.stepped, g + 1)
        dve.wait_ge(w.widened, 2 * g + 2)
        nc.vector.tensor_reduce(w.logits[:, :, 0:H], self.hidden[:].rearrange("p u (h f) -> p u h f", h=H), AX, ALU.add).then_inc(w.logits_made, 1)


def make_weight_buffers(sb):
    c, c_filter, c_mix = Parts(), Parts(), Parts()
    c.sage1 = sb("sage1", [P, P])
    c.sage1_bias = sb("sage1_bias", [P, P])
    c.sage2 = sb("sage2", [P, P])
    c.sage2_bias = sb("sage2_bias", [P, P])
    c.tables1 = sb("tables1", [P, 196])
    c.tables1_bias = sb("tables1_bias", [P, 196])
    c.value1 = sb("value1", [P, D])
    c.value1_bias = sb("value1_bias", [P, D])
    c.value_bias1 = sb("value_bias1", [P, D])
    c.out1 = sb("out1", [P, D])
    c.out1_bias = sb("out1_bias", [P, D])
    c.gcn = sb("gcn", [P, D])
    c.gcn_bias = sb("gcn_bias", [P, D])
    c.kqv = sb("kqv", [P, 3 * D])
    c.kqv_bias = sb("kqv_bias", [P, 3 * D])
    c.mix3 = sb("mix3", [P, P])
    c.mix3_bias = sb("mix3_bias", [P, P])
    c.out3 = sb("out3", [P, D])
    c.edge_count_bias = sb("edge_count_bias", [P, D])
    c.gamma = sb("gamma", [P, D])
    c.beta = sb("beta", [P, D])
    c_filter.hidden = sb("hidden_w", [P, P])
    c_filter.hidden_bias = sb("hidden_b", [P, 1])
    c_filter.filter = sb("filter_w", [P, P])
    c_filter.filter_bias = sb("filter_b", [1, P])
    c_filter.half = sb("half", [P, 1])
    c_mix.edge = sb("edge_w", [2 * U, U // 2, P])
    c_mix.edge_bias = sb("edge_b", [P, 1])
    c_mix.mix = sb("mix_w", [P, P])
    c_mix.out = sb("mix_out", [P, D])
    c_mix.out_bias = sb("mix_out_b", [P, 1])
    c.filter, c.mix = c_filter, c_mix
    return c


def load_weights(nc, name, k, a):
    c = k.weights
    with ExitStack() as ctx:
        at = Stage(nc, ctx, name)
        more1, more2 = at.sb("more1", [P, 2 * D]), at.sb("more2", [P, D])
        more_bias1, more_bias2 = at.sb("more_bias1", [P, 2 * D]), at.sb("more_bias2", [P, D])
        query, key = at.sb("query", [D, 2 * D]), at.sb("key", [D, D + 4])
        query_ps = at.ps("query_ps", [P, 512])
        cleared, loaded, stepped, multiplied = at.sem("cleared"), at.sem("loaded"), at.sem("stepped"), at.sem("multiplied")
        block = at.block()
        zeroed = [c.sage2_bias, c.tables1, c.tables1_bias, c.value1, c.out1, c.gcn, c.kqv, c.mix3, c.mix3_bias, c.out3,
                  c.filter.hidden, c.filter.filter, c.mix.edge, c.mix.mix, query, key]
        row = lambda v: v.rearrange("(o f) -> o f", o=1)
        every = lambda v: row(v).to_broadcast([P, v.shape[0]])
        column = lambda v: v.rearrange("(f o) -> f o", o=1)
        moves = [
            (c.sage1[0:D, :], a["W1n"]), (c.sage1[D:P, :], a["W1r"]), (more1[D:P, :], a["Wl1"]),
            (c.sage1_bias[:], every(a["b1n"])), (more_bias1[:], every(a["bl1"])),
            (c.sage2[:, 0:D], a["W2n"]), (c.sage2[:, D:P], a["W2r"]), (more2[:], a["Wl2"]),
            (c.sage2_bias[:, D:P], every(a["b2n"])), (more_bias2[:], every(a["bl2"])),
            (c.value1[D:P, :], a["cen_wT"]), (c.value1_bias[:], every(a["cen_b"])),
            (c.out1[0:D, :], a["out_wT"]), (c.out1_bias[:], every(a["out_b"])),
            (c.gcn[0:D, :], a["gcn_w"]), (c.gcn_bias[:], every(a["gcn_b"])),
            (c.kqv[D:P, :], a["W_kqv"]), (c.kqv_bias[:], every(a["b_kqv"])),
            (c.out3[0:D, :], a["W_out"]), (c.edge_count_bias[:], every(a["b_out"])),
            (c.gamma[:], every(a["gamma"])), (c.beta[:], every(a["beta"])),
            (c.mix.out_bias[:], every(a["b_att2"])),
        ]
        for h in range(4):
            s = slice(16 * h, 16 * (h + 1))
            under = slice(D + 16 * h, D + 16 * (h + 1))
            moves += [(c.tables1[under, s], a["k_wT"][h]), (c.tables1[under, under], a["v_wT"][h]),
                      (query[s, under], a["q_w"][h]), (key[s, s], a["wkl_w"]), (key[s, D + h:D + h + 1], column(a["wkl_b"])),
                      (c.value1[s, s], a["wvl_wT"]), (c.value_bias1[:, s], every(a["wvl_b"]))]
        for u in range(4):
            lo, hi = slice(32 * u, 32 * u + 16), slice(32 * u + 16, 32 * u + 32)
            both = slice(32 * u, 32 * u + 32)
            moves += [(c.filter.hidden[both, lo], a["wkn_w1T"]), (c.filter.hidden[both, hi], a["wvn_w1T"]),
                      (c.filter.hidden_bias[lo, :], column(a["wkn_b1"])), (c.filter.hidden_bias[hi, :], column(a["wvn_b1"])),
                      (c.filter.filter[lo, lo], a["wkn_w2T"]), (c.filter.filter[hi, hi], a["wvn_w2T"]),
                      (c.filter.filter_bias[:, lo], row(a["wkn_b2"])), (c.filter.filter_bias[:, hi], row(a["wvn_b2"]))]
            for half in range(2):
                chunk = u + 4 * half
                moves.append((c.mix.edge[2 * chunk:2 * chunk + 2, u, half * D:(half + 1) * D], a["W_edge"]))
        for h in range(2):
            s = slice(32 * h, 32 * (h + 1))
            under = slice(D + 32 * h, D + 32 * (h + 1))
            moves += [(c.mix3[s, under], a["W_att1"][32:64, :]), (c.mix3[under, s], a["W_att1"][0:32, :]),
                      (c.mix3_bias[:, under], every(a["b_att1"])), (c.mix.out[:, s], every(a["w_att2"])),
                      (c.mix.mix[s, s], a["W_att1"][64:96, :]), (c.mix.mix[under, under], a["W_att1"][64:96, :]),
                      (c.mix.edge_bias[h * D:(h + 1) * D, :], column(a["b_edge"]))]

        @block.sync
        def _(sp):
            sp.wait_ge(cleared, len(zeroed))
            with nc.allow_non_contiguous_dma(reason="small biases turned into columns"):
                for out, in_ in moves:
                    sp.dma_start(out, in_).then_inc(loaded, 16)

        @block.tensor
        def _(pe):
            pe.wait_ge(loaded, 16 * len(moves))
            nc.tensor.matmul(query_ps[:, 0:D + 4], query[:], key[:], start=True, stop=True).then_inc(multiplied, 1)

        @block.vector
        def _(dve):
            for z in zeroed:
                nc.vector.memset(z[:], 0.0).then_inc(cleared, 1)
            nc.vector.memset(c.filter.half[:], 0.5)
            step = Steps(dve, stepped)
            dve.wait_ge(loaded, 16 * len(moves))
            step(nc.vector.tensor_tensor(c.sage1[D:P, :], c.sage1[D:P, :], more1[D:P, :], ALU.add))
            step(nc.vector.tensor_tensor(c.sage2[:, D:P], c.sage2[:, D:P], more2[:], ALU.add))
            step(nc.vector.tensor_tensor(c.sage1_bias[:], c.sage1_bias[:], more_bias1[:], ALU.add))
            step(nc.vector.tensor_tensor(c.sage2_bias[:, D:P], c.sage2_bias[:, D:P], more_bias2[:], ALU.add))
            step(nc.vector.tensor_scalar(c.mix3[D:P, :], c.mix3[D:P, :], 32.0 ** -0.5, None, ALU.mult))
            dve.wait_ge(multiplied, 1)
            step(nc.vector.tensor_copy(c.tables1[:, P:P + D + 4], query_ps[:, 0:D + 4]))


def node_stage(nc, name, k, program, stores=(), roots=0):
    with ExitStack() as ctx:
        at = Stage(nc, ctx, name)
        centred, squares, stat = at.sb("centred", [P, NT, D]), at.sb("squares", [P, NT, D]), at.sb("stat", [P, NT])
        stepped, stored, finished = at.sem("stepped"), at.sem("stored"), at.sem("finished")
        squared, rooted = at.sem("squared"), at.sem("rooted")
        block = at.block()

        @block.vector
        def _(dve):
            step = Steps(dve, stepped)
            given = [0]

            def root():
                given[0] += 1
                dve.sem_inc(squared, 1)
                dve.wait_ge(rooted, given[0])

            norm = lambda x, out: layer_norm(nc, step, root, x, out, centred, squares, stat)
            o = Parts()
            o.v, o.step, o.root, o.norm, o.tmp, o.stat = nc.vector, step, root, norm, centred, stat
            program(o)
            dve.sem_inc(finished, 1)

        @block.scalar
        def _(act):
            for r in range(roots):
                act.wait_ge(squared, r + 1)
                nc.scalar.sqrt(stat[:], stat[:]).then_inc(rooted, 1)

        @block.sync
        def _(sp):
            sp.wait_ge(finished, 1)
            for out, in_ in stores:
                sp.dma_start(out, in_).then_inc(stored, 16)
            if stores:
                sp.wait_ge(stored, 16 * len(stores))


def shifted_softplus(nc, name, k, x, out):
    with ExitStack() as ctx:
        at = Stage(nc, ctx, name)
        size = at.sb("size", [P, NT, D])
        sized, logged, stepped = at.sem("sized"), at.sem("logged"), at.sem("stepped")
        block = at.block()

        @block.scalar
        def _(act):
            step = Steps(act, sized)
            step(nc.scalar.activation(size[:], x, ACT.Abs))
            step(nc.scalar.activation(size[:], size[:], ACT.Exp, scale=-1.0))
            nc.scalar.activation(size[:], size[:], ACT.Ln, scale=0.5, bias=k.weights.filter.half[:]).then_inc(logged, 1)

        @block.vector
        def _(dve):
            dve.wait_ge(logged, 1)
            nc.vector.scalar_tensor_tensor(out, x, 0.0, size[:], ALU.max, ALU.add).then_inc(stepped, 1)


def build(nc, a, out):
    dram = lambda name, shape, dt=F32: nc.dram_tensor(name, shape, dt, kind="Internal").ap()
    by_tile = lambda table: table.rearrange("(t p) f -> p t f", p=P)
    with ExitStack() as ctx:
        sb = Stage(nc, ctx, "all").sb
        count, before, upto, ident, ones = (sb(n, [P, P]) for n in ("count", "before", "upto", "ident", "ones"))
        k = Parts()
        k.count, k.before, k.upto, k.ident, k.ones = count, before, upto, ident, ones
        k.ones16, k.ident16, k.lanes16, k.later16 = (sb(n, [P, P], BF16) for n in ("ones16", "ident16", "lanes16", "later16"))
        k.tiles16 = sb("tiles16", [P, NT], BF16)
        k.weights = make_weight_buffers(sb)
        c = k.weights
        make_constants(nc, "constants", k)
        load_weights(nc, "weights", k, a)

        by_dst, by_src = dram("by_dst", (EP, 4), I32), dram("by_src", (EP, 34), I32)
        rows = [Parts(), Parts()]
        for r, n in zip(rows, ("dst", "src")):
            r.keep, r.far = dram(f"keep_{n}", (EP,)), dram(f"far_{n}", (EP,))
            r.count, r.some, r.crosses = sb(f"count_{n}", [P, NT]), sb(f"some_{n}", [P, NT]), sb(f"crosses_{n}", [P, NT])
            r.last, r.place = sb(f"last_{n}", [P, NT], I32), sb(f"place_{n}", [P, NT])
        into, outof = rows
        order_edges(nc, "sort_dst", k, a["src"], a["dst"], a["edge_attr_2"], DST, 4, into, by_dst)
        order_edges(nc, "sort_src", k, a["src"], a["dst"], a["edge_attr_32"], SRC, 34, outof, by_src)

        x, wide, tall = sb("x", [P, NT, D]), sb("wide", [P, NT, P]), sb("tall", [P, NT, 196])
        scale = sb("scale", [P, NT])
        summed, own = wide[:, :, 0:D], wide[:, :, D:P]
        over = lambda col: col[:].unsqueeze(2).to_broadcast([P, NT, D])
        each = lambda bias: bias[:].unsqueeze(1).to_broadcast([P, NT, D])
        table = dram("table", (NP, D))
        running, weighted = dram("running", (EP, D)), dram("weighted", (EP, P))
        with ExitStack() as first:
            at = Stage(nc, first, "load_x")
            loaded, cleared = at.sem("loaded"), at.sem("cleared")
            block = at.block()
            whole = N // P

            @block.vector
            def _(dve):
                nc.vector.memset(x[:, whole:NT, :], 0.0).then_inc(cleared, 1)

            @block.sync
            def _(sp):
                sp.dma_start(x[:, 0:whole, :], by_tile(a["x"][0:whole * P, :])).then_inc(loaded, 16)
                sp.wait_ge(cleared, 1)
                sp.dma_start(x[0:N - whole * P, whole, :], a["x"][whole * P:N, :]).then_inc(loaded, 16)
                sp.wait_ge(loaded, 32)

        def start0(o):
            v, step, tmp = o.v, o.step, o.tmp
            o.norm(x[:], own)
            step(v.tensor_scalar(scale[:], into.count[:], 1.0, None, ALU.max))
            step(v.reciprocal(scale[:], scale[:]))
        node_stage(nc, "start0", k, start0, [(by_tile(table), own)], roots=1)
        sum_over_edges(nc, "sage1_sum", k, by_dst, SRC, table, into.keep, running)
        node_sums(nc, "sage1_mean", running, into.last, into.some, into.crosses, scale, summed)
        linear(nc, "sage1", k, wide, c.sage1, P, c.sage1_bias, tall)

        def hidden0(o):
            v, step, tmp = o.v, o.step, o.tmp
            step(v.tensor_scalar(wide[:], tall[:, :, 0:P], 0.0, None, ALU.max))
        node_stage(nc, "hidden0", k, hidden0)
        linear(nc, "sage2", k, wide, c.sage2, P, c.sage2_bias, tall)

        def own0(o):
            v, step, tmp = o.v, o.step, o.tmp
            step(v.tensor_tensor(x[:], x[:], tall[:, :, D:P], ALU.add))
        node_stage(nc, "own0", k, own0, [(by_tile(table), tall[:, :, 0:D])])
        sum_over_edges(nc, "sage2_sum", k, by_dst, SRC, table, into.keep, running)
        node_sums(nc, "sage2_mean", running, into.last, into.some, into.crosses, scale, summed)

        def start1(o):
            v, step, tmp = o.v, o.step, o.tmp
            step(v.tensor_tensor(x[:], x[:], summed, ALU.add))
            o.norm(x[:], own)
        node_stage(nc, "start1", k, start1, roots=1)
        linear(nc, "tables1", k, wide, c.tables1, 196, c.tables1_bias, tall)
        keys_values, queries = dram("keys_values", (NP, P)), dram("queries", (NP, D + 4))
        node_stage(nc, "store1", k, lambda o: None, [(by_tile(keys_values), tall[:, :, 0:P]), (by_tile(queries), tall[:, :, P:P + D + 4])])
        attention_pass(nc, "attend1", k, by_src, 34, SRC, keys_values, queries, D + 4, outof.far, weighted, FilterFront(c.filter))
        node_averages(nc, "average1", weighted, outof.last, outof.some, summed)
        linear(nc, "value1", k, wide, c.value1, D, c.value1_bias, tall)

        def value1(o):
            v, step, tmp = o.v, o.step, o.tmp
            step(v.tensor_tensor(tmp[:], over(outof.some), each(c.value_bias1), ALU.mult))
            step(v.tensor_tensor(tmp[:], tmp[:], tall[:, :, 0:D], ALU.add))
            step(v.tensor_copy(own, tmp[:]))
        node_stage(nc, "biased1", k, value1)
        shifted_softplus(nc, "soft1", k, own, summed)
        linear(nc, "out1", k, wide, c.out1, D, c.out1_bias, tall)

        def start2(o):
            v, step, tmp = o.v, o.step, o.tmp
            step(v.tensor_tensor(x[:], x[:], tall[:, :, 0:D], ALU.add))
            o.norm(x[:], own)
            step(v.tensor_scalar(o.stat[:], outof.count[:], 1.0, None, ALU.max))
            o.root()
            step(v.reciprocal(o.stat[:], o.stat[:]))
            step(v.tensor_tensor(scale[:], o.stat[:], outof.some[:], ALU.mult))
            step(v.tensor_tensor(tmp[:], own, over(scale), ALU.mult))
            step(v.tensor_copy(own, tmp[:]))
        node_stage(nc, "start2", k, start2, [(by_tile(table), own)], roots=2)
        sum_over_edges(nc, "gcn_sum", k, by_src, DST, table, outof.keep, running)
        node_sums(nc, "gcn_scale", running, outof.last, outof.some, outof.crosses, scale, summed)
        linear(nc, "gcn", k, wide, c.gcn, D, c.gcn_bias, tall)

        def start3(o):
            v, step, tmp = o.v, o.step, o.tmp
            step(v.scalar_tensor_tensor(x[:], tall[:, :, 0:D], 0.0, x[:], ALU.max, ALU.add))
            o.norm(x[:], own)
        node_stage(nc, "start3", k, start3, roots=1)
        linear(nc, "kqv", k, wide, c.kqv, 3 * D, c.kqv_bias, tall)
        mixed, mix_values, mix_queries = sb("mixed", [P, NT, P]), dram("mix_values", (NP, 3 * D)), dram("mix_queries", (NP, D))
        linear(nc, "mix3", k, tall[:, :, 0:P], c.mix3, P, c.mix3_bias, mixed)

        def pack3(o):
            v, step, tmp = o.v, o.step, o.tmp
            step(v.tensor_copy(tall[:, :, 0:D], mixed[:, :, 0:D]))
            step(v.tensor_copy(tmp[:], tall[:, :, P:P + D]))
            step(v.memset(tall[:, :, P:P + D], 1.0))
            step(v.tensor_copy(tall[:, :, D:P], tmp[:]))
        node_stage(nc, "pack3", k, pack3, [(by_tile(mix_values), tall[:, :, 0:3 * D]), (by_tile(mix_queries), mixed[:, :, D:P])])
        attention_pass(nc, "attend3", k, by_dst, 4, DST, mix_values, mix_queries, D, into.far, weighted, MixFront(c.mix))
        node_averages(nc, "average3", weighted, into.last, into.some, summed)

        linear(nc, "out3", k, wide, c.out3, D, c.tables1_bias, tall)

        def finish3(o):
            v, step, tmp = o.v, o.step, o.tmp
            step(v.tensor_tensor(tmp[:], over(into.count), each(c.edge_count_bias), ALU.mult))
            step(v.tensor_tensor(tmp[:], tmp[:], tall[:, :, 0:D], ALU.add))
            step(v.tensor_tensor(tmp[:], tmp[:], own, ALU.add))
            step(v.tensor_scalar(tmp[:], tmp[:], (1.0 + EPS) ** -0.5, None, ALU.mult))
            step(v.tensor_tensor(tmp[:], tmp[:], each(c.gamma), ALU.mult))
            step(v.tensor_tensor(tmp[:], tmp[:], each(c.beta), ALU.add))
            step(v.tensor_tensor(x[:], x[:], tmp[:], ALU.add))
        whole = N // P
        node_stage(nc, "finish3", k, finish3, [(by_tile(out[0:whole * P, :]), x[:, 0:whole, :]), (out[whole * P:N, :], x[0:N - whole * P, whole, :])])


_NAMES = {
    "x": "x", "src": "src", "dst": "dst", "edge_attr_2": "edge_attr_2", "edge_attr_32": "edge_attr_32",
    "W1n": "L0_gnn_W1n", "b1n": "L0_gnn_b1n", "W1r": "L0_gnn_W1r", "Wl1": "L0_gnn_Wl1", "bl1": "L0_gnn_bl1",
    "W2n": "L0_gnn_W2n", "b2n": "L0_gnn_b2n", "W2r": "L0_gnn_W2r", "Wl2": "L0_gnn_Wl2", "bl2": "L0_gnn_bl2",
    "k_wT": "L1_gnn_k_w", "q_w": "L1_gnn_q_w", "v_wT": "L1_gnn_v_w",
    "wkn_w1T": "L1_gnn_wkn_w1", "wkn_b1": "L1_gnn_wkn_b1", "wkn_w2T": "L1_gnn_wkn_w2", "wkn_b2": "L1_gnn_wkn_b2",
    "wkl_w": "L1_gnn_wkl_w", "wkl_b": "L1_gnn_wkl_b",
    "wvn_w1T": "L1_gnn_wvn_w1", "wvn_b1": "L1_gnn_wvn_b1", "wvn_w2T": "L1_gnn_wvn_w2", "wvn_b2": "L1_gnn_wvn_b2",
    "wvl_wT": "L1_gnn_wvl_w", "wvl_b": "L1_gnn_wvl_b",
    "cen_wT": "L1_gnn_cen_w", "cen_b": "L1_gnn_cen_b", "out_wT": "L1_gnn_out_w", "out_b": "L1_gnn_out_b",
    "gcn_w": "L2_gnn_weight", "gcn_b": "L2_gnn_bias",
    "W_kqv": "L3_gnn_W_kqv", "b_kqv": "L3_gnn_b_kqv", "W_edge": "L3_gnn_W_edge", "b_edge": "L3_gnn_b_edge",
    "W_att1": "L3_gnn_W_att1", "b_att1": "L3_gnn_b_att1", "w_att2": "L3_gnn_W_att2", "b_att2": "L3_gnn_b_att2",
    "W_out": "L3_gnn_W_out", "b_out": "L3_gnn_b_out", "gamma": "L3_gnn_bn_gamma", "beta": "L3_gnn_bn_beta",
}


def kernel(**inputs):
    import numpy as np
    import concourse.bacc as bacc
    from concourse.bass_utils import run_bass_kernel_spmd

    nc = bacc.Bacc("TRN2", target_bir_lowering=False, num_devices=1)
    arrays, args = {}, {}
    for short, name in _NAMES.items():
        v = np.asarray(inputs[name])
        if short.endswith("T"):
            v = np.swapaxes(v, -1, -2)
        if short == "w_att2":
            v = v.reshape(-1)
        v = np.ascontiguousarray(v)
        arrays[f"in_{short}"] = v
        args[short] = nc.dram_tensor(f"in_{short}", v.shape, mybir.dt.from_np(v.dtype), kind="ExternalInput").ap()
    out = nc.dram_tensor("out_x", (N, D), F32, kind="ExternalOutput").ap()
    build(nc, args, out)
    return run_bass_kernel_spmd(nc, [arrays], core_ids=[0]).results[0]["out_x"]
```

```python
from contextlib import ExitStack

import concourse.bass as bass
from concourse import mybir

ALU = mybir.AluOpType
ACT = mybir.ActivationFunctionType
F32 = mybir.dt.float32
BF16 = mybir.dt.bfloat16
I32 = mybir.dt.int32
AX = mybir.AxisListType.X

P = 128
N, E = 3125, 53125
NT = -(-N // P)
NP = NT * P
CH = 416
EP = CH * P
HALF = EP // 2
PAD = NP - 1
D = 64
U = 8
G = CH // U
FAR = -1.0e30
LN2 = 0.6931471805599453
EPS = 1e-5

SRC, DST = 0, 1


def done(k):
    return k + 3


def freed(k):
    return k + 1


def flat(ap):
    return ap.rearrange("p a b -> p (a b)")


class Parts:
    pass


class Stage:

    def __init__(self, nc, ctx, name):
        self.nc, self.ctx, self.name, self.sems = nc, ctx, name, []

    def sb(self, name, shape, dt=F32):
        return self.ctx.enter_context(self.nc.sbuf_tensor(f"{self.name}_{name}", shape, dt))

    def ps(self, name, shape, dt=F32):
        return self.ctx.enter_context(self.nc.psum_tensor(f"{self.name}_{name}", shape, dt))

    def sem(self, name):
        self.sems.append(self.ctx.enter_context(self.nc.semaphore(f"{self.name}_{name}")))
        return self.sems[-1]

    def gather_sem(self, name):
        return self.nc.alloc_semaphore(f"{self.name}_{name}")

    def sb2(self, name, shape, dt=F32):
        return [self.sb(f"{name}{b}", shape, dt) for b in range(2)]

    def ps2(self, name, shape, dt=F32):
        return [self.ps(f"{name}{b}", shape, dt) for b in range(2)]

    def sem2(self, name):
        return [self.sem(f"{name}{b}") for b in range(2)]

    def block(self):
        self.ctx.callback(self.clear)
        return self.ctx.enter_context(self.nc.Block())

    def clear(self):
        for s in self.sems:
            self.nc.gpsimd.sem_clear(s)
        self.nc.all_engine_barrier()


class Steps:

    def __init__(self, eng, sem, at=0):
        self.eng, self.sem, self.n = eng, sem, at

    def __call__(self, ins):
        self.n += 1
        ins.then_inc(self.sem, 1)
        self.eng.wait_ge(self.sem, self.n)


def each_group(eng, body):
    with eng.Fori(0, G // 2 - 1) as i:
        for b in range(2):
            body(2 * i + b, b, i, True)
    for b in range(2):
        body(G - 2 + b, b, G // 2 - 1, b == 0)


def two_follow(g):
    return not isinstance(g, int) or g + 2 < G


def make_constants(nc, name, k):
    with ExitStack() as ctx:
        at = Stage(nc, ctx, name)
        col_i = at.sb("col_i", [P, P], I32)
        row_i = at.sb("row_i", [P, P], I32)
        row_f = at.sb("row_f", [P, P])
        iotas = at.sem("iotas")
        made = at.sem("made")
        block = at.block()

        @block.gpsimd
        def _(pool):
            nc.gpsimd.iota(col_i[:], pattern=[[1, P]], base=0, channel_multiplier=0).then_inc(iotas, 1)
            nc.gpsimd.iota(row_i[:], pattern=[[0, P]], base=0, channel_multiplier=1).then_inc(iotas, 1)

        @block.vector
        def _(dve):
            step = Steps(dve, made)
            dve.wait_ge(iotas, 2)
            step(nc.vector.tensor_copy(k.count[:], col_i[:]))
            step(nc.vector.tensor_copy(row_f[:], row_i[:]))
            step(nc.vector.tensor_scalar(k.spare[:], k.count[:, 0:NT], float(P), float(EP), ALU.mult, ALU.add))
            step(nc.vector.tensor_tensor(k.spare[:], k.spare[:], row_f[:, 0:NT], ALU.add))
            step(nc.vector.memset(k.zeros[:], 0.0))
            step(nc.vector.tensor_tensor(k.before[:], row_f[:], k.count[:], ALU.is_lt))
            step(nc.vector.tensor_tensor(k.upto[:], row_f[:], k.count[:], ALU.is_le))
            step(nc.vector.tensor_tensor(k.ident[:], row_f[:], k.count[:], ALU.is_equal))
            step(nc.vector.memset(k.ones[:], 1.0))
            step(nc.vector.tensor_copy(k.ones16[:], k.ones[:]))
            step(nc.vector.tensor_copy(k.ident16[:], k.ident[:]))
            step(nc.vector.tensor_copy(k.lanes16[:], k.count[:]))
            step(nc.vector.tensor_scalar(k.tiles16[:], k.count[:, 0:NT], float(P), None, ALU.mult))
            step(nc.vector.tensor_scalar(k.later16[:], k.before[:], -1.0, -2.0 ** 14, ALU.add, ALU.mult))


def load_edges(nc, name, src, dst, column, width, e):
    per, left = E // P, E % P
    assert per + 1 == CH
    with ExitStack() as ctx:
        at = Stage(nc, ctx, name)
        ends = at.sb("ends", [P, 2, CH], I32)
        lane, tile = at.sb("lane", [P, CH], I32), at.sb("tile", [P, CH], I32)
        loaded, padded, packed, split = at.sem("loaded"), at.sem("padded"), at.sem("packed"), at.sem("split")
        block = at.block()

        @block.vector
        def _(dve):
            nc.vector.memset(ends[:, :, per:CH], PAD).then_inc(padded, 1)
            if e.narrow:
                nc.vector.memset(e.narrow[:, per:CH, :], 0.0)
            else:
                nc.vector.memset(e.rec[:, per:CH, 2:width], 0)
            dve.wait_ge(loaded, 16 * 4)
            key = ends[:, column, :]
            nc.vector.tensor_scalar(lane[:], key, P - 1, None, ALU.bitwise_and).then_inc(split, 1)
            nc.vector.tensor_scalar(tile[:], key, 7, None, ALU.logical_shift_right).then_inc(split, 1)
            nc.vector.tensor_copy(e.key[:], key)
            for c in (SRC, DST):
                nc.vector.tensor_copy(e.rec[:, :, c], ends[:, c, :])
            dve.wait_ge(split, 2)
            nc.vector.tensor_copy(e.lane16[:], lane[:])
            nc.vector.tensor_scalar(e.tile16[:], tile[:], float(P), None, ALU.mult)

        @block.sync
        def _(sp):
            sp.wait_ge(padded, 1)
            for c, ap in ((SRC, src), (DST, dst)):
                sp.dma_start(ends[:, c, 0:per], ap[0:per * P].rearrange("(p j) -> p j", p=P)).then_inc(loaded, 16)
                sp.dma_start(ends[0:left, c, per:CH], ap[per * P:E].rearrange("(p j) -> p j", j=1)).then_inc(loaded, 16)


def load_features(eng, attr, width, e):
    per, left, f = E // P, E % P, width - 2
    a = attr.rearrange("e f -> (e f)")
    rec = e.narrow[:] if e.narrow else e.rec[:, :, 2:width].bitcast(F32)
    eng.dma_start(rec[:, 0:per, :], a[0:per * P * f].rearrange("(p j f) -> p j f", p=P, f=f)).then_inc(e.features_in, 16)
    eng.dma_start(rec[0:left, per:CH, :], a[per * P * f:E * f].rearrange("(p j f) -> p j f", p=left, f=f)).then_inc(e.features_in, 16)


class Counting:

    def __init__(self, at, nc, k, e, r):
        self.nc, self.k, self.e, self.r = nc, k, e, r
        self.lanes, self.tiles = at.sb2("counted_lanes", [P, U, P], BF16), at.sb2("counted_tiles", [P, U, NT], BF16)
        self.count_ps = at.ps("count_ps", [P, 512])
        self.tiles_hot, self.hot, self.counted = at.sem("counted_tiles_hot"), at.sem("counted_hot"), at.sem("counted")

    def dve_start(self, dve):
        dve.sem_inc(self.hot, 2)

    def dve(self, dve, g, b):
        nc, k, e = self.nc, self.k, self.e
        dve.wait_ge(self.counted, freed(g))
        nc.vector.tensor_tensor(self.tiles[b][:], e.tile16[:, bass.ds(g * U, U)].unsqueeze(2).to_broadcast([P, U, NT]),
                                k.tiles16[:].unsqueeze(1).to_broadcast([P, U, NT]), ALU.is_equal).then_inc(self.tiles_hot, 1)
        nc.vector.tensor_tensor(self.lanes[b][:], e.lane16[:, bass.ds(g * U, U)].unsqueeze(2).to_broadcast([P, U, P]),
                                k.lanes16[:].unsqueeze(1).to_broadcast([P, U, P]), ALU.is_equal).then_inc(self.hot, 1)

    def dve_end(self, dve):
        dve.wait_ge(self.counted, done(G - 1))
        self.nc.vector.tensor_copy(self.r.count[:], self.count_ps[:, 0:NT])

    def pe_start(self, pe):
        pe.sem_inc(self.counted, 2)
        self.nc.tensor.matmul(self.count_ps[:, 0:NT], self.k.ones[:], self.k.zeros[:, 0:NT], start=True, stop=True, skip_group_check=True)

    def pe(self, pe, g, b):
        pe.wait_ge(self.tiles_hot, g + 1)
        pe.wait_ge(self.hot, done(g))
        for u in range(U):
            last = self.nc.tensor.matmul(self.count_ps[:, 0:NT], self.lanes[b][:, u, :], self.tiles[b][:, u, :], start=False, stop=True, skip_group_check=True)
        last.then_inc(self.counted, 1)


def count_edges(nc, name, k, e, r, sync_beside, scalar_beside):
    with ExitStack() as ctx:
        at = Stage(nc, ctx, name)
        counting = Counting(at, nc, k, e, r)
        block = at.block()

        @block.sync
        def _(sp):
            sync_beside(sp)

        @block.scalar
        def _(act):
            scalar_beside(act)

        @block.vector
        def _(dve):
            counting.dve_start(dve)
            with dve.Fori(0, G // 2) as i:
                for b in range(2):
                    counting.dve(dve, 2 * i + b, b)
            counting.dve_end(dve)

        @block.tensor
        def _(pe):
            counting.pe_start(pe)
            with pe.Fori(0, G // 2) as i:
                for b in range(2):
                    counting.pe(pe, 2 * i + b, b)


def place_nodes(nc, name, k, r):
    with ExitStack() as ctx:
        at = Stage(nc, ctx, name)
        tile_upto, ends, starts = at.sb("tile_upto", [P, NT]), at.sb("node_ends", [P, NT]), at.sb("node_starts", [P, NT])
        ends_ps, sums_ps = at.ps("ends_ps", [P, 512]), at.ps("sums_ps", [P, 512])
        summed, stepped = at.sem("summed"), at.sem("stepped")
        block = at.block()

        @block.vector
        def _(dve):
            step = Steps(dve, stepped)
            dve.wait_ge(summed, 2)
            step(nc.vector.tensor_tensor_scan(tile_upto[:], sums_ps[:, 0:NT], k.zeros[:, 0:NT], 0.0, ALU.add, ALU.add))
            step(nc.vector.tensor_tensor(ends[:], tile_upto[:], sums_ps[:, 0:NT], ALU.subtract))
            step(nc.vector.tensor_tensor(ends[:], ends[:], ends_ps[:, 0:NT], ALU.add))
            step(nc.vector.tensor_tensor(starts[:], ends[:], r.count[:], ALU.subtract))
            step(nc.vector.tensor_copy(r.place[:], starts[:]))
            step(nc.vector.tensor_scalar(r.some[:], r.count[:], 1.0, None, ALU.min))
            step(nc.vector.tensor_tensor(tile_upto[:], starts[:], k.spare[:], ALU.subtract))
            step(nc.vector.tensor_tensor(tile_upto[:], tile_upto[:], r.some[:], ALU.mult))
            step(nc.vector.tensor_tensor(r.first[:], tile_upto[:], k.spare[:], ALU.add))
            step(nc.vector.tensor_scalar(r.last[:], ends[:], -1.0, 0.0, ALU.add, ALU.max))
            step(nc.vector.tensor_scalar(starts[:], starts[:], float(HALF), None, ALU.is_lt))
            step(nc.vector.tensor_scalar(ends[:], ends[:], float(HALF), None, ALU.is_gt))
            step(nc.vector.tensor_tensor(r.crosses[:], starts[:], ends[:], ALU.mult))

        @block.tensor
        def _(pe):
            nc.tensor.matmul(ends_ps[:, 0:NT], k.upto[:], r.count[:], start=True, stop=True).then_inc(summed, 1)
            nc.tensor.matmul(sums_ps[:, 0:NT], k.ones[:], r.count[:], start=True, stop=True).then_inc(summed, 1)


def move_edges(nc, name, k, e, width, r, out, other=None):
    T = NT
    with ExitStack() as ctx:
        at = Stage(nc, ctx, name)
        rec = at.sb2("rec", [P, U, width], I32)
        digits = at.sb2("digits", [P, 2, U], BF16)
        lanes, tiles = at.sb2("lanes", [P, U, P], BF16), at.sb2("tiles", [P, U, T], BF16)
        turned = at.sb2("turned", [P, U, P], BF16)
        base, base_high, base_rest = at.sb("base", [P, U, T]), at.sb2("base_high", [P, U, T], BF16), at.sb2("base_rest", [P, U, T], BF16)
        same, picked = at.sb2("same", [P, U, P], BF16), at.sb("picked", [P, U, T])
        place = at.sb2("place", [P, U], I32)
        gate = at.sb("gate", [P, 2])
        before_ps, look_ps = at.ps2("before_ps", [P, 512]), at.ps2("look_ps", [P, 512])
        turn_ps, key_ps = at.ps("turn_ps", [P, U, P], BF16), at.ps("key_ps", [P, U, P])
        moved = [at.gather_sem(f"moved{b}") for b in range(2)]
        tiles_hot, hot, held, grouped, turned_in = at.sem("tiles_hot"), at.sem("hot"), at.sem("held"), at.sem("grouped"), at.sem("turned_in")
        based, advanced, compared, looked, picks, placed = (
            at.sem("based"), at.sem("advanced"), at.sem("compared"), at.sem("looked"), at.sem("picks"), at.sem("placed"))
        gated, sent, rec_in, lanes_turned, rounded = at.sem("gated"), at.sem("sent"), at.sem("rec_in"), at.sem("lanes_turned"), at.sem("rounded")
        counting = Counting(at, nc, k, other.e, other.r) if other else None
        block = at.block()
        before = lambda b: before_ps[b][:, 0:U * T].rearrange("p (u t) -> p u t", u=U)
        look = lambda b: look_ps[b][:, 0:U * T].rearrange("p (u t) -> p u t", u=U)

        @block.sync
        def _(sp):
            sp.sem_inc(sent, 2)
            with sp.Fori(0, G // 2) as i:
                for b in range(2):
                    sp.wait_ge(moved[b], 16 * U * (i + 1))
                    sp.sem_inc(sent, 1)

        @block.scalar
        def _(act):
            def hold_digits(g, b):
                nc.scalar.copy(digits[b][:, 0, :], e.lane16[:, bass.ds(g * U, U)]).then_inc(held, 1)
                nc.scalar.copy(digits[b][:, 1, :], e.tile16[:, bass.ds(g * U, U)]).then_inc(held, 1)

            act.sem_inc(turned_in, 2)
            act.wait_ge(e.features_in, 32)
            hold_digits(0, 0)

            def body(g, b, i, more):
                act.wait_ge(looked, freed(g))
                act.wait_ge(lanes_turned, g + 1)
                nc.scalar.copy(turned[b][:], turn_ps[:]).then_inc(turned_in, 1)
                if more:
                    act.wait_ge(grouped, done(g - 1))
                    hold_digits(g + 1, 1 - b)
                act.wait_ge(sent, freed(g))
                nc.scalar.copy(rec[b][:].bitcast(F32), e.rec[:, bass.ds(g * U, U), :].bitcast(F32)).then_inc(rec_in, 1)

            each_group(act, body)

        @block.tensor
        def _(pe):
            def group(g, b):
                pe.wait_ge(advanced, freed(g))
                pe.wait_ge(tiles_hot, g + 1)
                pe.wait_ge(hot, done(g))
                pe.wait_ge(turned_in, done(g - 1))
                for u in range(U):
                    last = nc.tensor.transpose(turn_ps[:, u, :], lanes[b][:, u, :], k.ident16[:])
                last.then_inc(lanes_turned, 1)
                for u in range(1, U):
                    for earlier in range(u):
                        nc.tensor.matmul(before(b)[:, u, :], lanes[b][:, earlier, :], tiles[b][:, earlier, :], start=(earlier == 0), stop=(earlier == u - 1))
                for u in range(U):
                    nc.tensor.matmul(before(b)[:, 0, :], lanes[b][:, u, :], tiles[b][:, u, :], start=(u == 0), stop=(u == U - 1))
                pe.wait_ge(compared, done(g - 1))
                pe.wait_ge(held, 2 * g + 2)
                for h in range(2):
                    nc.tensor.matmul(flat(key_ps[:, 4 * h:4 * h + 4, :]), k.ident16[:], k.later16[:].unsqueeze(1).to_broadcast([P, 4, P]),
                                     start=True, stop=True, skip_group_check=True)
                    for u in range(4 * h, 4 * h + 4):
                        for d in range(2):
                            last = nc.tensor.matmul(key_ps[:, u, :], digits[b][:, d, u:u + 1].to_broadcast([P, P]), k.ident16[:],
                                                    start=False, stop=True, skip_group_check=True)
                last.then_inc(grouped, 1)

            pe.sem_inc(grouped, 2)
            pe.sem_inc(looked, 2)
            if counting:
                counting.pe_start(pe)
            group(0, 0)

            def body(g, b, i, more):
                pe.wait_ge(placed, freed(g))
                pe.wait_ge(turned_in, done(g))
                pe.wait_ge(compared, done(g))
                pe.wait_ge(rounded, 2 * g + 2)
                for u in range(U):
                    nc.tensor.matmul(look(b)[:, u, :], turned[b][:, u, :], base_high[b][:, u, :], start=True, stop=False)
                    nc.tensor.matmul(look(b)[:, u, :], turned[b][:, u, :], base_rest[b][:, u, :], start=False, stop=False)
                    last = nc.tensor.matmul(look(b)[:, u, :], same[b][:, u, :], k.ones16[:, 0:T], start=False, stop=True)
                last.then_inc(looked, 1)
                if more:
                    group(g + 1, 1 - b)
                if counting:
                    counting.pe(pe, g, b)

            each_group(pe, body)

        @block.vector
        def _(dve):
            def one_hots(g, b):
                dve.wait_ge(placed, freed(g))
                nc.vector.tensor_tensor(tiles[b][:], e.tile16[:, bass.ds(g * U, U)].unsqueeze(2).to_broadcast([P, U, T]),
                                        k.tiles16[:].unsqueeze(1).to_broadcast([P, U, T]), ALU.is_equal).then_inc(tiles_hot, 1)
                nc.vector.tensor_tensor(lanes[b][:], e.lane16[:, bass.ds(g * U, U)].unsqueeze(2).to_broadcast([P, U, P]),
                                        k.lanes16[:].unsqueeze(1).to_broadcast([P, U, P]), ALU.is_equal).then_inc(hot, 1)

            for s in (hot, based, advanced, compared, picks, placed):
                dve.sem_inc(s, 2)
            if counting:
                counting.dve_start(dve)
            one_hots(0, 0)

            def body(g, b, i, more):
                dve.wait_ge(grouped, done(g))
                dve.wait_ge(advanced, done(g - 1))
                dve.wait_ge(looked, freed(g))
                nc.vector.tensor_tensor(base[:, 1:U, :], before(b)[:, 1:U, :], r.place[:].unsqueeze(1).to_broadcast([P, U - 1, T]), ALU.add).then_inc(based, 1)
                nc.vector.tensor_copy(base[:, 0, :], r.place[:]).then_inc(based, 1)
                nc.vector.tensor_tensor(same[b][:], key_ps[:], e.key[:, bass.ds(g * U, U)].unsqueeze(2).to_broadcast([P, U, P]), ALU.is_equal).then_inc(compared, 1)
                dve.wait_ge(based, 2 * g + 4)
                nc.vector.tensor_copy(base_high[b][:], base[:]).then_inc(rounded, 1)
                dve.wait_ge(rounded, 2 * g + 1)
                nc.vector.tensor_tensor(base_rest[b][:], base[:], base_high[b][:], ALU.subtract).then_inc(rounded, 1)
                nc.vector.tensor_tensor(r.place[:], r.place[:], before(b)[:, 0, :], ALU.add).then_inc(advanced, 1)
                if more:
                    one_hots(g + 1, 1 - b)
                dve.wait_ge(looked, done(g))
                dve.wait_ge(tiles_hot, g + 1)
                dve.wait_ge(placed, done(g - 1))
                nc.vector.tensor_tensor(picked[:], look(b), tiles[b][:], ALU.mult).then_inc(picks, 1)
                dve.wait_ge(picks, done(g))
                dve.wait_ge(sent, freed(g))
                with nc.allow_low_precision(reason="whole numbers below 2**24 sum in float32 and land as integers"):
                    nc.vector.tensor_reduce(place[b][:], picked[:], AX, ALU.add).then_inc(placed, 1)
                if counting:
                    counting.dve(dve, g, b)

            each_group(dve, body)
            if counting:
                counting.dve_end(dve)

        @block.gpsimd
        def _(pool):
            nc.gpsimd.memset(gate[:], 0.0).then_inc(gated, 1)
            with pool.Fori(0, G // 2) as i:
                for b in range(2):
                    g = 2 * i + b
                    pool.wait_ge(gated, g + 1)
                    pool.wait_ge(rec_in, g + 1)
                    pool.wait_ge(placed, done(g))
                    nc.gpsimd.tensor_tensor(gate[:, 0:1], gate[:, 1:2], gate[:, 1:2], ALU.add).then_inc(gated, 1)
                    for u in range(U):
                        nc.gpsimd.indirect_dma_start(out=out, out_offset=bass.IndirectOffsetOnAxis(ap=place[b][:, u:u + 1], axis=0),
                                                     in_=rec[b][:, u, :], in_offset=None).then_inc(moved[b], 16)


def mark_segments(nc, name, record, column, width, keep_row, far_row):
    with ExitStack() as ctx:
        at = Stage(nc, ctx, name)
        here, keep, far = at.sb("here", [P, CH, width], I32), at.sb("keep", [P, CH]), at.sb("far", [P, CH])
        prior = at.sb("prior", [P, 2], I32)
        loaded, cleared, marked, fars, stored = at.sem("loaded"), at.sem("cleared"), at.sem("marked"), at.sem("fars"), at.sem("stored")
        block = at.block()

        @block.sync
        def _(sp):
            sp.dma_start(here[:], record.rearrange("(p j) w -> p j w", p=P)).then_inc(loaded, 16)
            sp.wait_ge(cleared, 1)
            sp.dma_start(prior[1:P, :], record.rearrange("(p j) w -> p j w", p=P)[0:P - 1, CH - 1, 0:2]).then_inc(loaded, 16)
            sp.wait_ge(fars, 1)
            sp.dma_start(keep_row.rearrange("(p j) -> p j", p=P), keep[:]).then_inc(stored, 16)
            sp.dma_start(far_row.rearrange("(p j) -> p j", p=P), far[:]).then_inc(stored, 16)
            sp.wait_ge(stored, 32)

        @block.vector
        def _(dve):
            nc.vector.memset(prior[:], -1).then_inc(cleared, 1)
            dve.wait_ge(loaded, 32)
            nc.vector.tensor_tensor(keep[:, 1:CH], here[:, 1:CH, column], here[:, 0:CH - 1, column], ALU.is_equal).then_inc(marked, 1)
            nc.vector.tensor_tensor(keep[:, 0:1], here[:, 0:1, column], prior[:, column:column + 1], ALU.is_equal).then_inc(marked, 1)
            dve.wait_ge(marked, 2)
            nc.vector.tensor_scalar(far[:], keep[:], -1.0, -FAR, ALU.add, ALU.mult).then_inc(fars, 1)


def order_edges(nc, k, names, src, dst, attrs, columns, widths, known, outs, sync_beside, scalar_beside):
    with ExitStack() as ctx:
        edges = []
        for name, attr, column, width, r in zip(names, attrs, columns, widths, known):
            at = Stage(nc, ctx, name)
            e = Parts()
            e.rec, e.key = at.sb("all_rec", [P, CH, width], I32), at.sb("all_key", [P, CH])
            e.lane16, e.tile16 = at.sb("all_lane", [P, CH], BF16), at.sb("all_tile", [P, CH], BF16)
            e.features_in = at.gather_sem("features_in")
            e.narrow = at.sb("narrow", [P, CH, width - 2]) if width < 16 else None
            load_edges(nc, f"{name}_load", src, dst, column, width, e)
            other = Parts()
            other.e, other.r = e, r
            edges.append(other)

        def transfers(sp):
            load_features(sp, attrs[0], widths[0], edges[0].e)
            sync_beside(sp)
            load_features(sp, attrs[1], widths[1], edges[1].e)

        def copies(act):
            scalar_beside(act)
            for edge, width in zip(edges, widths):
                if edge.e.narrow:
                    act.wait_ge(edge.e.features_in, 32)
                    nc.scalar.copy(edge.e.rec[:, :, 2:width].bitcast(F32), edge.e.narrow[:])

        count_edges(nc, f"{names[0]}_count", k, edges[0].e, known[0], transfers, copies)
        for o, other in ((0, edges[1]), (1, None)):
            place_nodes(nc, f"{names[o]}_place", k, known[o])
            move_edges(nc, f"{names[o]}_move", k, edges[o].e, widths[o], known[o], outs[o], other)
    for o in range(2):
        mark_segments(nc, f"{names[o]}_mark", outs[o], columns[o], widths[o], known[o].keep, known[o].far)


def sum_over_edges(nc, name, k, record, ends, table, keep_row, running):
    Q = U // 2
    with ExitStack() as ctx:
        at = Stage(nc, ctx, name)
        rec = at.sb2("rec", [P, 2, Q, 2], I32)
        keep = at.sb2("keep", [P, Q * P])
        rows = at.sb2("rows", [P, Q, 2, D])
        run = at.sb2("run", [P, Q * P])
        back = at.sb2("back", [P, Q, 2, D])
        gate = at.sb("gate", [P, 2])
        rows_ps, back_ps = at.ps2("rows_ps", [P, Q, P]), at.ps2("back_ps", [P, Q, P])
        rec_in, keep_in, gathered, stored = at.sem2("rec_in"), at.sem2("keep_in"), [at.gather_sem(f"gathered{b}") for b in range(2)], at.sem("stored")
        turned, scanned, returned, copied, sent = at.sem("turned"), at.sem("scanned"), at.sem("returned"), at.sem("copied"), at.sem("sent")
        cleared, gated = at.sem("cleared"), at.sem("gated")
        block = at.block()
        records = record.rearrange("(s c p) w -> s p c w", s=2, p=P)
        runs = running.rearrange("(s c p) f -> s p c f", s=2, p=P)

        def load_records(sp, g, b):
            for s in range(2):
                sp.dma_start(rec[b][:, s, :, :], records[s][:, bass.ds(g * Q, Q), 0:2]).then_inc(rec_in[b], 16)

        def load_keep(sp, g, b):
            for s in range(2):
                row = keep_row[s * HALF:(s + 1) * HALF].rearrange("(o e) -> o e", o=1)[:, bass.ds(g * Q * P, Q * P)]
                sp.dma_start(keep[b][s * D:(s + 1) * D, :], row.to_broadcast([D, Q * P])).then_inc(keep_in[b], 16)

        def store(sp, g, b):
            sp.wait_ge(copied, done(g))
            for s in range(2):
                sp.dma_start(runs[s][:, bass.ds(g * Q, Q), :], back[b][:, :, s, :]).then_inc(stored, 16)
            sp.wait_ge(stored, 32 * (g + 1))
            sp.sem_inc(sent, 1)

        @block.sync
        def _(sp):
            sp.sem_inc(sent, 2)
            for b in range(2):
                load_records(sp, b, b)
                load_keep(sp, b, b)
            with sp.Fori(0, G // 2 - 1) as i:
                for b in range(2):
                    g = 2 * i + b
                    sp.wait_ge(gathered[b], 16 * U * (i + 1))
                    load_records(sp, g + 2, b)
                    sp.wait_ge(scanned, done(g))
                    load_keep(sp, g + 2, b)
                    store(sp, g, b)
            for b in range(2):
                store(sp, G - 2 + b, b)

        @block.gpsimd
        def _(pool):
            nc.gpsimd.memset(gate[:], 0.0).then_inc(gated, 1)
            with pool.Fori(0, G // 2) as i:
                for b in range(2):
                    g = 2 * i + b
                    pool.wait_ge(gated, g + 1)
                    pool.wait_ge(turned, freed(g))
                    pool.wait_ge(rec_in[b], 32 * (i + 1))
                    nc.gpsimd.tensor_tensor(gate[:, 0:1], gate[:, 1:2], gate[:, 1:2], ALU.add).then_inc(gated, 1)
                    for u in range(Q):
                        for s in range(2):
                            nc.gpsimd.indirect_dma_start(out=rows[b][:, u, s, :], out_offset=None, in_=table,
                                                         in_offset=bass.IndirectOffsetOnAxis(ap=rec[b][:, s, u, ends:ends + 1], axis=0)).then_inc(gathered[b], 16)

        @block.tensor
        def _(pe):
            pe.sem_inc(turned, 2)
            pe.sem_inc(returned, 2)
            with pe.Fori(0, G // 2) as i:
                for b in range(2):
                    g = 2 * i + b
                    pe.wait_ge(scanned, freed(g))
                    pe.wait_ge(gathered[b], 16 * U * (i + 1))
                    for u in range(Q):
                        last = nc.tensor.transpose(rows_ps[b][:, u, :], flat(rows[b][:, u, :, :]), k.ident[:])
                    last.then_inc(turned, 1)
                    pe.wait_ge(copied, freed(g))
                    pe.wait_ge(scanned, done(g))
                    for u in range(Q):
                        last = nc.tensor.transpose(back_ps[b][:, u, :], run[b][:, u * P:(u + 1) * P], k.ident[:])
                    last.then_inc(returned, 1)

        @block.vector
        def _(dve):
            nc.vector.memset(run[1][:], 0.0).then_inc(cleared, 1)
            dve.wait_ge(cleared, 1)
            dve.sem_inc(scanned, 2)
            with dve.Fori(0, G // 2) as i:
                for b in range(2):
                    g = 2 * i + b
                    dve.wait_ge(keep_in[b], 32 * (i + 1))
                    dve.wait_ge(returned, freed(g))
                    dve.wait_ge(scanned, done(g - 1))
                    dve.wait_ge(turned, done(g))
                    nc.vector.tensor_tensor_scan(run[b][:], keep[b][:], flat(rows_ps[b][:]), run[1 - b][:, Q * P - 1:Q * P],
                                                 ALU.mult, ALU.add).then_inc(scanned, 1)

        @block.scalar
        def _(act):
            act.sem_inc(copied, 2)
            with act.Fori(0, G // 2) as i:
                for b in range(2):
                    g = 2 * i + b
                    act.wait_ge(sent, freed(g))
                    act.wait_ge(returned, done(g))
                    nc.scalar.copy(back[b][:].rearrange("p a s f -> p (a s f)"), flat(back_ps[b][:])).then_inc(copied, 1)


def rows_at_last_edges(nc, name, running, last_edge, out):
    with ExitStack() as ctx:
        at = Stage(nc, ctx, name)
        gathered = at.gather_sem("gathered")
        block = at.block()

        @block.gpsimd
        def _(pool):
            for t in range(NT):
                nc.gpsimd.indirect_dma_start(out=out[:, t, :], out_offset=None, in_=running,
                                             in_offset=bass.IndirectOffsetOnAxis(ap=last_edge[:, t:t + 1], axis=0)).then_inc(gathered, 16)
            pool.wait_ge(gathered, 16 * NT)


def rows_to_first_edges(nc, name, rows, first_edge, cleared, clears, starts):
    with ExitStack() as ctx:
        at = Stage(nc, ctx, name)
        scattered = at.gather_sem("scattered")
        block = at.block()

        @block.gpsimd
        def _(pool):
            pool.wait_ge(cleared, clears)
            for t in range(NT):
                nc.gpsimd.indirect_dma_start(out=starts, out_offset=bass.IndirectOffsetOnAxis(ap=first_edge[:, t:t + 1], axis=0),
                                             in_=rows[:, t, :], in_offset=None).then_inc(scattered, 16)
            pool.wait_ge(scattered, 16 * NT)


def node_sums(nc, name, running, last_edge, has_edges, crosses, scale, out):
    with ExitStack() as ctx:
        at = Stage(nc, ctx, name)
        sums, middle, part = at.sb("sums", [P, NT, D]), at.sb("middle", [P, D]), at.sb("part", [P, NT, D])
        rows_at_last_edges(nc, f"{name}_ends", running, last_edge, sums)
        loaded, stepped = at.sem("loaded"), at.sem("stepped")
        block = at.block()
        wide = lambda col: col[:].unsqueeze(2).to_broadcast([P, NT, D])

        @block.sync
        def _(sp):
            sp.dma_start(middle[:], running[HALF - 1:HALF, :].to_broadcast([P, D])).then_inc(loaded, 16)

        @block.vector
        def _(dve):
            step = Steps(dve, stepped)
            dve.wait_ge(loaded, 16)
            step(nc.vector.tensor_tensor(part[:], middle[:].unsqueeze(1).to_broadcast([P, NT, D]), wide(crosses), ALU.mult))
            step(nc.vector.tensor_tensor(sums[:], sums[:], part[:], ALU.add))
            step(nc.vector.tensor_tensor(sums[:], sums[:], wide(has_edges), ALU.mult))
            step(nc.vector.tensor_tensor(out, sums[:], wide(scale), ALU.mult))


def node_averages(nc, name, running, last_edge, has_edges, out):
    with ExitStack() as ctx:
        at = Stage(nc, ctx, name)
        sums, part = at.sb("sums", [P, NT, 2 * D]), at.sb("part", [P, NT, D])
        rows_at_last_edges(nc, f"{name}_ends", running, last_edge, sums)
        stepped = at.sem("stepped")
        block = at.block()

        @block.vector
        def _(dve):
            step = Steps(dve, stepped)
            step(nc.vector.reciprocal(part[:], sums[:, :, 0:D]))
            step(nc.vector.tensor_tensor(part[:], part[:], has_edges[:].unsqueeze(2).to_broadcast([P, NT, D]), ALU.mult))
            step(nc.vector.tensor_tensor(out, sums[:, :, D:2 * D], part[:], ALU.mult))


def linear(nc, name, k, rows, weights, width, bias, out):
    B = 5
    with ExitStack() as ctx:
        at = Stage(nc, ctx, name)
        held, turned_rows = at.sb("held", [P, B, P]), at.sb("turned_rows", [P, B, P])
        turn_ps, out_ps = at.ps("turn_ps", [P, 8, P]), at.ps("out_ps", [P, 6, 256])
        in_hand, turned, copied, multiplied, added = at.sem("in_hand"), at.sem("turned"), at.sem("copied"), at.sem("multiplied"), at.sem("added")
        block = at.block()

        @block.tensor
        def _(pe):
            pe.sem_inc(turned, 1)
            pe.sem_inc(multiplied, 1)
            with pe.Fori(0, NT // B) as j:
                pe.wait_ge(copied, j + 1)
                pe.wait_ge(in_hand, j + 1)
                for t in range(B):
                    last = nc.tensor.transpose(turn_ps[:, t, :], held[:, t, :], k.ident[:])
                last.then_inc(turned, 1)
                pe.wait_ge(added, j + 1)
                pe.wait_ge(copied, j + 2)
                for t in range(B):
                    last = nc.tensor.matmul(out_ps[:, t, 0:width], turned_rows[:, t, :], weights[:, 0:width], start=True, stop=True)
                last.then_inc(multiplied, 1)

        @block.scalar
        def _(act):
            act.sem_inc(copied, 1)
            with act.Fori(0, NT // B) as j:
                act.wait_ge(turned, j + 1)
                nc.scalar.copy(held[:], rows[:, bass.ds(B * j, B), :]).then_inc(in_hand, 1)
                act.wait_ge(multiplied, j + 1)
                act.wait_ge(turned, j + 2)
                nc.scalar.copy(flat(turned_rows[:]), flat(turn_ps[:, 0:B, :])).then_inc(copied, 1)

        @block.vector
        def _(dve):
            dve.sem_inc(added, 1)
            with dve.Fori(0, NT // B) as j:
                dve.wait_ge(multiplied, j + 2)
                nc.vector.tensor_tensor(out[:, bass.ds(B * j, B), 0:width], out_ps[:, 0:B, 0:width],
                                        bias[:, 0:width].unsqueeze(1).to_broadcast([P, B, width]), ALU.add).then_inc(added, 1)


def layer_norm(nc, step, root, x, out, centred, squares, stat):
    v = nc.vector
    wide = lambda: stat[:].unsqueeze(2).to_broadcast([P, NT, D])
    step(v.tensor_reduce(stat[:], x, AX, ALU.add))
    step(v.tensor_scalar(stat[:], stat[:], 1.0 / D, None, ALU.mult))
    step(v.tensor_tensor(centred[:], x, wide(), ALU.subtract))
    step(v.tensor_tensor(squares[:], centred[:], centred[:], ALU.mult))
    step(v.tensor_reduce(stat[:], squares[:], AX, ALU.add))
    step(v.tensor_scalar(stat[:], stat[:], 1.0 / D, EPS, ALU.mult, ALU.add))
    root()
    step(v.reciprocal(stat[:], stat[:]))
    step(v.tensor_tensor(centred[:], centred[:], wide(), ALU.mult))
    step(v.tensor_scalar(out, centred[:], 0.0, None, ALU.max))


def attention_pass(nc, name, k, record, width, far_end, table, starts, near_width, keep_row, far_row, running, front):
    L, Q = U * P, U // 2
    M = Q * P
    W = near_width
    with ExitStack() as ctx:
        at = Stage(nc, ctx, name)
        w = Parts()
        w.at, w.nc, w.k, w.Q, w.M = at, nc, k, Q, M
        w.rec = at.sb2("rec", [P, U, width], I32)
        w.far_rows = at.sb2("far_rows", [P, U, P])
        near_rows = at.sb2("near_rows", [P, U, D + 4])
        w.terms = at.sb("terms", [P, L])
        carry = at.sb("carry", [P, 1])
        w.rows_ps = at.ps2("rows_ps", [P, Q, P])
        near_ps, logits_ps = at.ps("near_ps", [P, Q, P]), at.ps("logits_ps", [P, U, P])
        back_ps = at.ps("back_ps", [P, Q, P])
        keep, far = at.sb2("keep", [W, L]), at.sb2("far", [P, L])
        top = at.sb2("top", [P, 1 + L])
        fade = at.sb("fade", [P, 2, L])
        faded_top = at.sb("faded_top", [P, L])
        run = at.sb2("run", [P, L])
        back = at.sb2("back", [P, U, P])
        gate = at.sb("gate", [P, 2])
        w.rec_in, near_in, keep_in, far_in = at.sem2("rec_in"), at.sem2("near_in"), at.sem2("keep_in"), at.sem2("far_in")
        w.gathered, stored = [at.gather_sem(f"gathered{b}") for b in range(2)], at.sem2("stored")
        w.rec_used, gated, cleared = at.sem("rec_used"), at.sem("gated"), at.sem("cleared")
        near_turned, w.rows_turned, w.rows_read, filled, carried = (
            at.sem("near_turned"), at.sem("rows_turned"), at.sem("rows_read"), at.sem("filled"), at.sem("carried"))
        w.terms_made, logits_made, sized = at.sem("terms_made"), at.sem("logits_made"), at.sem("sized")
        topped, exponents, factors = at.sem("topped"), at.sem("exponents"), at.sem("factors")
        w.weighted, scanned, returned, copied = at.sem("weighted"), at.sem("scanned"), at.sem("returned"), at.sem("copied")
        front.buffers(w)
        block = at.block()
        records = record.rearrange("(c p) w -> p c w", p=P)
        firsts = starts[0:EP, :].rearrange("(c p) w -> p c w", p=P)
        runs = running.rearrange("(c p) f -> p c f", p=P)
        row = lambda r, g, n: r.rearrange("(o e) -> o e", o=1)[:, bass.ds(g * L, L)].to_broadcast([n, L])

        @block.sync
        def _(sp):
            def load(g, b):
                sp.dma_start(w.rec[b][:], records[:, bass.ds(g * U, U), :]).then_inc(w.rec_in[b], 16)

            def load_near(g, b):
                sp.dma_start(near_rows[b][:, :, 0:W], firsts[:, bass.ds(g * U, U), :]).then_inc(near_in[b], 16)

            def load_keep(g, b):
                sp.dma_start(keep[b][:], row(keep_row, g, W)).then_inc(keep_in[b], 16)

            def load_far(g, b):
                sp.dma_start(far[b][:], row(far_row, g, P)).then_inc(far_in[b], 16)

            sp.wait_ge(cleared, 6)
            for b in range(2):
                load(b, b)
                load_near(b, b)
                load_keep(b, b)
                load_far(b, b)

            def store(g, b):
                sp.wait_ge(copied, 2 * g + 3)
                sp.dma_start(runs[:, bass.ds((g - 1) * U, U), :], back[1 - b][:]).then_inc(stored[1 - b], 16)

            def body(g, b, i, after, more):
                if more:
                    sp.wait_ge(w.rec_used, done(g))
                    sp.wait_ge(w.gathered[b], 16 * U * (i + 1))
                    load(g + 2, b)
                if after:
                    store(g, b)
                if more:
                    sp.wait_ge(near_turned, 2 * g + 2)
                    load_near(g + 2, b)
                    sp.wait_ge(filled, 2 * g + 3)
                    load_keep(g + 2, b)
                    sp.wait_ge(exponents, done(g))
                    load_far(g + 2, b)

            for g in range(2):
                body(g, g, 0, g > 0, True)
            with sp.Fori(1, G // 2 - 1) as i:
                for b in range(2):
                    body(2 * i + b, b, i, True, True)
            for b in range(2):
                body(G - 2 + b, b, G // 2 - 1, True, False)
            store(G, 0)
            for b in range(2):
                sp.wait_ge(stored[b], 16 * (G // 2 + 1 + b))

        @block.gpsimd
        def _(pool):
            nc.gpsimd.memset(gate[:], 0.0).then_inc(gated, 1)
            with pool.Fori(0, G // 2) as i:
                for b in range(2):
                    g = 2 * i + b
                    pool.wait_ge(gated, g + 1)
                    pool.wait_ge(w.rows_turned, 2 * g + 2)
                    pool.wait_ge(w.rec_in[b], 16 * (i + 1))
                    nc.gpsimd.tensor_tensor(gate[:, 0:1], gate[:, 1:2], gate[:, 1:2], ALU.add).then_inc(gated, 1)
                    for u in range(U):
                        nc.gpsimd.indirect_dma_start(out=w.far_rows[b][:, u, :], out_offset=None, in_=table,
                                                     in_offset=bass.IndirectOffsetOnAxis(ap=w.rec[b][:, u, far_end:far_end + 1], axis=0)).then_inc(w.gathered[b], 16)

        @block.tensor
        def _(pe):
            def turn_near(g, b, i, h):
                pe.wait_ge(near_in[b], 16 * (i + 1))
                pe.wait_ge(filled, 2 * g + h + 1)
                for u in range(Q):
                    last = nc.tensor.transpose(near_ps[0:D + 4, u, :], near_rows[b][:, Q * h + u, :], k.ident[:])
                last.then_inc(near_turned, 1)

            def add_up(g):
                for h in range(2):
                    pe.wait_ge(exponents, done(g - 1))
                    pe.wait_ge(w.terms_made, 2 * g + h + 1)
                    nc.tensor.matmul(flat(logits_ps[:, Q * h:Q * h + Q, :]), front.c.sums[:], w.terms[0:front.terms, h * M:(h + 1) * M],
                                     start=True, stop=True).then_inc(logits_made, 1)

            def turn_back(g, b, h):
                pe.wait_ge(scanned, done(g - 1))
                pe.wait_ge(copied, 2 * g + h + 1)
                for u in range(Q):
                    c = h * Q + u
                    last = nc.tensor.transpose(back_ps[:, u, :], run[1 - b][:, c * P:(c + 1) * P], k.ident[:])
                last.then_inc(returned, 1)

            pe.sem_inc(w.rows_turned, 4)
            pe.sem_inc(returned, 2)
            front.pe_start(w, pe)
            for g in range(2):
                front.pe_features(w, pe, g, g, 0)
                front.pe_hidden(w, pe, g)
                front.pe_filters(w, pe, g, 0)
                if g == 0:
                    front.pe_filters(w, pe, g, 1)
            turn_near(0, 0, 0, 0)
            for h in range(2):
                front.pe_rows(w, pe, 0, 0, 0, h, h)
            turn_near(0, 0, 0, 1)
            add_up(0)

            def body(g, b, i, more):
                if more:
                    turn_near(g + 1, 1 - b, i + b, 0)
                    front.pe_filters(w, pe, g + 1, 1)
                    for h in range(2):
                        front.pe_rows(w, pe, g + 1, 1 - b, i + b, 2 * g + 2 + h, h)
                turn_back(g, b, 0)
                if more and not front.sums_first:
                    turn_near(g + 1, 1 - b, i + b, 1)
                if two_follow(g):
                    front.pe_features(w, pe, g + 2, b, i + 1)
                turn_back(g, b, 1)
                if two_follow(g):
                    front.pe_hidden(w, pe, g + 2)
                if more and front.sums_first:
                    turn_near(g + 1, 1 - b, i + b, 1)
                if more:
                    add_up(g + 1)
                if two_follow(g):
                    front.pe_filters(w, pe, g + 2, 0)

            each_group(pe, body)
            for h in range(2):
                turn_back(G, 0, h)

        @block.vector
        def _(dve):
            def terms(g, b, i):
                dve.wait_ge(keep_in[b], 16 * (i + 1))
                for h in range(2):
                    q = 2 * g + h
                    part = slice(h * M, (h + 1) * M)
                    dve.wait_ge(carried, q + 1)
                    dve.wait_ge(near_turned, q + 1)
                    nc.vector.tensor_tensor_scan(w.terms[0:W, part], keep[b][:, part], flat(near_ps[0:W, :, :]), carry[0:W, :],
                                                 ALU.mult, ALU.add).then_inc(filled, 1)
                    dve.wait_ge(filled, q + 2)
                    nc.vector.tensor_copy(carry[0:W, :], w.terms[0:W, (h + 1) * M - 1:(h + 1) * M]).then_inc(carried, 1)
                    front.dve_terms(w, dve, g, b, q, h, part)

            for b in range(2):
                nc.vector.memset(near_rows[b][:], 0.0).then_inc(cleared, 1)
            nc.vector.memset(run[1][:], 0.0).then_inc(cleared, 1)
            nc.vector.memset(top[1][:], FAR).then_inc(cleared, 1)
            nc.vector.memset(w.terms[:], 1.0).then_inc(cleared, 1)
            nc.vector.memset(carry[:], 0.0).then_inc(cleared, 1)
            for s in (topped, exponents, w.weighted, scanned):
                dve.sem_inc(s, 2)
            for s in (filled, carried):
                dve.sem_inc(s, 1)
            dve.wait_ge(cleared, 6)
            w.carried = carried
            front.dve_start(w, dve)
            front.dve_early(w, dve, 0, 0, 0)
            front.dve_early(w, dve, 1, 1, 0)
            terms(0, 0, 0)

            def body(g, b, i, more):
                dve.wait_ge(exponents, done(g - 1))
                nc.vector.tensor_copy(top[b][:, 0:1], top[1 - b][:, L:L + 1]).then_inc(topped, 1)
                dve.wait_ge(topped, 2 * g + 1 + 2)
                dve.wait_ge(far_in[b], 16 * (i + 1))
                dve.wait_ge(logits_made, 2 * g + 2)
                nc.vector.tensor_tensor_scan(top[b][:, 1:1 + L], far[b][:], flat(logits_ps[:]), top[b][:, 0:1],
                                             ALU.add, ALU.max).then_inc(topped, 1)
                dve.wait_ge(scanned, done(g - 1))
                dve.wait_ge(topped, 2 * g + 2 + 2)
                nc.vector.tensor_tensor(faded_top[:], top[b][:, 0:L], far[b][:], ALU.add).then_inc(sized, 1)
                nc.vector.tensor_tensor(fade[:, 1, :], flat(logits_ps[:]), top[b][:, 1:1 + L], ALU.subtract).then_inc(sized, 1)
                dve.wait_ge(sized, 2 * g + 2)
                nc.vector.tensor_tensor(fade[:, 0, :], faded_top[:], top[b][:, 1:1 + L], ALU.subtract).then_inc(exponents, 1)
                if more:
                    terms(g + 1, 1 - b, i + b)
                if two_follow(g):
                    front.dve_early(w, dve, g + 2, b, i + 1)
                dve.wait_ge(exponents, done(g))
                dve.wait_ge(factors, g + 1)
                front.values_ready(w, dve, g)
                nc.vector.tensor_tensor(fade[D:P, 1, :], w.values[b][D:P, :], fade[D:P, 1, :], ALU.mult).then_inc(w.weighted, 1)
                dve.wait_ge(w.weighted, done(g))
                dve.wait_ge(returned, 2 * g + 2)
                nc.vector.tensor_tensor_scan(run[b][:], fade[:, 0, :], fade[:, 1, :], run[1 - b][:, L - 1:L], ALU.mult, ALU.add).then_inc(scanned, 1)

            each_group(dve, body)

        @block.scalar
        def _(act):
            act.sem_inc(copied, 1)
            front.act_start(w, act)
            for g in range(2):
                front.act_records(w, act, g, g, 0)
                front.act_features(w, act, g)
                front.act_hidden(w, act, g, g)
                front.act_filters(w, act, g, g)
            front.act_values(w, act, 0, 0)
            front.act_terms(w, act, 0)

            def raise_factors(g):
                act.wait_ge(exponents, done(g))
                nc.scalar.activation(fade[:].rearrange("p a l -> p (a l)"), fade[:].rearrange("p a l -> p (a l)"), ACT.Exp).then_inc(factors, 1)

            def copy_back(g, b, i, h):
                act.wait_ge(stored[1 - b], 16 * (i + 1))
                act.wait_ge(returned, 2 * g + h + 3)
                nc.scalar.copy(flat(back[1 - b][:, h * Q:(h + 1) * Q, :]), flat(back_ps[:])).then_inc(copied, 1)

            def body(g, b, i, more):
                if two_follow(g):
                    front.act_records(w, act, g + 2, b, i + 1)
                if more:
                    front.act_values(w, act, g + 1, 1 - b)
                copy_back(g, b, i, 0)
                if two_follow(g):
                    front.act_features(w, act, g + 2)
                if not front.sums_first:
                    raise_factors(g)
                copy_back(g, b, i, 1)
                if two_follow(g):
                    front.act_hidden(w, act, g + 2, b)
                if front.sums_first:
                    raise_factors(g)
                if more:
                    front.act_terms(w, act, g + 1)
                if two_follow(g):
                    front.act_filters(w, act, g + 2, b)

            for b in range(2):
                act.sem_inc(stored[b], 16 * (b + 1))
            each_group(act, body)
            for h in range(2):
                copy_back(G, 0, G // 2, h)


class FilterFront:

    F = 32
    terms = D + 4
    sums_first = True

    def __init__(self, weights):
        self.c = weights

    def buffers(self, w):
        at = w.at
        self.features_ps = at.ps("features_ps", [P, 2, 2 * P])
        self.filter_ps = at.ps("filter_ps", [P, w.Q, P])
        self.filters = [at.sb2(f"filters{b}", [P, w.M]) for b in range(2)]
        self.packed = at.sb("packed", [P, U, self.F])
        self.features, self.size, self.log = at.sb("features", [P, 2 * P]), at.sb("size", [P, 2 * P]), at.sb("log", [P, 2 * P])
        self.positive, self.soft = at.sb("positive", [P, 2 * P]), at.sb("soft", [P, 2 * P])
        w.values = at.sb2("filtered_rows", [P, U * P])
        self.features_turned, self.features_in, self.hidden, self.sized, self.raised, self.logged = (
            at.sem("features_turned"), at.sem("features_in"), at.sem("hidden"), at.sem("unit_sized"), at.sem("raised"), at.sem("logged"))
        self.rectified, self.softened, self.filtered, self.filters_in = at.sem("rectified"), at.sem("softened"), at.sem("filtered"), at.sem("filters_in")

    def values_ready(self, w, dve, g):
        dve.wait_ge(w.rows_read, 2 * g + 4)

    def act_start(self, w, act):
        for s in (w.rec_used, self.features_in, self.sized, self.raised, self.logged):
            act.sem_inc(s, 2)
        act.sem_inc(self.filters_in, 1)

    def act_records(self, w, act, g, b, i):
        nc = w.nc
        act.wait_ge(self.features_turned, done(g - 1))
        act.wait_ge(w.rec_in[b], 16 * (i + 1))
        nc.scalar.copy(self.packed[:], w.rec[b][:, :, 2:2 + self.F].bitcast(F32)).then_inc(w.rec_used, 1)

    def act_features(self, w, act, g):
        nc = w.nc
        act.wait_ge(self.hidden, done(g - 1))
        act.wait_ge(self.features_turned, done(g))
        nc.scalar.copy(self.features[:], self.features_ps[:, 0, :]).then_inc(self.features_in, 1)

    def act_hidden(self, w, act, g, b):
        nc = w.nc
        act.wait_ge(self.softened, done(g - 1))
        act.wait_ge(self.hidden, done(g))
        nc.scalar.activation(self.size[:], self.features_ps[:, 1, :], ACT.Abs, bias=self.c.hidden_bias[:]).then_inc(self.sized, 1)
        act.wait_ge(self.sized, done(g))
        nc.scalar.activation(self.size[:], self.size[:], ACT.Exp, scale=-1.0).then_inc(self.raised, 1)
        act.wait_ge(self.raised, done(g))
        nc.scalar.activation(self.log[:], self.size[:], ACT.Ln, scale=0.5, bias=self.c.half[:]).then_inc(self.logged, 1)

    def act_filters(self, w, act, g, b):
        nc = w.nc
        for h in range(2):
            if not (isinstance(g, int) and g < 2):
                act.wait_ge(w.rows_read, 2 * g + h - 1)
            act.wait_ge(self.filtered, 2 * g + h + 1)
            nc.scalar.activation(self.filters[b][h][:], flat(self.filter_ps[:]), ACT.Identity, bias=self.c.filter_bias[:]).then_inc(self.filters_in, 1)

    def act_values(self, w, act, g, b):
        pass

    def act_terms(self, w, act, g):
        pass

    def pe_start(self, w, pe):
        for s in (self.features_turned, self.hidden):
            pe.sem_inc(s, 2)

    def pe_features(self, w, pe, g, b, i):
        nc, k = w.nc, w.k
        pe.wait_ge(self.softened, done(g - 1))
        pe.wait_ge(w.rec_used, done(g))
        for h in range(2):
            last = nc.tensor.transpose(self.features_ps[:, 0, h * P:(h + 1) * P], flat(self.packed[:, 4 * h:4 * h + 4, :]), k.ident[:])
        last.then_inc(self.features_turned, 1)

    def pe_hidden(self, w, pe, g):
        nc = w.nc
        pe.wait_ge(self.features_in, done(g))
        nc.tensor.matmul(self.features_ps[:, 1, :], self.c.hidden[:], self.features[:], start=True, stop=True).then_inc(self.hidden, 1)

    def pe_filters(self, w, pe, g, h):
        pe.wait_ge(self.softened, done(g))
        pe.wait_ge(self.filters_in, 2 * g + h + 1)
        for u in range(w.Q):
            last = w.nc.tensor.matmul(self.filter_ps[:, u, :], self.c.filter[:, u, :], self.soft[:, h * P:(h + 1) * P], start=True, stop=True)
        last.then_inc(self.filtered, 1)

    def pe_rows(self, w, pe, g, b, i, q, h):
        nc = w.nc
        pe.wait_ge(w.gathered[b], 16 * U * (i + 1))
        pe.wait_ge(w.rows_read, q + 1)
        for u in range(w.Q):
            last = nc.tensor.transpose(w.rows_ps[h][:, u, :], w.far_rows[b][:, w.Q * h + u, :], w.k.ident[:])
        last.then_inc(w.rows_turned, 1)

    def dve_start(self, w, dve):
        for s in (w.rows_read, self.rectified, self.softened):
            dve.sem_inc(s, 2)

    def dve_early(self, w, dve, g, b, i):
        nc = w.nc
        dve.wait_ge(self.softened, done(g - 1))
        dve.wait_ge(self.sized, done(g))
        nc.vector.tensor_scalar(self.positive[:], self.features_ps[:, 1, :], self.c.hidden_bias[:], 0.0, ALU.add, ALU.max).then_inc(self.rectified, 1)
        dve.wait_ge(self.rectified, done(g))
        if not (isinstance(g, int) and g == 0):
            dve.wait_ge(self.filtered, 2 * g)
        dve.wait_ge(self.logged, done(g))
        nc.vector.tensor_tensor(self.soft[:], self.positive[:], self.log[:], ALU.add).then_inc(self.softened, 1)

    def dve_terms(self, w, dve, g, b, q, h, part):
        nc = w.nc
        dve.wait_ge(w.rows_turned, q + 5)
        dve.wait_ge(self.filters_in, q + 2)
        nc.vector.tensor_tensor(w.values[b][:, part], self.filters[b][h][:], flat(w.rows_ps[h][:]), ALU.mult).then_inc(w.rows_read, 1)
        dve.wait_ge(w.carried, q + 2)
        dve.wait_ge(w.rows_read, q + 3)
        nc.vector.tensor_tensor(w.terms[0:D, part], w.terms[0:D, part], w.values[b][0:D, part], ALU.mult).then_inc(w.terms_made, 1)


class MixFront:

    F = 2
    terms = D + 1
    sums_first = False

    def __init__(self, weights):
        self.c = weights

    def buffers(self, w):
        at = w.at
        self.features = at.sb("features", [P, U, self.F])
        self.turned_features = at.sb("turned_features", [U * self.F, P])
        self.edge = at.sb2("edge", [P, U // 2, P])
        self.features_ps = at.ps("features_ps", [P, 4 * P])
        self.edge_ps = at.ps("edge_ps", [P, U // 2, P])
        w.values = at.sb2("values", [P, U * P])
        self.features_turned, self.features_in, self.edged, self.rectified = (
            at.sem("features_turned"), at.sem("features_in"), at.sem("edged"), at.sem("rectified"))
        self.added, self.values_in = at.sem("added"), at.sem("values_in")

    def values_ready(self, w, dve, g):
        dve.wait_ge(self.values_in, 2 * g + 4)

    def act_start(self, w, act):
        for s in (w.rec_used, self.features_in, self.rectified, self.values_in):
            act.sem_inc(s, 2)

    def act_records(self, w, act, g, b, i):
        nc = w.nc
        act.wait_ge(self.features_turned, done(g - 1))
        act.wait_ge(w.rec_in[b], 16 * (i + 1))
        nc.scalar.copy(self.features[:], w.rec[b][:, :, 2:4].bitcast(F32)).then_inc(w.rec_used, 1)

    def act_features(self, w, act, g):
        nc = w.nc
        act.wait_ge(self.edged, done(g - 1))
        act.wait_ge(self.features_turned, done(g))
        nc.scalar.copy(self.turned_features[:], self.features_ps[0:U * self.F, 0:P]).then_inc(self.features_in, 1)

    def act_hidden(self, w, act, g, b):
        pass

    def act_filters(self, w, act, g, b):
        nc = w.nc
        act.wait_ge(w.rows_turned, 2 * g + 2)
        act.wait_ge(self.edged, done(g))
        nc.scalar.activation(flat(self.edge[b][:]), flat(self.edge_ps[:]), ACT.Relu, bias=self.c.edge_bias[:]).then_inc(self.rectified, 1)

    def act_values(self, w, act, g, b):
        nc = w.nc
        act.wait_ge(w.weighted, freed(g))
        for h in range(2):
            act.wait_ge(w.rows_turned, 2 * g + h + 5)
            nc.scalar.copy(w.values[b][D:P, h * w.M:(h + 1) * w.M], flat(w.rows_ps[h][D:P, :, :])).then_inc(self.values_in, 1)

    def act_terms(self, w, act, g):
        nc = w.nc
        for h in range(2):
            part = slice(h * w.M, (h + 1) * w.M)
            act.wait_ge(self.added, 2 * g + h + 3)
            nc.scalar.activation(w.terms[0:D, part], w.terms[0:D, part], ACT.Relu, scale=self.c.out_size[0:D, :]).then_inc(w.terms_made, 1)

    def pe_start(self, w, pe):
        for s in (self.features_turned, self.edged):
            pe.sem_inc(s, 2)

    def pe_hidden(self, w, pe, g):
        pass

    def pe_filters(self, w, pe, g, h):
        pass

    def pe_features(self, w, pe, g, b, i):
        nc, k = w.nc, w.k
        pe.wait_ge(self.features_in, done(g - 1))
        pe.wait_ge(w.rec_used, done(g))
        nc.tensor.transpose(self.features_ps[0:U * self.F, 0:P], flat(self.features[:]), k.ident[:]).then_inc(self.features_turned, 1)
        pe.wait_ge(self.rectified, done(g - 1))
        pe.wait_ge(self.features_in, done(g))
        for u in range(U // 2):
            last = nc.tensor.matmul(self.edge_ps[:, u, :], self.c.edge[:, u, :], self.turned_features[:], start=True, stop=True)
        last.then_inc(self.edged, 1)

    def pe_rows(self, w, pe, g, b, i, q, h):
        nc = w.nc
        pe.wait_ge(self.added, q + 1)
        pe.wait_ge(self.rectified, done(g))
        nc.tensor.matmul(flat(w.rows_ps[h][:]), self.c.mix[:, h, :], flat(self.edge[b][:]), start=True, stop=True, skip_group_check=True)
        pe.wait_ge(w.gathered[b], 16 * U * (i + 1))
        for u in range(w.Q):
            last = nc.tensor.matmul(w.rows_ps[h][:, u, :], w.far_rows[b][:, w.Q * h + u, :], w.k.ident[:], start=False, stop=True, skip_group_check=True)
        last.then_inc(w.rows_turned, 1)

    def dve_start(self, w, dve):
        dve.sem_inc(self.added, 2)

    def dve_early(self, w, dve, g, b, i):
        pass

    def dve_terms(self, w, dve, g, b, q, h, part):
        nc = w.nc
        dve.wait_ge(self.values_in, q + 3)
        dve.wait_ge(w.rows_turned, q + 5)
        dve.wait_ge(w.carried, q + 2)
        nc.vector.tensor_tensor(w.terms[0:D, part], w.terms[0:D, part], flat(w.rows_ps[h][0:D, :, :]), ALU.add).then_inc(self.added, 1)


def make_weight_buffers(sb):
    c, c_filter, c_mix = Parts(), Parts(), Parts()
    c.sage1 = sb("sage1", [P, P])
    c.sage1_bias = sb("sage1_bias", [P, P])
    c.sage2 = sb("sage2", [P, P])
    c.sage2_bias = sb("sage2_bias", [P, P])
    c.tables1 = sb("tables1", [P, 196])
    c.tables1_bias = sb("tables1_bias", [P, 196])
    c.value1 = sb("value1", [P, D])
    c.value1_bias = sb("value1_bias", [P, D])
    c.value_bias1 = sb("value_bias1", [P, D])
    c.out1 = sb("out1", [P, D])
    c.out1_bias = sb("out1_bias", [P, D])
    c.gcn = sb("gcn", [P, D])
    c.gcn_bias = sb("gcn_bias", [P, D])
    c.kqv = sb("kqv", [P, 3 * D])
    c.kqv_bias = sb("kqv_bias", [P, 3 * D])
    c.mix3 = sb("mix3", [P, P])
    c.mix3_bias = sb("mix3_bias", [P, P])
    c.out3 = sb("out3", [P, D])
    c.edge_count_bias = sb("edge_count_bias", [P, D])
    c.gamma = sb("gamma", [P, D])
    c.beta = sb("beta", [P, D])
    c_filter.hidden = sb("hidden_w", [P, P])
    c_filter.hidden_bias = sb("hidden_b", [P, 1])
    c_filter.filter = sb("filter_w", [P, 4, P])
    c_filter.filter_bias = sb("filter_b", [P, 1])
    c_filter.sums = sb("filter_sums", [D + 4, P])
    c_filter.half = sb("half", [P, 1])
    c_mix.edge = sb("edge_w", [2 * U, U // 2, P])
    c_mix.edge_bias = sb("edge_b", [P, 1])
    c_mix.mix = sb("mix_w", [P, 2, P])
    c_mix.sums = sb("mix_sums", [D + 1, P])
    c_mix.out_size = sb("mix_out_size", [D + 1, 1])
    c.filter, c.mix = c_filter, c_mix
    return c


def weight_moves(nc, at, name, k, a):
    c, p = k.weights, Parts()
    with ExitStack() as ctx:
        more1, more2 = at.sb("more1", [P, 2 * D]), at.sb("more2", [P, D])
        more_bias1, more_bias2 = at.sb("more_bias1", [P, 2 * D]), at.sb("more_bias2", [P, D])
        out_weight, negative = at.sb("out_weight", [D + 1, 1]), at.sb("negative", [D + 1, 1])
        query, key = at.sb("query", [D, 2 * D]), at.sb("key", [D, D + 4])
        p.more1, p.more2, p.more_bias1, p.more_bias2 = more1, more2, more_bias1, more_bias2
        p.out_weight, p.negative, p.query, p.key = out_weight, negative, query, key
        p.loaded = at.sem("weights_loaded")
        block = Stage(nc, ctx, name).block()
        zeroed = [c.sage2_bias, c.tables1, c.tables1_bias, c.value1, c.out1, c.gcn, c.kqv, c.mix3, c.mix3_bias, c.out3,
                  c.filter.hidden, c.filter.filter, c.mix.edge, c.mix.mix, query, key]
        row = lambda v: v.rearrange("(o f) -> o f", o=1)
        every = lambda v: row(v).to_broadcast([P, v.shape[0]])
        column = lambda v: v.rearrange("(f o) -> f o", o=1)
        moves = [
            (c.sage1[0:D, :], a["W1n"]), (c.sage1[D:P, :], a["W1r"]), (more1[D:P, :], a["Wl1"]),
            (c.sage1_bias[:], every(a["b1n"])), (more_bias1[:], every(a["bl1"])),
            (c.sage2[:, 0:D], a["W2n"]), (c.sage2[:, D:P], a["W2r"]), (more2[:], a["Wl2"]),
            (c.sage2_bias[:, D:P], every(a["b2n"])), (more_bias2[:], every(a["bl2"])),
            (c.value1[D:P, :], a["cen_wT"]), (c.value1_bias[:], every(a["cen_b"])),
            (c.out1[0:D, :], a["out_wT"]), (c.out1_bias[:], every(a["out_b"])),
            (c.gcn[0:D, :], a["gcn_w"]), (c.gcn_bias[:], every(a["gcn_b"])),
            (c.kqv[D:P, :], a["W_kqv"]), (c.kqv_bias[:], every(a["b_kqv"])),
            (c.out3[0:D, :], a["W_out"]), (c.edge_count_bias[:], every(a["b_out"])),
            (c.gamma[:], every(a["gamma"])), (c.beta[:], every(a["beta"])),
            (c.filter.sums[:], a["same_head4"]), (c.mix.sums[:], a["same_head2"]), (out_weight[D:D + 1, :], row(a["b_att2"])),
        ]
        for h in range(4):
            s = slice(16 * h, 16 * (h + 1))
            under = slice(D + 16 * h, D + 16 * (h + 1))
            moves += [(c.tables1[under, s], a["k_wT"][h]), (c.tables1[under, under], a["v_wT"][h]),
                      (query[s, under], a["q_w"][h]), (key[s, s], a["wkl_w"]), (key[s, D + h:D + h + 1], column(a["wkl_b"])),
                      (c.value1[s, s], a["wvl_wT"]), (c.value_bias1[:, s], every(a["wvl_b"])),
                      (c.filter.filter_bias[s, :], column(a["wkn_b2"])), (c.filter.filter_bias[under, :], column(a["wvn_b2"]))]
        for u in range(4):
            lo, hi = slice(32 * u, 32 * u + 16), slice(32 * u + 16, 32 * u + 32)
            both = slice(32 * u, 32 * u + 32)
            moves += [(c.filter.hidden[both, lo], a["wkn_w1T"]), (c.filter.hidden[both, hi], a["wvn_w1T"]),
                      (c.filter.hidden_bias[lo, :], column(a["wkn_b1"])), (c.filter.hidden_bias[hi, :], column(a["wvn_b1"])),
                      (c.filter.filter[lo, u, 0:D].rearrange("i (h o) -> i h o", h=4), a["wkn_w2T"].unsqueeze(1).to_broadcast([16, 4, 16])),
                      (c.filter.filter[hi, u, D:P].rearrange("i (h o) -> i h o", h=4), a["wvn_w2T"].unsqueeze(1).to_broadcast([16, 4, 16]))]
            for half in range(2):
                chunk = u + 4 * half
                moves.append((c.mix.edge[2 * chunk:2 * chunk + 2, u, half * D:(half + 1) * D], a["W_edge"]))
        for h in range(2):
            s = slice(32 * h, 32 * (h + 1))
            under = slice(D + 32 * h, D + 32 * (h + 1))
            moves += [(c.mix3[s, under], a["W_att1"][32:64, :]), (c.mix3[under, s], a["W_att1"][0:32, :]),
                      (c.mix3_bias[:, under], every(a["b_att1"])), (out_weight[s, :], column(a["w_att2"])),
                      (c.mix.mix[s, 0, s], a["W_att1"][64:96, :]), (c.mix.mix[under, 1, s], a["W_att1"][64:96, :]),
                      (c.mix.edge_bias[h * D:(h + 1) * D, :], column(a["b_edge"]))]

        @block.vector
        def _(dve):
            for z in zeroed:
                nc.vector.memset(z[:], 0.0)
            nc.vector.memset(c.filter.half[:], 0.5)
    p.moves = moves
    return p


def finish_weights(nc, name, k, p):
    c = k.weights
    more1, more2, more_bias1, more_bias2 = p.more1, p.more2, p.more_bias1, p.more_bias2
    out_weight, negative, query, key = p.out_weight, p.negative, p.query, p.key
    loads = 16 * len(p.moves)
    with ExitStack() as ctx:
        at = Stage(nc, ctx, name)
        query_ps = at.ps("query_ps", [P, 512])
        stepped, multiplied = at.sem("stepped"), at.sem("multiplied")
        block = at.block()

        @block.tensor
        def _(pe):
            pe.wait_ge(p.loaded, loads)
            nc.tensor.matmul(query_ps[:, 0:D + 4], query[:], key[:], start=True, stop=True).then_inc(multiplied, 1)

        @block.vector
        def _(dve):
            step = Steps(dve, stepped)
            dve.wait_ge(p.loaded, loads)
            step(nc.vector.tensor_tensor(c.sage1[D:P, :], c.sage1[D:P, :], more1[D:P, :], ALU.add))
            step(nc.vector.tensor_tensor(c.sage2[:, D:P], c.sage2[:, D:P], more2[:], ALU.add))
            step(nc.vector.tensor_tensor(c.sage1_bias[:], c.sage1_bias[:], more_bias1[:], ALU.add))
            step(nc.vector.tensor_tensor(c.sage2_bias[:, D:P], c.sage2_bias[:, D:P], more_bias2[:], ALU.add))
            step(nc.vector.tensor_scalar(c.mix3[D:P, :], c.mix3[D:P, :], 32.0 ** -0.5, None, ALU.mult))
            step(nc.vector.tensor_scalar(negative[:], out_weight[:], -1.0, None, ALU.mult))
            step(nc.vector.tensor_tensor(c.mix.out_size[:], out_weight[:], negative[:], ALU.max))
            step(nc.vector.tensor_tensor(negative[0:D, :], negative[0:D, :], out_weight[0:D, :], ALU.is_lt))
            step(nc.vector.tensor_scalar(out_weight[0:D, :], negative[0:D, :], 2.0, -1.0, ALU.mult, ALU.add))
            step(nc.vector.tensor_scalar(c.mix.sums[:], c.mix.sums[:], out_weight[:], None, ALU.mult))
            dve.wait_ge(multiplied, 1)
            step(nc.vector.tensor_copy(c.tables1[:, P:P + D + 4], query_ps[:, 0:D + 4]))


def node_stage(nc, name, k, program, stores=(), roots=0):
    with ExitStack() as ctx:
        at = Stage(nc, ctx, name)
        centred, squares, stat = at.sb("centred", [P, NT, D]), at.sb("squares", [P, NT, D]), at.sb("stat", [P, NT])
        stepped, stored, finished = at.sem("stepped"), at.sem("stored"), at.sem("finished")
        squared, rooted = at.sem("squared"), at.sem("rooted")
        block = at.block()

        @block.vector
        def _(dve):
            step = Steps(dve, stepped)
            given = [0]

            def root():
                given[0] += 1
                dve.sem_inc(squared, 1)
                dve.wait_ge(rooted, given[0])

            norm = lambda x, out: layer_norm(nc, step, root, x, out, centred, squares, stat)
            o = Parts()
            o.v, o.step, o.root, o.norm, o.tmp, o.stat = nc.vector, step, root, norm, centred, stat
            program(o)
            dve.sem_inc(finished, 1)

        @block.scalar
        def _(act):
            for r in range(roots):
                act.wait_ge(squared, r + 1)
                nc.scalar.sqrt(stat[:], stat[:]).then_inc(rooted, 1)

        @block.sync
        def _(sp):
            sp.wait_ge(finished, 1)
            for out, in_ in stores:
                sp.dma_start(out, in_).then_inc(stored, 16)
            if stores:
                sp.wait_ge(stored, 16 * len(stores))


def shifted_softplus(nc, name, k, x, out):
    with ExitStack() as ctx:
        at = Stage(nc, ctx, name)
        size = at.sb("size", [P, NT, D])
        sized, logged, stepped = at.sem("sized"), at.sem("logged"), at.sem("stepped")
        block = at.block()

        @block.scalar
        def _(act):
            step = Steps(act, sized)
            step(nc.scalar.activation(size[:], x, ACT.Abs))
            step(nc.scalar.activation(size[:], size[:], ACT.Exp, scale=-1.0))
            nc.scalar.activation(size[:], size[:], ACT.Ln, scale=0.5, bias=k.weights.filter.half[:]).then_inc(logged, 1)

        @block.vector
        def _(dve):
            dve.wait_ge(logged, 1)
            nc.vector.scalar_tensor_tensor(out, x, 0.0, size[:], ALU.max, ALU.add).then_inc(stepped, 1)


ZEROS = 4 * CH


def build(nc, a, out):
    dram = lambda name, shape, dt=F32: nc.dram_tensor(name, shape, dt, kind="Internal").ap()
    by_tile = lambda table: table.rearrange("(t p) f -> p t f", p=P)
    with ExitStack() as ctx:
        sb = Stage(nc, ctx, "all").sb
        count, before, upto, ident, ones = (sb(n, [P, P]) for n in ("count", "before", "upto", "ident", "ones"))
        k = Parts()
        k.count, k.before, k.upto, k.ident, k.ones = count, before, upto, ident, ones
        k.ones16, k.ident16, k.lanes16, k.later16 = (sb(n, [P, P], BF16) for n in ("ones16", "ident16", "lanes16", "later16"))
        k.tiles16 = sb("tiles16", [P, NT], BF16)
        k.weights = make_weight_buffers(sb)
        c = k.weights
        k.spare, k.zeros = sb("spare", [P, NT]), sb("zeros", [P, ZEROS])
        make_constants(nc, "constants", k)

        starts1, starts3 = dram("starts1", (EP + NP, D + 4)), dram("starts3", (EP + NP, D))
        starts_cleared = nc.alloc_semaphore("starts_cleared")

        def move_weights(sp):
            with nc.allow_non_contiguous_dma(reason="small biases turned into columns"):
                for out, in_ in weights.moves:
                    sp.dma_start(out, in_).then_inc(weights.loaded, 16)

        def clear_starts(act):
            for starts in (starts1, starts3):
                words = starts[0:EP, :].rearrange("(p j) w -> p (j w)", p=P)
                for at in range(0, words.shape[1], ZEROS):
                    act.dma_start(words[:, at:at + ZEROS], k.zeros[:]).then_inc(starts_cleared, 16)
        clears = 16 * CH * (D + 4 + D) // ZEROS
        weights = weight_moves(nc, Stage(nc, ctx, "all_weights"), "zero_weights", k, a)

        by_dst, by_src = dram("by_dst", (EP, 4), I32), dram("by_src", (EP, 34), I32)
        rows = [Parts(), Parts()]
        for r, n in zip(rows, ("dst", "src")):
            r.keep, r.far = dram(f"keep_{n}", (EP,)), dram(f"far_{n}", (EP,))
            r.count, r.some, r.crosses = sb(f"count_{n}", [P, NT]), sb(f"some_{n}", [P, NT]), sb(f"crosses_{n}", [P, NT])
            r.last, r.first, r.place = sb(f"last_{n}", [P, NT], I32), sb(f"first_{n}", [P, NT], I32), sb(f"place_{n}", [P, NT])
        into, outof = rows
        order_edges(nc, k, ("sort_dst", "sort_src"), a["src"], a["dst"], (a["edge_attr_2"], a["edge_attr_32"]), (DST, SRC), (4, 34),
                    (into, outof), (by_dst, by_src), move_weights, clear_starts)
        finish_weights(nc, "weights", k, weights)

        x, wide, tall = sb("x", [P, NT, D]), sb("wide", [P, NT, P]), sb("tall", [P, NT, 196])
        scale = sb("scale", [P, NT])
        summed, own = wide[:, :, 0:D], wide[:, :, D:P]
        over = lambda col: col[:].unsqueeze(2).to_broadcast([P, NT, D])
        each = lambda bias: bias[:].unsqueeze(1).to_broadcast([P, NT, D])
        table = dram("table", (NP, D))
        running, weighted = dram("running", (EP, D)), dram("weighted", (EP, P))
        with ExitStack() as first:
            at = Stage(nc, first, "load_x")
            loaded, cleared = at.sem("loaded"), at.sem("cleared")
            block = at.block()
            whole = N // P

            @block.vector
            def _(dve):
                nc.vector.memset(x[:, whole:NT, :], 0.0).then_inc(cleared, 1)

            @block.sync
            def _(sp):
                sp.dma_start(x[:, 0:whole, :], by_tile(a["x"][0:whole * P, :])).then_inc(loaded, 16)
                sp.wait_ge(cleared, 1)
                sp.dma_start(x[0:N - whole * P, whole, :], a["x"][whole * P:N, :]).then_inc(loaded, 16)
                sp.wait_ge(loaded, 32)

        def start0(o):
            v, step, tmp = o.v, o.step, o.tmp
            o.norm(x[:], own)
            step(v.tensor_scalar(scale[:], into.count[:], 1.0, None, ALU.max))
            step(v.reciprocal(scale[:], scale[:]))
        node_stage(nc, "start0", k, start0, [(by_tile(table), own)], roots=1)
        sum_over_edges(nc, "sage1_sum", k, by_dst, SRC, table, into.keep, running)
        node_sums(nc, "sage1_mean", running, into.last, into.some, into.crosses, scale, summed)
        linear(nc, "sage1", k, wide, c.sage1, P, c.sage1_bias, tall)

        def hidden0(o):
            v, step, tmp = o.v, o.step, o.tmp
            step(v.tensor_scalar(wide[:], tall[:, :, 0:P], 0.0, None, ALU.max))
        node_stage(nc, "hidden0", k, hidden0)
        linear(nc, "sage2", k, wide, c.sage2, P, c.sage2_bias, tall)

        def own0(o):
            v, step, tmp = o.v, o.step, o.tmp
            step(v.tensor_tensor(x[:], x[:], tall[:, :, D:P], ALU.add))
        node_stage(nc, "own0", k, own0, [(by_tile(table), tall[:, :, 0:D])])
        sum_over_edges(nc, "sage2_sum", k, by_dst, SRC, table, into.keep, running)
        node_sums(nc, "sage2_mean", running, into.last, into.some, into.crosses, scale, summed)

        def start1(o):
            v, step, tmp = o.v, o.step, o.tmp
            step(v.tensor_tensor(x[:], x[:], summed, ALU.add))
            o.norm(x[:], own)
        node_stage(nc, "start1", k, start1, roots=1)
        linear(nc, "tables1", k, wide, c.tables1, 196, c.tables1_bias, tall)
        keys_values = dram("keys_values", (NP, P))
        node_stage(nc, "store1", k, lambda o: None, [(by_tile(keys_values), tall[:, :, 0:P])])
        rows_to_first_edges(nc, "queries1", tall[:, :, P:P + D + 4], outof.first, starts_cleared, clears, starts1)
        attention_pass(nc, "attend1", k, by_src, 34, DST, keys_values, starts1, D + 4, outof.keep, outof.far, weighted, FilterFront(c.filter))
        node_averages(nc, "average1", weighted, outof.last, outof.some, summed)
        linear(nc, "value1", k, wide, c.value1, D, c.value1_bias, tall)

        def value1(o):
            v, step, tmp = o.v, o.step, o.tmp
            step(v.tensor_tensor(tmp[:], over(outof.some), each(c.value_bias1), ALU.mult))
            step(v.tensor_tensor(tmp[:], tmp[:], tall[:, :, 0:D], ALU.add))
            step(v.tensor_copy(own, tmp[:]))
        node_stage(nc, "biased1", k, value1)
        shifted_softplus(nc, "soft1", k, own, summed)
        linear(nc, "out1", k, wide, c.out1, D, c.out1_bias, tall)

        def start2(o):
            v, step, tmp = o.v, o.step, o.tmp
            step(v.tensor_tensor(x[:], x[:], tall[:, :, 0:D], ALU.add))
            o.norm(x[:], own)
            step(v.tensor_scalar(o.stat[:], outof.count[:], 1.0, None, ALU.max))
            o.root()
            step(v.reciprocal(o.stat[:], o.stat[:]))
            step(v.tensor_tensor(scale[:], o.stat[:], outof.some[:], ALU.mult))
            step(v.tensor_tensor(tmp[:], own, over(scale), ALU.mult))
            step(v.tensor_copy(own, tmp[:]))
        node_stage(nc, "start2", k, start2, [(by_tile(table), own)], roots=2)
        sum_over_edges(nc, "gcn_sum", k, by_src, DST, table, outof.keep, running)
        node_sums(nc, "gcn_scale", running, outof.last, outof.some, outof.crosses, scale, summed)
        linear(nc, "gcn", k, wide, c.gcn, D, c.gcn_bias, tall)

        def start3(o):
            v, step, tmp = o.v, o.step, o.tmp
            step(v.scalar_tensor_tensor(x[:], tall[:, :, 0:D], 0.0, x[:], ALU.max, ALU.add))
            o.norm(x[:], own)
        node_stage(nc, "start3", k, start3, roots=1)
        linear(nc, "kqv", k, wide, c.kqv, 3 * D, c.kqv_bias, tall)
        mixed, mix_values = sb("mixed", [P, NT, P]), dram("mix_values", (NP, P))
        linear(nc, "mix3", k, tall[:, :, 0:P], c.mix3, P, c.mix3_bias, mixed)

        node_stage(nc, "store3", k, lambda o: None, [(by_tile(mix_values[:, 0:D]), mixed[:, :, 0:D]), (by_tile(mix_values[:, D:P]), tall[:, :, P:P + D])])
        rows_to_first_edges(nc, "queries3", mixed[:, :, D:P], into.first, starts_cleared, clears, starts3)
        attention_pass(nc, "attend3", k, by_dst, 4, SRC, mix_values, starts3, D, into.keep, into.far, weighted, MixFront(c.mix))
        node_averages(nc, "average3", weighted, into.last, into.some, summed)

        linear(nc, "out3", k, wide, c.out3, D, c.tables1_bias, tall)

        def finish3(o):
            v, step, tmp = o.v, o.step, o.tmp
            step(v.tensor_tensor(tmp[:], over(into.count), each(c.edge_count_bias), ALU.mult))
            step(v.tensor_tensor(tmp[:], tmp[:], tall[:, :, 0:D], ALU.add))
            step(v.tensor_tensor(tmp[:], tmp[:], own, ALU.add))
            step(v.tensor_scalar(tmp[:], tmp[:], (1.0 + EPS) ** -0.5, None, ALU.mult))
            step(v.tensor_tensor(tmp[:], tmp[:], each(c.gamma), ALU.mult))
            step(v.tensor_tensor(tmp[:], tmp[:], each(c.beta), ALU.add))
            step(v.tensor_tensor(x[:], x[:], tmp[:], ALU.add))
        whole = N // P
        node_stage(nc, "finish3", k, finish3, [(by_tile(out[0:whole * P, :]), x[:, 0:whole, :]), (out[whole * P:N, :], x[0:N - whole * P, whole, :])])


_NAMES = {
    "x": "x", "src": "src", "dst": "dst", "edge_attr_2": "edge_attr_2", "edge_attr_32": "edge_attr_32",
    "W1n": "L0_gnn_W1n", "b1n": "L0_gnn_b1n", "W1r": "L0_gnn_W1r", "Wl1": "L0_gnn_Wl1", "bl1": "L0_gnn_bl1",
    "W2n": "L0_gnn_W2n", "b2n": "L0_gnn_b2n", "W2r": "L0_gnn_W2r", "Wl2": "L0_gnn_Wl2", "bl2": "L0_gnn_bl2",
    "k_wT": "L1_gnn_k_w", "q_w": "L1_gnn_q_w", "v_wT": "L1_gnn_v_w",
    "wkn_w1T": "L1_gnn_wkn_w1", "wkn_b1": "L1_gnn_wkn_b1", "wkn_w2T": "L1_gnn_wkn_w2", "wkn_b2": "L1_gnn_wkn_b2",
    "wkl_w": "L1_gnn_wkl_w", "wkl_b": "L1_gnn_wkl_b",
    "wvn_w1T": "L1_gnn_wvn_w1", "wvn_b1": "L1_gnn_wvn_b1", "wvn_w2T": "L1_gnn_wvn_w2", "wvn_b2": "L1_gnn_wvn_b2",
    "wvl_wT": "L1_gnn_wvl_w", "wvl_b": "L1_gnn_wvl_b",
    "cen_wT": "L1_gnn_cen_w", "cen_b": "L1_gnn_cen_b", "out_wT": "L1_gnn_out_w", "out_b": "L1_gnn_out_b",
    "gcn_w": "L2_gnn_weight", "gcn_b": "L2_gnn_bias",
    "W_kqv": "L3_gnn_W_kqv", "b_kqv": "L3_gnn_b_kqv", "W_edge": "L3_gnn_W_edge", "b_edge": "L3_gnn_b_edge",
    "W_att1": "L3_gnn_W_att1", "b_att1": "L3_gnn_b_att1", "w_att2": "L3_gnn_W_att2", "b_att2": "L3_gnn_b_att2",
    "W_out": "L3_gnn_W_out", "b_out": "L3_gnn_b_out", "gamma": "L3_gnn_bn_gamma", "beta": "L3_gnn_bn_beta",
}


def kernel(**inputs):
    import numpy as np
    import concourse.bacc as bacc
    from concourse.bass_utils import run_bass_kernel_spmd

    nc = bacc.Bacc("TRN2", target_bir_lowering=False, num_devices=1)
    arrays, args = {}, {}
    for short, name in _NAMES.items():
        v = np.asarray(inputs[name])
        if short.endswith("T"):
            v = np.swapaxes(v, -1, -2)
        if short == "w_att2":
            v = v.reshape(-1)
        v = np.ascontiguousarray(v)
        arrays[f"in_{short}"] = v
        args[short] = nc.dram_tensor(f"in_{short}", v.shape, mybir.dt.from_np(v.dtype), kind="ExternalInput").ap()
    head = lambda count: (np.arange(D) * count // D)[:, None] == (np.arange(P) % D * count // D)[None, :]
    per_head = np.arange(4)[:, None] == (np.arange(P) % D * 4 // D)[None, :]
    for short, v in (("same_head4", np.concatenate([head(4), per_head])), ("same_head2", np.concatenate([head(2), np.ones((1, P), bool)]))):
        arrays[f"in_{short}"] = v.astype(np.float32)
        args[short] = nc.dram_tensor(f"in_{short}", v.shape, F32, kind="ExternalInput").ap()
    out = nc.dram_tensor("out_x", (N, D), F32, kind="ExternalOutput").ap()
    build(nc, args, out)
    return run_bass_kernel_spmd(nc, [arrays], core_ids=[0]).results[0]["out_x"]
```
